# Optimizing a Trainium2 kernel written in Bass

```python
import numpy as np
import jax
import jax.numpy as jnp

def _softmax(x, axis=-1):
    return jax.nn.softmax(x, axis=axis)

def _gelu(x):
    return jax.nn.gelu(x, approximate=True)

def _silu(x):
    return jax.nn.silu(x)

def _sigmoid(x):
    return jax.nn.sigmoid(x)

def _layernorm(x, axis=-1, eps=1e-05):
    m = jnp.mean(x, axis=axis, keepdims=True)
    v = jnp.var(x, axis=axis, keepdims=True)
    return (x - m) / jnp.sqrt(v + eps)

def _scatter_add(tgt, idx, src, axis=0):
    return tgt.at[idx].add(src)

def _segment_sum(src, seg, n):
    return jax.ops.segment_sum(src, seg, n)
kernel_name = 'mk_xattn_ffn_d2_seqx_r4_86ec36'

def setup_inputs(seed: int=0):
    np.random.seed(seed)
    _w = jnp.asarray

    def _rec_inputs():
        import jax
        import jax.numpy as jnp
        _rk = jax.random.key(seed)
        x = -0.0002928 + 1 * jax.random.normal(jax.random.fold_in(_rk, 1), (8, 256, 256), jnp.float32)
        _lenS = 256 - jax.random.randint(jax.random.fold_in(_rk, 7), (8,), 0, max(1, 256 // 4) + 1, jnp.int32)
        _lenS2 = 256 - jax.random.randint(jax.random.fold_in(_rk, 8), (8,), 0, max(1, 256 // 4) + 1, jnp.int32)
        _ctx_1024P = jax.random.normal(jax.random.fold_in(_rk, 11), (8, 16, 256), jnp.float32)
        _ctx_1024c = jax.random.dirichlet(jax.random.fold_in(_rk, 511), 0.3 * jnp.ones((16,), jnp.float32), (8, 256))
        _ctx_1024t = jnp.einsum('bsk,bkd->bsd', _ctx_1024c, _ctx_1024P)
        _ctx_1024t = _ctx_1024t * jax.lax.rsqrt(jnp.mean(jnp.square(_ctx_1024t)) + 1e-12) * 0.953939
        ctx_1024 = -1.39393e-06 + 0.999914 * (_ctx_1024t + 0.3 * jax.random.normal(jax.random.fold_in(_rk, 611), (8, 256, 256), jnp.float32))
        return (x, ctx_1024)
    x, ctx_1024 = _rec_inputs()

    def _L0_xattn_setup():
        import jax, jax.numpy as jnp
        import numpy as np
        H = 16
        key = jax.random.key(seed)
        kq, kk, kv = jax.random.split(key, 3)
        B, S, D = (2, 512, 256)
        Q = jax.random.normal(kq, (B, S, D), dtype=jnp.float32)
        K = jax.random.normal(kk, (B, S, D), dtype=jnp.float32)
        V = jax.random.normal(kv, (B, S, D), dtype=jnp.float32)
        return {'Q': Q, 'K': K, 'V': V}
    _L0_xattn_all = _L0_xattn_setup()
    _L0_xattn_in = {k: v for k, v in _L0_xattn_all.items() if k in ()}
    del _L0_xattn_all

    def _L0_ffn_setup():
        import jax, jax.numpy as jnp
        import numpy as np
        TOP_K = 8
        key = jax.random.key(seed)
        k1, k2, k3, k4, k5 = jax.random.split(key, 5)
        B, S, D, F, E = (2, 512, 256, 192, 64)
        return {'hidden_states': jax.random.normal(k1, (B, S, D), dtype=jnp.float32), 'gate_w': jax.random.normal(k2, (E, D), dtype=jnp.float32) * 0.02, 'w_gate': jax.random.normal(k3, (E, F, D), dtype=jnp.float32) * 0.02, 'w_up': jax.random.normal(k4, (E, F, D), dtype=jnp.float32) * 0.02, 'w_down': jax.random.normal(k5, (E, D, F), dtype=jnp.float32) * 0.02}
    _L0_ffn_all = _L0_ffn_setup()
    _L0_ffn_in = {k: v for k, v in _L0_ffn_all.items() if k in ('gate_w', 'w_gate', 'w_up', 'w_down')}
    del _L0_ffn_all

    def _L1_xattn_setup():
        import jax, jax.numpy as jnp
        import numpy as np
        D_MODEL = 256
        NUM_HEADS = 16
        HEAD_DIM = D_MODEL // NUM_HEADS
        B, T = (4, 512)
        key = jax.random.key(seed)
        ks = jax.random.split(key, 6)
        s = 1.0 / np.sqrt(D_MODEL)
        return {'x_q': jax.random.normal(ks[0], (B, T, D_MODEL), jnp.float32), 'x_kv': jax.random.normal(ks[1], (B, T, D_MODEL), jnp.float32), 'Wq': jax.random.uniform(ks[2], (D_MODEL, D_MODEL), jnp.float32, -s, s), 'Wk': jax.random.uniform(ks[3], (D_MODEL, D_MODEL), jnp.float32, -s, s), 'Wv': jax.random.uniform(ks[4], (D_MODEL, D_MODEL), jnp.float32, -s, s), 'Wo': jax.random.uniform(ks[5], (D_MODEL, D_MODEL), jnp.float32, -s, s)}
    _L1_xattn_all = _L1_xattn_setup()
    _L1_xattn_in = {k: v for k, v in _L1_xattn_all.items() if k in ('Wq', 'Wk', 'Wv', 'Wo')}
    del _L1_xattn_all

    def _L1_ffn_setup():
        import jax, jax.numpy as jnp
        import numpy as np
        IN_F, OUT_F, BLOCK, NBLK = (256, 1024, 64, 16)
        TOPK = NBLK // 4
        key = jax.random.key(seed)
        ks = jax.random.split(key, 7)
        s = 1.0 / np.sqrt(IN_F)
        s2 = 1.0 / np.sqrt(OUT_F)
        return {'x': jax.random.normal(ks[0], (4, 1024, IN_F), jnp.float32), 'router_w': jax.random.uniform(ks[1], (NBLK, IN_F), jnp.float32, -s, s), 'router_b': jax.random.uniform(ks[2], (NBLK,), jnp.float32, -s, s), 'w1': jax.random.uniform(ks[3], (OUT_F, IN_F), jnp.float32, -s, s), 'b1': jax.random.uniform(ks[4], (OUT_F,), jnp.float32, -s, s), 'w2': jax.random.uniform(ks[5], (IN_F, OUT_F), jnp.float32, -s2, s2), 'b2': jax.random.uniform(ks[6], (IN_F,), jnp.float32, -s2, s2)}
    _L1_ffn_all = _L1_ffn_setup()
    _L1_ffn_in = {k: v for k, v in _L1_ffn_all.items() if k in ('router_w', 'router_b', 'w1', 'b1', 'w2', 'b2')}
    del _L1_ffn_all
    return {'x': x, 'ctx_1024': ctx_1024, 'L0_ffn_gate_w': _L0_ffn_in['gate_w'], 'L0_ffn_w_gate': _L0_ffn_in['w_gate'], 'L0_ffn_w_up': _L0_ffn_in['w_up'], 'L0_ffn_w_down': _L0_ffn_in['w_down'], 'L1_xattn_Wq': _L1_xattn_in['Wq'], 'L1_xattn_Wk': _L1_xattn_in['Wk'], 'L1_xattn_Wv': _L1_xattn_in['Wv'], 'L1_xattn_Wo': _L1_xattn_in['Wo'], 'L1_ffn_router_w': _L1_ffn_in['router_w'], 'L1_ffn_router_b': _L1_ffn_in['router_b'], 'L1_ffn_w1': _L1_ffn_in['w1'], 'L1_ffn_b1': _L1_ffn_in['b1'], 'L1_ffn_w2': _L1_ffn_in['w2'], 'L1_ffn_b2': _L1_ffn_in['b2']}

def reference(x, ctx_1024, L0_ffn_gate_w, L0_ffn_w_gate, L0_ffn_w_up, L0_ffn_w_down, L1_xattn_Wq, L1_xattn_Wk, L1_xattn_Wv, L1_xattn_Wo, L1_ffn_router_w, L1_ffn_router_b, L1_ffn_w1, L1_ffn_b1, L1_ffn_w2, L1_ffn_b2):
    import jax
    import jax.numpy as jnp

    def _L0_xattn_ref(Q, K, V):
        import jax, jax.numpy as jnp
        import numpy as np
        H = 16
        B, S, D = Q.shape
        dh = D // H
        q = Q.reshape(B, S, H, dh)
        k = K.reshape(B, S, H, dh)
        v = V.reshape(B, S, H, dh)
        scale = 1.0 / np.float32(np.sqrt(D))
        scores = jnp.einsum('bqhd,bkhd->bhqk', q, k) * scale
        attn = jax.nn.softmax(scores, axis=-1)
        out = jnp.einsum('bhqk,bkhd->bqhd', attn, v)
        return out.reshape(B, S, D)

    def _L0_ffn_ref(hidden_states, gate_w, w_gate, w_up, w_down):
        import jax, jax.numpy as jnp
        import numpy as np
        TOP_K = 8
        B, S, D = hidden_states.shape
        E = gate_w.shape[0]
        x = hidden_states.reshape(-1, D)
        logits = x.astype(jnp.float32) @ gate_w.astype(jnp.float32).T
        scores = jax.nn.softmax(logits, axis=-1)
        topk_w, topk_ids = jax.lax.top_k(scores, TOP_K)
        topk_w = topk_w / (topk_w.sum(axis=-1, keepdims=True) + 1e-20)
        flat_ids = topk_ids.reshape(-1)
        sort_idx = jnp.argsort(flat_ids)
        sorted_tokens = x[sort_idx // TOP_K]
        group_sizes = jnp.zeros((E,), jnp.int32).at[flat_ids].add(1)
        g = jax.lax.ragged_dot(sorted_tokens, jnp.swapaxes(w_gate, 1, 2), group_sizes)
        u = jax.lax.ragged_dot(sorted_tokens, jnp.swapaxes(w_up, 1, 2), group_sizes)
        h = jax.nn.silu(g) * u
        out = jax.lax.ragged_dot(h, jnp.swapaxes(w_down, 1, 2), group_sizes)
        unsorted = jnp.zeros_like(out).at[sort_idx].set(out)
        y = (unsorted.reshape(B * S, TOP_K, D) * topk_w[..., None]).sum(axis=1)
        return y.reshape(B, S, D)

    def _L1_xattn_ref(x_q, x_kv, Wq, Wk, Wv, Wo):
        import jax, jax.numpy as jnp
        import numpy as np
        D_MODEL = 256
        NUM_HEADS = 16
        HEAD_DIM = D_MODEL // NUM_HEADS
        B, T = (4, 512)
        Bq, Tq, C = x_q.shape
        Tk = x_kv.shape[1]
        q = (x_q @ Wq.T).reshape(Bq, Tq, NUM_HEADS, HEAD_DIM).transpose(0, 2, 1, 3)
        k = (x_kv @ Wk.T).reshape(Bq, Tk, NUM_HEADS, HEAD_DIM).transpose(0, 2, 1, 3)
        v = (x_kv @ Wv.T).reshape(Bq, Tk, NUM_HEADS, HEAD_DIM).transpose(0, 2, 1, 3)
        scores = jnp.einsum('bhqd,bhkd->bhqk', q, k) / jnp.sqrt(jnp.asarray(HEAD_DIM, x_q.dtype))
        causal = jnp.triu(jnp.ones((Tq, Tk), bool), k=1)
        scores = jnp.where(causal, -jnp.inf, scores)
        attn = jax.nn.softmax(scores, axis=-1)
        out = jnp.einsum('bhqk,bhkd->bhqd', attn, v)
        out = out.transpose(0, 2, 1, 3).reshape(Bq, Tq, C)
        return out @ Wo.T

    def _L1_ffn_ref(x, router_w, router_b, w1, b1, w2, b2):
        import jax, jax.numpy as jnp
        import numpy as np
        IN_F, OUT_F, BLOCK, NBLK = (256, 1024, 64, 16)
        TOPK = NBLK // 4
        x_shape = x.shape
        xf = x.reshape(-1, IN_F)
        n = xf.shape[0]
        prob = jax.nn.softmax(xf @ router_w.T + router_b, axis=-1)
        _, idx = jax.lax.top_k(prob, TOPK)
        mask = jnp.zeros((n, NBLK), bool).at[jnp.arange(n)[:, None], idx].set(True)
        w1b = w1.reshape(NBLK, BLOCK, IN_F)
        b1b = b1.reshape(NBLK, BLOCK)
        h = jnp.einsum('nd,ibd->nib', xf, w1b) + b1b
        h = jnp.where(mask[:, :, None], h, jnp.zeros((), h.dtype))
        h = jax.nn.relu(h)
        w2b = w2.reshape(IN_F, NBLK, BLOCK)
        y = jnp.einsum('nib,dib->nd', jnp.where(mask[:, :, None], h, 0.0), w2b) + b2
        return y.reshape(x_shape)
    x = x + _L0_xattn_ref(_layernorm(x, axis=-1), ctx_1024, ctx_1024)
    x = x + _L0_ffn_ref(_layernorm(x, axis=-1), L0_ffn_gate_w, L0_ffn_w_gate, L0_ffn_w_up, L0_ffn_w_down)
    x = x + _L1_xattn_ref(_layernorm(x, axis=-1), ctx_1024, L1_xattn_Wq, L1_xattn_Wk, L1_xattn_Wv, L1_xattn_Wo)
    x = x + _L1_ffn_ref(_layernorm(x, axis=-1), L1_ffn_router_w, L1_ffn_router_b, L1_ffn_w1, L1_ffn_b1, L1_ffn_w2, L1_ffn_b2)
    return x

_drawn_inputs = setup_inputs


def setup_inputs(seed=0):
    import zlib

    import numpy as np

    out = dict(_drawn_inputs(seed))
    spreads = {}
    factors = {'L0_ffn_gate_w': 6.568,
     'L0_ffn_w_gate': 6.615,
     'L0_ffn_w_up': 7.138,
     'L0_ffn_w_down': 6.801,
     'L1_ffn_b1': 29.01,
     'L1_ffn_b2': 10.51,
     'L1_xattn_Wq': 7.724,
     'L1_xattn_Wk': 7.645,
     'L1_ffn_router_b': 6.097}
    for name, (base, spread) in spreads.items():
        noise = np.random.default_rng([zlib.crc32(name.encode()), seed]).standard_normal(out[name].shape)
        drawn = base * np.exp(spread * noise) if base else spread * noise
        out[name] = jnp.asarray(drawn.astype(out[name].dtype))
    for name, factor in factors.items():
        out[name] = (out[name] * factor).astype(out[name].dtype)
    return out
```

```python
from contextlib import ExitStack

import numpy as np

import concourse.bass as bass
from concourse import mybir

F32 = mybir.dt.float32
BF16 = mybir.dt.bfloat16
I32 = mybir.dt.int32
ALU = mybir.AluOpType
ACT = mybir.ActivationFunctionType
AX = mybir.AxisListType

P = 128
BATCH, SEQ, D = 8, 256, 256
TOK = BATCH * SEQ
TILES = TOK // P
DC = D // P
HEADS, DH = 16, 16
HSTEP = HEADS // 2
STEPS = 2 * BATCH
TERMS = 6
ROWS = TERMS * DH
MROWS = 2
VW = 32
EPS = 1e-5
MASKED = -1e30

EXPERTS, TOP_K, FF = 64, 8, 192
FH = FF // 2
ETILES = -(-((TOK * TOP_K + EXPERTS * (P - 1)) // P) // 4) * 4
ETABLE = 256
LISTS = EXPERTS * TILES
WRING = 4

BLOCKS, TOP_B, HID = 16, 4, 1024
FC = HID // P

K_PARTS = [(0, 3), (0, 2), (0, 1)]
Q_PARTS = [(0, 3), (1, 2), (2, 1)]


def wait(eng, sem, count):
    if not (isinstance(count, int) and count <= 0):
        eng.wait_ge(sem, count)


def phase_semaphores(nc, ctx, prefix, used):
    def make(name):
        used.append(ctx.enter_context(nc.semaphore(f"{prefix}_{name}")))
        return used[-1]
    return make


def sweep(nc, used):
    with nc.Block() as block:

        @block.sync
        def _(sp):
            for sem in used:
                sp.sem_clear(sem)


NEWTON_STEPS = 4


def refine(nc, own, n, rstd, variance, scratch):
    nc.vector.tensor_tensor(scratch, rstd, rstd, ALU.mult).then_inc(own, 1)
    nc.vector.wait_ge(own, n + 1)
    nc.vector.scalar_tensor_tensor(scratch, variance, EPS, scratch, ALU.add, ALU.mult).then_inc(own, 1)
    nc.vector.wait_ge(own, n + 2)
    nc.vector.tensor_scalar(scratch, scratch, -0.5, 1.5, ALU.mult, ALU.add).then_inc(own, 1)
    nc.vector.wait_ge(own, n + 3)
    nc.vector.tensor_tensor(rstd, rstd, scratch, ALU.mult).then_inc(own, 1)
    nc.vector.wait_ge(own, n + NEWTON_STEPS)


class Kernel:
    pass


def constants(nc, k, ctx):
    sb = lambda name, shape, dt: ctx.enter_context(nc.sbuf_tensor(name, shape, dt))
    k.ident = sb("ident", [P, P], F32)
    k.ident_b = sb("ident_b", [P, P], BF16)
    k.mask_qk = sb("mask_qk", [P, P], BF16)
    k.mask_kq = sb("mask_kq", [P, P], BF16)
    loaded = ctx.enter_context(nc.semaphore("constants_loaded"))
    with nc.Block() as block:

        @block.sync
        def _(sp):
            pairs = [(k.ident, "c_ident"), (k.ident_b, "c_ident_b"), (k.mask_qk, "c_mask_qk"), (k.mask_kq, "c_mask_kq")]
            for tile, name in pairs:
                sp.dma_start(tile[:], k.dram[name]).then_inc(loaded, 16)
            sp.wait_ge(loaded, 16 * len(pairs))


def prepare(nc, k):
    with ExitStack() as ctx:
        sb = lambda name, shape, dt: ctx.enter_context(nc.sbuf_tensor(name, shape, dt))
        used = []
        sem = phase_semaphores(nc, ctx, "prep", used)
        ctx_t = sb("ctx_t", [P, 2, DC, SEQ], F32)
        wk = sb("wk", [P, DC, DC, P], F32)
        wv = sb("wv", [P, DC, D], F32)
        stats = sb("ln0_stats", [P, 2, 6], F32)
        moments = sb("ln0_moments", [P, 2, 2], F32)
        deviation = sb("ln0_deviation", [P, 2], F32)
        rstd = sb("ln0_rstd", [P, 2], F32)
        newton = sb("ln0_newton", [P, 2], F32)
        eps = sb("ln0_eps", [P, 1], F32)
        xn = sb("ln0_out", [P, 2, 2, D], F32)
        rest = sb("split_rest", [P, 2, 3, DC * SEQ], F32)
        parts = sb("split_parts", [P, 2, 3, 3, DC * SEQ], BF16)
        v1 = sb("v1", [P, 2, 2, D], F32)
        ps = ctx.enter_context(nc.psum_tensor("ps_prep", [P, 8, 512], F32))
        w_in = sem("w_in")
        x_in = [sem("x_in0"), sem("x_in1")]
        c_in = [sem("ctx_in0"), sem("ctx_in1")]
        own = sem("own")
        eps_set = sem("eps_set")
        moments_ready = sem("moments")
        deviations = sem("deviations")
        xn_ready = sem("xn_ready")
        q_turned = sem("q_turned")
        k1_ready = sem("k1_ready")
        v1_ready = sem("v1_ready")
        high = sem("high")
        rested = sem("rested")
        middle = sem("middle")
        split = sem("split")
        v1_out = sem("v1_out")
        written = [sem("written0"), sem("written1")]
        WRITES = 10
        K0, Q0, K1 = 0, 1, 2
        stacks = {K0: k.k0_stack, Q0: k.q0_stack, K1: k.k1_stack}

        def source(kind, u):
            if kind == K0:
                return ctx_t[:, u].rearrange("p c t -> p (c t)")
            return ps[:, (0 if kind == Q0 else 2) + u, :]

        with nc.Block() as block:

            @block.sync
            def _(sp):
                sp.dma_start(wk[:], k.dram["wk"]).then_inc(w_in, 16)
                sp.dma_start(wv[:], k.dram["wv"]).then_inc(w_in, 16)

                def load(b, u):
                    sp.dma_start(k.x[:, bass.ds(2 * b, 2), :],
                                 k.dram["x"][bass.ds(2 * b, 2)].rearrange("t p d -> p t d")).then_inc(x_in[u], 16)
                    sp.dma_start(ctx_t[:, u], k.dram["ctx_t"][bass.ds(b, 1)].rearrange("b p c t -> (b p) c t")).then_inc(c_in[u], 16)

                def write(b, u):
                    for kind in (K0, Q0, K1):
                        sp.wait_ge(split, 3 * b + kind + 1)
                        stack = stacks[kind][bass.ds(b, 1)].rearrange("b t p n -> p (b t) n")
                        t = 0
                        for first, n in (Q_PARTS if kind == Q0 else K_PARTS):
                            if kind == Q0:
                                src = parts[:, u, kind, first:first + 1, :].to_broadcast([P, n, DC * SEQ])
                            else:
                                src = parts[:, u, kind, first:first + n, :]
                            sp.dma_start(stack[:, t:t + n, :], src).then_inc(written[u], 16)
                            t += n
                    sp.wait_ge(v1_out, b + 1)
                    sp.dma_start(k.v1[bass.ds(b, 1)].rearrange("b t p d -> p (b t) d"), v1[:, u]).then_inc(written[u], 16)

                load(0, 0)
                load(1, 1)
                with sp.Fori(0, BATCH // 2 - 1) as i:
                    for u in range(2):
                        write(2 * i + u, u)
                        load(2 * i + u + 2, u)
                for u in range(2):
                    write(BATCH - 2 + u, u)
                for u in range(2):
                    sp.wait_ge(written[u], 16 * WRITES * (BATCH // 2))

            @block.vector
            def _(dve):
                with dve.Fori(0, BATCH // 2) as i:
                    for u in range(2):
                        b = 2 * i + u
                        dve.sem_clear(own)
                        dve.wait_ge(x_in[u], 16 * i + 16)
                        for j in range(2):
                            nc.vector.bn_stats(stats[:, j, :], k.x[:, bass.ds(2 * b + j, 1), :].rearrange("p a d -> p (a d)")).then_inc(own, 1)
                        for j in range(2):
                            dve.wait_ge(own, 1 + j)
                            nc.vector.bn_aggr(moments[:, j, :], stats[:, j, :]).then_inc(moments_ready, 1)
                        dve.wait_ge(deviations, b + 1)
                        nc.vector.reciprocal(rstd[:], deviation[:]).then_inc(own, 1)
                        dve.wait_ge(own, 3)
                        refine(nc, own, 3, rstd[:], moments[:, :, 1], newton[:])
                        for j in range(2):
                            nc.vector.tensor_scalar(xn[:, u, j, :].rearrange("p (c d h) -> p c h d", c=DC, d=DH),
                                                    k.x[:, bass.ds(2 * b + j, 1), :].rearrange("p a (c h d) -> p (a c) h d", c=DC, d=DH),
                                                    moments[:, j, 0:1], rstd[:, j:j + 1], ALU.subtract, ALU.mult).then_inc(xn_ready, 1)
                        for kind in (K0, Q0, K1):
                            dve.wait_ge(high, 3 * b + kind + 1)
                            nc.vector.tensor_tensor(rest[:, u, kind, :], source(kind, u), parts[:, u, kind, 0, :],
                                                    ALU.subtract).then_inc(rested, 1)

            @block.scalar
            def _(act):
                def take_middle(b, u, kind):
                    act.wait_ge(rested, 3 * b + kind + 1)
                    nc.scalar.copy(parts[:, u, kind, 1, :], rest[:, u, kind, :]).then_inc(middle, 1)

                def batch(i, u, first):
                    b = 2 * i + u
                    act.wait_ge(moments_ready, 2 * b + 2)
                    nc.scalar.activation(deviation[:], moments[:, :, 1], ACT.Sqrt, bias=eps[:, 0:1]).then_inc(deviations, 1)
                    if not first:
                        act.wait_ge(written[u], 16 * WRITES * i)
                    act.wait_ge(c_in[u], 16 * i + 16)
                    nc.scalar.copy(parts[:, u, K0, 0, :], source(K0, u)).then_inc(high, 1)
                    act.wait_ge(q_turned, b + 1)
                    nc.scalar.copy(parts[:, u, Q0, 0, :], source(Q0, u)).then_inc(high, 1)
                    take_middle(b, u, K0)
                    act.wait_ge(k1_ready, b + 1)
                    nc.scalar.copy(parts[:, u, K1, 0, :], source(K1, u)).then_inc(high, 1)
                    take_middle(b, u, Q0)
                    act.wait_ge(v1_ready, b + 1)
                    nc.scalar.copy(v1[:, u].rearrange("p t d -> p (t d)"), ps[:, 4 + u, :]).then_inc(v1_out, 1)
                    take_middle(b, u, K1)

                act.wait_ge(eps_set, 1)
                batch(0, 0, True)
                batch(0, 1, True)
                with act.Fori(1, BATCH // 2) as i:
                    for u in range(2):
                        batch(i, u, False)

            @block.gpsimd
            def _(pool):
                nc.gpsimd.memset(eps[:], EPS).then_inc(eps_set, 1)

                def low(b, u, kind):
                    pool.wait_ge(middle, 3 * b + kind + 1)
                    nc.gpsimd.tensor_tensor(parts[:, u, kind, 2, :], rest[:, u, kind, :], parts[:, u, kind, 1, :],
                                            ALU.subtract).then_inc(split, 1)

                with pool.Fori(0, BATCH // 2) as i:
                    for u in range(2):
                        for kind in (K0, Q0, K1):
                            low(2 * i + u, u, kind)

            @block.tensor
            def _(pe):
                pe.wait_ge(w_in, 32)

                def batch(i, u, first):
                    b = 2 * i + u
                    pe.wait_ge(xn_ready, 2 * b + 2)
                    if not first:
                        pe.wait_ge(rested, 3 * b - 3)
                        pe.wait_ge(v1_out, b - 1)
                    for j in range(2):
                        for c in range(DC):
                            last = pe.transpose(ps[:, u, c * SEQ + j * P:c * SEQ + (j + 1) * P],
                                                xn[:, u, j, c * P:(c + 1) * P], k.ident[:])
                    last.then_inc(q_turned, 1)
                    pe.wait_ge(c_in[u], 16 * i + 16)
                    for m in range(DC):
                        for c in range(DC):
                            last = pe.matmul(ps[:, 2 + u, m * SEQ:(m + 1) * SEQ], wk[:, c, m, :], ctx_t[:, u, c, :],
                                             start=(c == 0), stop=(c == DC - 1))
                    last.then_inc(k1_ready, 1)
                    for j in range(2):
                        for c in range(DC):
                            last = pe.matmul(ps[:, 4 + u, j * D:(j + 1) * D], ctx_t[:, u, c, j * P:(j + 1) * P], wv[:, c, :],
                                             start=(c == 0), stop=(c == DC - 1))
                    last.then_inc(v1_ready, 1)

                batch(0, 0, True)
                batch(0, 1, True)
                with pe.Fori(1, BATCH // 2) as i:
                    for u in range(2):
                        batch(i, u, False)
        sweep(nc, used)


def attention(nc, k, name, q_stack, k_stack, values, scale, causal, out):
    blocks = 3 if causal else 4
    cols = blocks * P
    LAG = 2
    with ExitStack() as ctx:
        sb = lambda n, shape, dt: ctx.enter_context(nc.sbuf_tensor(f"{name}_{n}", shape, dt))
        used = []
        sem = phase_semaphores(nc, ctx, name, used)
        kst = sb("kst", [ROWS + MROWS, 4, HSTEP, SEQ], BF16)
        qst = sb("qst", [ROWS + MROWS, 4, HSTEP, SEQ], BF16)
        v_raw = sb("v_raw", [P, 2, 2, D], F32)
        v_aug = sb("v_aug", [P, 2, 2, HEADS, VW], F32)
        probs = sb("probs", [P, HSTEP, 4 * P], F32)
        blockmax = sb("blockmax", [P, 2, HSTEP, 3], F32)
        negmax = sb("negmax", [P, 2, 2, HSTEP], F32)
        maxparts = sb("maxparts", [P, 2, 2, 2, HSTEP], BF16)
        maxrows = sb("maxrows", [2 * HSTEP, 2, SEQ], BF16)
        turned_in = sb("turned_in", [P, 2, SEQ], F32)
        recip = sb("recip", [P, 2, HSTEP], F32)
        ps = ctx.enter_context(nc.psum_tensor(f"{name}_ps", [P, 8, 512], F32))
        outs_dq = ps[:, 6, 0:SEQ]
        max_t = ps[0:2 * HSTEP, 6, SEQ:SEQ + P].bitcast(BF16)
        outs_qd = ps[:, 7, :].rearrange("p (j n) -> p j n", j=2)

        stack_in = [sem(f"stack_in{j}") for j in range(4)]
        v_in = [sem("v_in0"), sem("v_in1")]
        max_in = [sem(f"max_in{j}") for j in range(4)]
        ones_set = sem("ones_set")
        v_ready = sem("v_ready")
        own = sem("own")
        cut_step = sem("cut_step")
        recips = sem("recips")
        s_ready = sem("s_ready")
        s_free = sem("s_free")
        max_ready = sem("max_ready")
        max_turned = sem("max_turned")
        max_copied = sem("max_copied")
        t_ready = sem("t_ready")
        exped = sem("exped")
        pv_done = sem("pv_done")
        out_copied = sem("out_copied")
        out_turned = sem("out_turned")
        divided = sem("divided")

        def emit(eng, step, last=STEPS // 4):
            for u in range(4):
                step((0, u))
            with eng.Fori(1, last) as i:
                for u in range(4):
                    step((i, u))
            for i in range(last, STEPS // 4 + 1):
                for u in range(4):
                    step((i, u))

        def after(st, n):
            i, u = st
            return i + (u + n) // 4, (u + n) % 4

        def number(st):
            return 4 * st[0] + st[1]

        def batch_of(st):
            return 2 * st[0] + st[1] // 2

        def scores(st):
            return not isinstance(st[0], int) or 0 <= number(st) < STEPS

        with nc.Block() as block:

            @block.sync
            def _(sp):
                half = HSTEP * SEQ

                def load(st):
                    i, u = st
                    b, part = batch_of(st), u % 2
                    for stack, tile in ((q_stack, qst), (k_stack, kst)):
                        rows = stack[bass.ds(b, 1)].rearrange("b t (d h) n -> (b t d) (h n)", d=DH)
                        sp.dma_start(tile[0:ROWS, u].rearrange("p s n -> p (s n)"),
                                     rows[:, part * half:(part + 1) * half]).then_inc(stack_in[u], 16)
                    if part == 0:
                        wait(sp, v_ready, b - 1)
                        sp.dma_start(v_raw[:, u // 2], values[bass.ds(b, 1)].rearrange("b t p d -> p (b t) d")).then_inc(v_in[u // 2], 16)

                def step(st):
                    if scores(after(st, 1)):
                        wait(sp, t_ready, HSTEP * (number(st) - LAG))
                        load(after(st, 1))
                    before = after(st, -1)
                    if scores(before):
                        sp.wait_ge(max_copied, number(before) + 1)
                        v = before[1]
                        for part in range(MROWS):
                            sp.dma_start(qst[ROWS + part:ROWS + part + 1, v],
                                         maxrows[part * HSTEP:(part + 1) * HSTEP, v % 2, :]).then_inc(max_in[v], 16)

                load((0, 0))
                emit(sp, step, last=STEPS // 4 - 1)

            @block.tensor
            def _(pe):
                def scores_qk(st, s):
                    i, u = st
                    h = number(st)
                    if s == 0:
                        pe.wait_ge(stack_in[u], 32 * i + 32)
                    wait(pe, s_free, HSTEP * h + s - 1)
                    bank = ps[:, s % 2, :]
                    for j in range(2):
                        keys = SEQ if not causal or j else P
                        at = j * (P if causal else SEQ)
                        last = pe.matmul(bank[:, at:at + keys], qst[0:ROWS, u, s, j * P:(j + 1) * P], kst[0:ROWS, u, s, 0:keys],
                                         start=True, stop=True)
                        if causal:
                            last = pe.matmul(bank[:, 2 * j * P:(2 * j + 1) * P], k.ident_b[:], k.mask_qk[:], start=False, stop=True,
                                             skip_group_check=True)
                    last.then_inc(s_ready, 1)

                def scores_kq(st, s):
                    i, u = st
                    h = number(st)
                    if s == 0:
                        pe.wait_ge(max_in[u], 32 * i + 32)
                    wait(pe, exped, HSTEP * h + s - 3)
                    bank = ps[:, 2 + s % 4, :]
                    for j in range(2):
                        first = P if causal and j else 0
                        at = j * SEQ
                        last = pe.matmul(bank[:, at:at + SEQ - first], kst[:, u, s, j * P:(j + 1) * P], qst[:, u, s, first:SEQ],
                                         start=True, stop=True)
                        if causal:
                            last = pe.matmul(bank[:, at:at + P], k.ident_b[:], k.mask_kq[:], start=False, stop=True,
                                             skip_group_check=True)
                    last.then_inc(t_ready, 1)

                def outputs(st, g):
                    i, u = st
                    h = number(st)
                    pe.wait_ge(exped, HSTEP * h + 4 * g + 4)
                    wait(pe, out_copied, 2 * h + g)
                    b_par = u // 2
                    if g == 0:
                        pe.wait_ge(max_copied, min(h + LAG, STEPS) if isinstance(h, int) else h + LAG)
                    if g == 0 and u % 2 == 0:
                        pe.wait_ge(v_ready, batch_of(st) + 1)
                    for j in range(2):
                        first = P if causal and j else 0
                        for r in range(4):
                            s = HSTEP * (u % 2) + 4 * g + r
                            last = pe.matmul(outs_dq[VW * r:VW * (r + 1), first:SEQ], v_aug[:, b_par, j, s, :],
                                             probs[:, 4 * g + r, j * SEQ:j * SEQ + SEQ - first],
                                             start=(j == 0), stop=(j == 1), skip_group_check=True)
                    last.then_inc(pv_done, 1)

                def turn_outputs(st, g):
                    h = number(st)
                    pe.wait_ge(out_copied, 2 * h + g + 1)
                    if g == 0:
                        wait(pe, divided, h)
                    for j in range(2):
                        last = pe.transpose(outs_qd[:, j, g * P:(g + 1) * P], turned_in[:, g, j * P:(j + 1) * P], k.ident[:])
                    last.then_inc(out_turned, 1)

                def turn_maxima(st):
                    h, u = number(st), st[1]
                    pe.wait_ge(max_ready, h + 1)
                    wait(pe, out_copied, 2 * h - 2)
                    for j in range(2):
                        last = pe.transpose(max_t[:, j * P:(j + 1) * P],
                                            maxparts[:, u % 2, j].rearrange("p a s -> p (a s)"), k.ident_b[:])
                    last.then_inc(max_turned, 1)

                pe.wait_ge(ones_set, 1)

                def step(st):
                    t = after(st, -LAG)
                    for s in range(HSTEP):
                        if scores(st):
                            scores_qk(st, s)
                        if scores(t):
                            scores_kq(t, s)
                        if s == 0 and scores(after(t, -1)):
                            turn_outputs(after(t, -1), 0)
                        if s == 1 and scores(after(t, -1)):
                            outputs(after(t, -1), 1)
                        if s == 3 and scores(after(t, -1)):
                            turn_outputs(after(t, -1), 1)
                        if s == 4 and scores(after(st, -1)):
                            turn_maxima(after(st, -1))
                        if s == 6 and scores(t):
                            outputs(t, 0)

                emit(pe, step)

            @block.vector
            def _(dve):
                nc.vector.memset(kst[ROWS:ROWS + MROWS], 1.0).then_inc(ones_set, 1)

                def reduce(st, s):
                    h, u = number(st), st[1]
                    dve.wait_ge(s_ready, HSTEP * h + s + 1)
                    if causal:
                        nc.vector.tensor_reduce(blockmax[:, u % 2, s, :], ps[:, s % 2, 0:cols].rearrange("p (b n) -> p b n", n=P),
                                                AX.X, ALU.max, negate=True).then_inc(s_free, 1)
                    else:
                        nc.vector.tensor_reduce(negmax[:, u % 2, :, s], ps[:, s % 2, :].rearrange("p (j n) -> p j n", j=2),
                                                AX.X, ALU.max, negate=True).then_inc(s_free, 1)

                def cut(st):
                    h, u = number(st), st[1]
                    v = u % 2
                    dve.wait_ge(s_free, HSTEP * h + HSTEP)
                    if causal:
                        nc.vector.tensor_copy(negmax[:, v, 0, :], blockmax[:, v, :, 0]).then_inc(cut_step, 1)
                        nc.vector.tensor_tensor(negmax[:, v, 1, :], blockmax[:, v, :, 1], blockmax[:, v, :, 2], ALU.min).then_inc(cut_step, 1)
                        dve.wait_ge(cut_step, 3 * h + 2)
                    wait(dve, max_turned, h - 1)
                    nc.vector.tensor_copy(maxparts[:, v, :, 0, :], negmax[:, v]).then_inc(cut_step, 1)
                    per = 3 if causal else 1
                    dve.wait_ge(cut_step, per * h + per)
                    nc.vector.tensor_tensor(maxparts[:, v, :, 1, :], negmax[:, v], maxparts[:, v, :, 0, :], ALU.subtract).then_inc(max_ready, 1)

                def divide(st):
                    h, b, half = number(st), batch_of(st), st[1] % 2
                    dve.wait_ge(out_turned, 2 * h + 2)
                    o = outs_qd.rearrange("p j (s e) -> p j s e", e=VW)
                    nc.vector.reciprocal(recip[:], o[:, :, :, DH]).then_inc(recips, 1)
                    dve.wait_ge(recips, h + 1)
                    for j in range(2):
                        dst = out[:, bass.ds(2 * b + j, 1), :].rearrange("p a (c h d) -> p (a c) h d", c=DC, d=DH)
                        dst = dst[:, :, 4 * half:4 * half + 4, :].rearrange("p c h d -> p h c d")
                        last = nc.vector.tensor_tensor(dst, o[:, j, :, 0:DH].rearrange("p (h c) d -> p h c d", c=DC),
                                                       recip[:, j, :].rearrange("p (h c) -> p h c", c=DC).unsqueeze(3).to_broadcast([P, 4, DC, DH]),
                                                       ALU.mult)
                    last.then_inc(divided, 1)


                def step(st):
                    before = after(st, -LAG - 1)
                    for s in range(HSTEP):
                        if scores(st):
                            reduce(st, s)
                        if s == 5 and scores(before):
                            divide(before)
                    if scores(st):
                        cut(st)

                emit(dve, step)

            @block.scalar
            def _(act):
                nc.scalar.memzero(v_aug[:]).then_inc(own, 1)
                act.wait_ge(own, 1)
                nc.scalar.activation(v_aug[:, :, :, :, DH], v_aug[:, :, :, :, DH], ACT.Exp).then_inc(own, 1)

                def exponential(st, s):
                    h = number(st)
                    act.wait_ge(t_ready, HSTEP * h + s + 1)
                    if s % 4 == 0:
                        wait(act, pv_done, 2 * h - 1 + s // 4)
                    nc.scalar.activation(probs[:, s, 0:cols], ps[:, 2 + s % 4, 0:cols], ACT.Exp, scale=scale).then_inc(exped, 1)

                def copy_values(st):
                    b, v = batch_of(st), st[1] // 2
                    act.wait_ge(v_in[v], 16 * st[0] + 16)
                    wait(act, pv_done, 4 * b - 4)
                    for j in range(2):
                        done = nc.scalar.copy(v_aug[:, v, j, :, 0:DH].rearrange("p (h c) d -> p c h d", c=DC),
                                              v_raw[:, v, j, :].rearrange("p (c h d) -> p c h d", c=DC, d=DH))
                    done.then_inc(v_ready, 1)

                def copy_outputs(st, g):
                    h = number(st)
                    act.wait_ge(pv_done, 2 * h + g + 1)
                    wait(act, out_turned, 2 * h + g - 1)
                    nc.scalar.copy(turned_in[:, g, :], outs_dq).then_inc(out_copied, 1)

                def copy_maxima(st):
                    h, u = number(st), st[1]
                    act.wait_ge(max_turned, h + 1)
                    old = after(st, -2)
                    if scores(old):
                        act.wait_ge(max_in[old[1]], 32 * old[0] + 32)
                    nc.scalar.copy(maxrows[:, u % 2, :], max_t).then_inc(max_copied, 1)

                act.wait_ge(own, 2)

                def step(st):
                    t = after(st, -LAG)
                    for s in range(HSTEP):
                        if scores(t):
                            exponential(t, s)
                        if s == 2 and scores(after(t, -1)):
                            copy_outputs(after(t, -1), 1)
                        if s == 4 and scores(after(st, -1)):
                            copy_maxima(after(st, -1))
                        if s == 5 and st[1] % 2 and scores(st):
                            copy_values(st)
                        if s == 7 and scores(t):
                            copy_outputs(t, 0)

                emit(act, step)
        sweep(nc, used)


def pass_on(eng, sem, count, passed):
    eng.wait_ge(sem, count)
    eng.sem_inc(passed, 1)


def route(nc, k):
    with ExitStack() as ctx:
        sb = lambda n, shape, dt: ctx.enter_context(nc.sbuf_tensor(f"rt_{n}", shape, dt))
        used = []
        sem = phase_semaphores(nc, ctx, "rt", used)
        E = EXPERTS
        gate = sb("gate", [P, DC, E], F32)
        before = sb("before", [P, P], BF16)
        ones = sb("ones", [P, P], BF16)
        list_end = sb("list_end", [P, E], F32)
        token = sb("token", [P, TILES], I32)
        tile_no = sb("tile_no", [P, 2], F32)
        zeros = sb("zeros", [P, LISTS], I32)
        eps = sb("eps", [P, 1], F32)
        stats = sb("stats", [P, TILES, 6], F32)
        moments = sb("moments", [P, TILES, 2], F32)
        deviation = sb("deviation", [P, TILES], F32)
        rstd = sb("rstd", [P, TILES], F32)
        newton = sb("newton", [P, TILES], F32)
        xn = sb("xn", [P, 2, D], F32)
        xn_t = sb("xn_t", [P, 2, DC * P], F32)
        logits = sb("logits", [P, TILES, E], F32)
        others = sb("others", [P, TILES, E], F32)
        best = sb("best", [P, TILES, 8], F32)
        mask = sb("mask", [P, TILES, E], F32)
        mask_b = sb("mask_b", [P, TILES, E], BF16)
        earlier = sb("earlier", [P, TILES + 1, E], BF16)
        expo = sb("expo", [P, TILES, E], F32)
        chosen = sb("chosen", [P, TILES, E], F32)
        total = sb("total", [P, 3, TILES], F32)
        place = sb("place", [P, TILES, E], F32)
        place_g = sb("place_g", [P, TILES, E], F32)
        top = sb("top", [P, 2, TILES, TOP_K], F32)
        slot = sb("slot", [P, TILES, TOP_K], I32)
        idx = sb("idx", [P, 2, TOP_K + 1], I32)
        count = sb("count", [P, 6, E], F32)
        count_i = sb("count_i", [P, E], I32)
        end_g = sb("end_g", [P, E], F32)
        below = sb("below", [P, 2, 3, E], F32)
        sums = sb("sums", [P, 2, 4], F32)
        distinct = sb("distinct", [P, 1], F32)
        row = sb("row", [P, 2], F32)
        row_i = sb("row_i", [P, 2], I32)
        ids_raw = sb("ids_raw", [P, 2, P], I32)
        ids_f = sb("ids_f", [P, 2, P], F32)
        line = sb("line", [1, 3, ETABLE], F32)
        line_i = sb("line_i", [1, ETABLE], I32)
        ps = ctx.enter_context(nc.psum_tensor("rt_ps", [P, 8, 512], F32))
        logit_ps = ps[:, 2:4, :].rearrange("p b (t e) -> p (b t) e", e=E)
        rank_ps = ps[:, 4:6, :].rearrange("p b (t e) -> p (b t) e", e=E)
        count_ps = ps[:, 6, 0:E]

        c_in = sem("constants_in")
        zero_set, zeroed = sem("zero_set"), sem("lists_zeroed")
        eps_set = sem("eps_set")
        x_ready, stats_done, moments_done = sem("x_ready"), sem("stats_done"), sem("moments_done")
        deviations, recips = sem("deviations"), sem("recips")
        xn_ready, xn_turned, xn_copied, logits_ready = sem("xn_ready"), sem("xn_turned"), sem("xn_copied"), sem("logits_ready")
        xn_out = [sem("xn_out0"), sem("xn_out1")]
        own = sem("own")
        shifted, exped, weights_ready, weights_out = sem("shifted"), sem("exped"), sem("weights_ready"), sem("weights_out")
        counted, ranked = sem("counted"), sem("ranked")
        slots_ready, staged = sem("slots_ready"), sem("staged")
        scattered = [sem("scattered0"), sem("scattered1")]
        rows_ready, ids_in, ids_f_ready, turned = sem("rows_ready"), sem("ids_in"), sem("ids_f_ready"), sem("turned")
        CONSTANTS = [(gate, "gate"), (before, "c_before"), (ones, "c_ones"), (list_end, "c_list_end"), (token, "c_token"), (tile_no, "c_tile")]
        GEND = float((ETILES + 1) * P)

        with nc.Block() as block:

            @block.sync
            def _(sp):
                for tile, name in CONSTANTS:
                    sp.dma_start(tile[:], k.dram[name]).then_inc(c_in, 16)
                sp.wait_ge(zero_set, 1)
                sp.dma_start(k.lists.rearrange("(p n) o -> p (n o)", p=P), zeros[:]).then_inc(zeroed, 16)
                with sp.Fori(0, TILES // 2) as i:
                    for u in range(2):
                        t = 2 * i + u
                        sp.wait_ge(xn_ready, t + 1)
                        sp.dma_start(k.xn[bass.ds(t, 1)].rearrange("t p d -> (t p) d")[:, 0:D], xn[:, u]).then_inc(xn_out[u], 16)
                sp.wait_ge(weights_ready, 1)
                sp.dma_start(k.xn.rearrange("t p d -> p t d")[:, :, D:D + E], chosen[:]).then_inc(weights_out, 16)
                sp.wait_ge(weights_out, 16)
                sp.wait_ge(xn_out[0], 16 * (TILES // 2))
                sp.wait_ge(xn_out[1], 16 * (TILES // 2))

            @block.gpsimd
            def _(pool):
                nc.gpsimd.memset(zeros[:], 0).then_inc(zero_set, 1)
                pool.wait_ge(zero_set, 1)
                nc.gpsimd.memset(eps[:], EPS).then_inc(eps_set, 1)
                with pool.Fori(0, TILES) as t:
                    nc.gpsimd.tensor_tensor(k.x[:, bass.ds(t, 1), :], k.x[:, bass.ds(t, 1), :], k.ao[:, bass.ds(t, 1), :], ALU.add).then_inc(x_ready, 1)
                pool.wait_ge(slots_ready, 1)
                pool.wait_ge(c_in, 16 * len(CONSTANTS))
                pool.wait_ge(zeroed, 16)

                def scatter(t, u):
                    nc.gpsimd.tensor_copy(idx[:, u, 0:TOP_K], slot[:, bass.ds(t, 1), :].rearrange("p a s -> p (a s)")).then_inc(staged, 1)
                    nc.gpsimd.tensor_copy(idx[:, u, TOP_K:TOP_K + 1], token[:, bass.ds(t, 1)]).then_inc(staged, 1)
                    pass_on(pool, staged, 2 * t + 2, k.passed)
                    for j in range(TOP_K):
                        nc.gpsimd.indirect_dma_start(k.lists, bass.IndirectOffsetOnAxis(ap=idx[:, u, j:j + 1], axis=0),
                                                     idx[:, u, TOP_K:TOP_K + 1], None).then_inc(scattered[u], 16)

                scatter(0, 0)
                scatter(1, 1)
                with pool.Fori(1, TILES // 2) as i:
                    for u in range(2):
                        pass_on(pool, scattered[u], 16 * TOP_K * i, k.passed)
                        scatter(2 * i + u, u)
                for u in range(2):
                    pool.wait_ge(scattered[u], 16 * TOP_K * (TILES // 2))
                pool.wait_ge(rows_ready, 2)
                for a in range(2):
                    nc.gpsimd.indirect_dma_start(ids_raw[:, a, :], None, k.lists.rearrange("(r n) o -> r (n o)", n=P),
                                                 bass.IndirectOffsetOnAxis(ap=row_i[:, a:a + 1], axis=0)).then_inc(ids_in, 16)
                pool.wait_ge(ids_in, 32)

            @block.scalar
            def _(act):
                act.wait_ge(eps_set, 1)
                act.wait_ge(moments_done, TILES)
                nc.scalar.activation(deviation[:], moments[:, :, 1], ACT.Sqrt, bias=eps[:, 0:1]).then_inc(deviations, 1)
                with act.Fori(0, TILES // 2) as i:
                    for u in range(2):
                        act.wait_ge(xn_turned, 2 * i + u + 1)
                        nc.scalar.copy(xn_t[:, u], ps[:, u, 0:DC * P]).then_inc(xn_copied, 1)
                act.wait_ge(shifted, 1)
                nc.scalar.activation(expo[:], expo[:], ACT.Exp).then_inc(exped, 1)

            @block.tensor
            def _(pe):
                pe.wait_ge(c_in, 16 * len(CONSTANTS))
                with pe.Fori(0, TILES // 2) as i:
                    for u in range(2):
                        t = 2 * i + u
                        pe.wait_ge(xn_ready, t + 1)
                        for c in range(DC):
                            last = pe.transpose(ps[:, u, c * P:(c + 1) * P], xn[:, u, c * P:(c + 1) * P], k.ident[:])
                        last.then_inc(xn_turned, 1)
                        pe.wait_ge(xn_copied, t + 1)
                        for c in range(DC):
                            last = pe.matmul(logit_ps[:, bass.ds(t, 1), :].rearrange("p a e -> p (a e)"), xn_t[:, u, c * P:(c + 1) * P],
                                             gate[:, c, :], start=(c == 0), stop=(c == DC - 1))
                        last.then_inc(logits_ready, 1)
                pe.wait_ge(counted, 1)
                half = TILES // 2
                for a in range(2):
                    ranks = rank_ps[:, a * half:(a + 1) * half, :]
                    pe.matmul(ranks, before[:], mask_b[:, a * half:(a + 1) * half, :], start=True, stop=False)
                    pe.matmul(ranks, ones[:], earlier[:, a * half:(a + 1) * half, :], start=False, stop=True)
                pe.matmul(count_ps, ones[:], earlier[:, TILES, :], start=True, stop=True).then_inc(ranked, 1)
                pe.wait_ge(rows_ready, 2)
                for a in range(2):
                    for q in range(2):
                        last = pe.transpose(ps[0:1, 7, (2 * q + a) * P:(2 * q + a + 1) * P], sums[:, a, q:q + 1], k.ident[:])
                last.then_inc(turned, 1)
                pe.wait_ge(ids_f_ready, 1)
                for a in range(2):
                    last = pe.transpose(ps[:, 6, a * P:(a + 1) * P], ids_f[:, a, :], k.ident[:])
                last.then_inc(turned, 1)

            @block.vector
            def _(dve):
                steps = [0]

                def then(ins):
                    ins.then_inc(own, 1)
                    steps[0] += 1
                    dve.wait_ge(own, steps[0])

                with dve.Fori(0, TILES) as t:
                    dve.wait_ge(x_ready, t + 1)
                    nc.vector.bn_stats(stats[:, bass.ds(t, 1), :].rearrange("p a s -> p (a s)"),
                                       k.x[:, bass.ds(t, 1), :].rearrange("p a d -> p (a d)")).then_inc(stats_done, 1)
                dve.wait_ge(stats_done, TILES)
                for t in range(TILES):
                    nc.vector.bn_aggr(moments[:, t, :], stats[:, t, :]).then_inc(moments_done, 1)
                dve.wait_ge(deviations, 1)
                then(nc.vector.reciprocal(rstd[:], deviation[:]))
                refine(nc, own, steps[0], rstd[:], moments[:, :, 1], newton[:])
                steps[0] += NEWTON_STEPS

                def normalise(t, u):
                    nc.vector.tensor_scalar(xn[:, u], k.x[:, bass.ds(t, 1), :].rearrange("p a d -> p (a d)"),
                                            moments[:, bass.ds(t, 1), 0:1].rearrange("p a s -> p (a s)"), rstd[:, bass.ds(t, 1)],
                                            ALU.subtract, ALU.mult).then_inc(xn_ready, 1)

                normalise(0, 0)
                normalise(1, 1)
                with dve.Fori(1, TILES // 2) as i:
                    for u in range(2):
                        dve.wait_ge(xn_turned, 2 * i + u - 1)
                        dve.wait_ge(xn_out[u], 16 * i)
                        normalise(2 * i + u, u)

                dve.wait_ge(logits_ready, TILES)
                then(nc.vector.tensor_copy(logits[:], logit_ps))
                for t in range(TILES):
                    last = nc.vector.max(best[:, t, :], logits[:, t, :])
                then(last)
                for t in range(TILES):
                    last = nc.vector.match_replace(others[:, t, :], best[:, t, :], logits[:, t, :], -3.0e38)
                then(last)
                then(nc.vector.tensor_tensor(mask_b[:], others[:], logits[:], ALU.not_equal))
                nc.vector.tensor_tensor(expo[:], logits[:], best[:, :, 0:1].to_broadcast([P, TILES, E]), ALU.subtract).then_inc(shifted, 1)
                then(nc.vector.memset(earlier[:, 0, :], 0.0))
                with dve.Fori(1, TILES + 1) as t:
                    dve.wait_ge(own, steps[0] - 1 + t)
                    nc.vector.tensor_tensor(earlier[:, bass.ds(t, 1), :], earlier[:, bass.ds(t - 1, 1), :], mask_b[:, bass.ds(t - 1, 1), :],
                                            ALU.add).then_inc(own, 1)
                steps[0] += TILES
                dve.wait_ge(own, steps[0])
                nc.vector.tensor_copy(mask[:], mask_b[:]).then_inc(counted, 1)
                dve.wait_ge(ranked, 1)
                dve.wait_ge(counted, 1)
                dve.wait_ge(c_in, 16 * len(CONSTANTS))

                def places(out, ends, place_q):
                    then(nc.vector.tensor_tensor(out[:], ends.unsqueeze(1).to_broadcast([P, TILES, E]), rank_ps, ALU.subtract))
                    then(nc.vector.tensor_tensor(out[:], out[:], mask[:], ALU.mult))
                    for t in range(TILES):
                        last = nc.vector.max(top[:, place_q, t, :], out[:, t, :])
                    then(last)

                places(place, list_end[:], 0)
                nc.vector.tensor_scalar(slot[:], top[:, 0], -1.0, float(E * TOK), ALU.mult, ALU.add).then_inc(slots_ready, 1)

                counts, tiles, ends, starts, one, some = (count[:, n, :] for n in range(6))
                then(nc.vector.tensor_scalar(count_i[:], count_ps, float(P - 1), None, ALU.add))
                then(nc.vector.tensor_scalar(count_i[:], count_i[:], 7, None, ALU.logical_shift_right))
                then(nc.vector.tensor_copy(tiles, count_i[:]))
                then(nc.vector.memset(one, 1.0))
                then(nc.vector.tensor_tensor_scan(ends, one, tiles, 0.0, ALU.mult, ALU.add))
                then(nc.vector.tensor_tensor(starts, ends, tiles, ALU.subtract))
                then(nc.vector.tensor_scalar(some, tiles, 0.5, None, ALU.is_gt))
                then(nc.vector.tensor_scalar(end_g[:], starts, -float(P), GEND, ALU.mult, ALU.add))
                then(nc.vector.tensor_reduce(distinct[:], some, AX.X, ALU.add))
                then(nc.vector.tensor_scalar(distinct[:], distinct[:], -1.0, None, ALU.add))
                for a in range(2):
                    then(nc.vector.tensor_scalar(below[:, a, 0, :], ends, tile_no[:, a:a + 1], None, ALU.is_le))
                    then(nc.vector.tensor_tensor(below[:, a, 1, :], below[:, a, 0, :], some, ALU.mult))
                    then(nc.vector.tensor_tensor(below[:, a, 2, :], below[:, a, 0, :], tiles, ALU.mult))
                    then(nc.vector.tensor_reduce(sums[:, a, 0:3], below[:, a], AX.X, ALU.add))
                    then(nc.vector.tensor_scalar(sums[:, a, 0:1], sums[:, a, 0:1], float(E - 1), None, ALU.min))
                    then(nc.vector.tensor_tensor(sums[:, a, 1:2], sums[:, a, 1:2], distinct[:], ALU.min))
                    then(nc.vector.tensor_tensor(sums[:, a, 3:4], tile_no[:, a:a + 1], sums[:, a, 2:3], ALU.subtract))
                    then(nc.vector.tensor_scalar(sums[:, a, 3:4], sums[:, a, 3:4], float(TILES - 1), None, ALU.min))
                    then(nc.vector.tensor_scalar(row[:, a:a + 1], sums[:, a, 0:1], float(TILES), None, ALU.mult))
                    nc.vector.tensor_tensor(row_i[:, a:a + 1], row[:, a:a + 1], sums[:, a, 3:4], ALU.add).then_inc(rows_ready, 1)

                places(place_g, end_g[:], 1)
                then(nc.vector.tensor_scalar(k.slot[:], top[:, 1], -1.0, GEND, ALU.mult, ALU.add))

                dve.wait_ge(exped, 1)
                then(nc.vector.tensor_tensor(chosen[:], expo[:], mask[:], ALU.mult))
                then(nc.vector.tensor_reduce(total[:, 0, :], expo[:], AX.X, ALU.add))
                then(nc.vector.tensor_reduce(total[:, 1, :], chosen[:], AX.X, ALU.add))
                then(nc.vector.scalar_tensor_tensor(total[:, 2, :], total[:, 0, :], 1e-20, total[:, 1, :], ALU.mult, ALU.add))
                then(nc.vector.reciprocal(total[:, 2, :], total[:, 2, :]))
                nc.vector.tensor_tensor(chosen[:], chosen[:], total[:, 2, :].unsqueeze(2).to_broadcast([P, TILES, E]),
                                        ALU.mult).then_inc(weights_ready, 1)

                dve.wait_ge(turned, 1)
                then(nc.vector.tensor_copy(line[:, 0:2, :].rearrange("p q n -> p (q n)"), ps[0:1, 7, :]))
                then(nc.vector.memset(line[:, 2, 0:1], 1.0))
                then(nc.vector.tensor_tensor(line[:, 2, 1:ETABLE], line[:, 1, 1:ETABLE], line[:, 1, 0:ETABLE - 1], ALU.not_equal))
                then(nc.vector.tensor_copy(k.table[:, 0, :], line[:, 0, :]))
                then(nc.vector.tensor_copy(line_i[:], line[:, 1, :]))
                then(nc.vector.tensor_scalar(k.table[:, 1, :], line_i[:], WRING - 1, None, ALU.bitwise_and))
                then(nc.vector.tensor_copy(k.table[:, 2, :], line[:, 2, :]))
                dve.wait_ge(ids_in, 32)
                nc.vector.tensor_copy(ids_f[:], ids_raw[:]).then_inc(ids_f_ready, 1)
                dve.wait_ge(turned, 2)
                then(nc.vector.tensor_copy(k.ids[:], ps[:, 6, 0:ETABLE]))
        sweep(nc, used)


def experts(nc, k):
    with ExitStack() as ctx:
        sb = lambda n, shape, dt: ctx.enter_context(nc.sbuf_tensor(f"ex_{n}", shape, dt))
        used = []
        sem = phase_semaphores(nc, ctx, "ex", used)
        R = 4
        w_gu = sb("w_gu", [P, WRING, DC, 2 * FF], F32)
        w_down = sb("w_down", [FH, WRING, 2, D], F32)
        idx = sb("idx", [P, R], I32)
        rows = sb("rows", [P, R, D + EXPERTS], F32)
        rows_t = sb("rows_t", [P, 2, DC * P], F32)
        act_g = sb("act_g", [P, 2, FF], F32)
        hidden = sb("hidden", [P, 2, FF], F32)
        hidden_t = sb("hidden_t", [FH, 2, 2 * P], F32)
        result = sb("result", [P, R, D], F32)
        ps = ctx.enter_context(nc.psum_tensor("ex_ps", [P, 8, 512], F32))
        w_in = [sem(f"w_in{j}") for j in range(R)]
        staged = sem("staged")
        rows_in = [sem(f"rows_in{j}") for j in range(R)]
        rows_turned, rows_copied = sem("rows_turned"), sem("rows_copied")
        gu_ready, silu_ready, hidden_ready = sem("gu_ready"), sem("silu_ready"), sem("hidden_ready")
        hidden_turned, hidden_copied, down_ready = sem("hidden_turned"), sem("hidden_copied"), sem("down_ready")
        result_ready = sem("result_ready")
        out_done = [sem(f"out_done{j}") for j in range(R)]
        ROUNDS = ETILES // R

        with nc.Block() as block:

            def rounds(eng, step, last=ROUNDS):
                for j in range(R):
                    step(0, j)
                with eng.Fori(1, last) as i:
                    for j in range(R):
                        step(i, j)

            @block.sync
            def _(sp):
                def step(i, j):
                    t = R * i + j
                    expert = sp.value_load(k.table[0:1, 0, bass.ds(t, 1)], min_val=0, max_val=EXPERTS - 1)
                    ring = sp.value_load(k.table[0:1, 1, bass.ds(t, 1)], min_val=0, max_val=WRING - 1)
                    other = sp.value_load(k.table[0:1, 2, bass.ds(t, 1)], min_val=0, max_val=1)
                    wait(sp, down_ready, t - R + 1)
                    sp.dma_start(w_gu[:, bass.ds(ring, 1)].rearrange("p a c n -> p (a c n)"),
                                 k.dram["w_gu"][bass.ds(expert, 1)].rearrange("e p c n -> (e p) (c n)"), cond=other > 0).then_inc(w_in[j], 16)
                    sp.dma_start(w_down[:, bass.ds(ring, 1)].rearrange("p a c n -> p (a c n)"),
                                 k.dram["w_down"][bass.ds(expert, 1)].rearrange("e p c n -> (e p) (c n)"), cond=other > 0).then_inc(w_in[j], 16)

                rounds(sp, step)

            @block.gpsimd
            def _(pool):
                def step(i, j):
                    t = R * i + j
                    if not isinstance(i, int):
                        pass_on(pool, result_ready, t - R + 1, k.passed)
                    nc.gpsimd.tensor_copy(idx[:, j:j + 1], k.ids[:, bass.ds(t, 1)]).then_inc(staged, 1)
                    pass_on(pool, staged, t + 1, k.passed)
                    nc.gpsimd.indirect_dma_start(rows[:, j, :], None, k.xn.rearrange("t p d -> (t p) d"),
                                                 bass.IndirectOffsetOnAxis(ap=idx[:, j:j + 1], axis=0)).then_inc(rows_in[j], 16)

                rounds(pool, step)

            @block.tensor
            def _(pe):
                def turn_rows(i, j):
                    t = R * i + j
                    pe.wait_ge(rows_in[j], 16 * i + 16)
                    wait(pe, rows_copied, t - 1)
                    for c in range(DC):
                        last = pe.transpose(ps[:, j % 2, c * P:(c + 1) * P], rows[:, j, c * P:(c + 1) * P], k.ident[:])
                    last.then_inc(rows_turned, 1)

                def gate_up(i, j, ring):
                    t = R * i + j
                    pe.wait_ge(w_in[j], 32 * i + 32)
                    pe.wait_ge(rows_copied, t + 1)
                    wait(pe, hidden_ready, t - 1)
                    for c in range(DC):
                        last = pe.matmul(ps[:, 2 + j % 2, 0:2 * FF], rows_t[:, j % 2, c * P:(c + 1) * P],
                                         w_gu[:, bass.ds(ring, 1), c, :].rearrange("p a n -> p (a n)"), start=(c == 0), stop=(c == DC - 1))
                    last.then_inc(gu_ready, 1)

                def turn_hidden(i, j):
                    t = R * i + j
                    pe.wait_ge(hidden_ready, t + 1)
                    wait(pe, hidden_copied, t - 1)
                    for c in range(2):
                        last = pe.transpose(ps[0:FH, 4 + j % 2, c * P:(c + 1) * P], hidden[:, j % 2, c * FH:(c + 1) * FH], k.ident[:])
                    last.then_inc(hidden_turned, 1)

                def down(i, j, ring):
                    t = R * i + j
                    pe.wait_ge(hidden_copied, t + 1)
                    wait(pe, result_ready, t - 1)
                    for c in range(2):
                        last = pe.matmul(ps[:, 6 + j % 2, 0:D], hidden_t[:, j % 2, c * P:(c + 1) * P],
                                         w_down[:, bass.ds(ring, 1), c, :].rearrange("p a n -> p (a n)"), start=(c == 0), stop=(c == 1))
                    last.then_inc(down_ready, 1)

                def buffer_of(i, j):
                    return pe.value_load(k.table[0:1, 1, bass.ds(R * i + j, 1)], min_val=0, max_val=WRING - 1)

                def step(i, j, first=False, last=False):
                    ring = buffer_of(i, j)
                    if not first:
                        before = (i, j - 1) if j else (i - 1, R - 1)
                        turn_hidden(*before)
                    if not last:
                        turn_rows(*((i, j + 1) if j < R - 1 else (i + 1, 0)))
                    gate_up(i, j, ring)
                    if not first:
                        down(*before, buffer_of(*before))

                turn_rows(0, 0)
                for j in range(R):
                    step(0, j, first=(j == 0))
                with pe.Fori(1, ROUNDS - 1) as i:
                    for j in range(R):
                        step(i, j)
                for j in range(R):
                    step(ROUNDS - 1, j, last=(j == R - 1))
                turn_hidden(ROUNDS - 1, R - 1)
                down(ROUNDS - 1, R - 1, buffer_of(ROUNDS - 1, R - 1))

            @block.scalar
            def _(act):
                def copy_rows(i, j):
                    t = R * i + j
                    act.wait_ge(rows_turned, t + 1)
                    wait(act, gu_ready, t - 1)
                    nc.scalar.copy(rows_t[:, j % 2], ps[:, j % 2, 0:DC * P]).then_inc(rows_copied, 1)

                def silu(i, j):
                    t = R * i + j
                    act.wait_ge(gu_ready, t + 1)
                    wait(act, hidden_ready, t - 1)
                    nc.scalar.activation(act_g[:, j % 2], ps[:, 2 + j % 2, 0:FF], ACT.Silu).then_inc(silu_ready, 1)

                def store(i, j):
                    t = R * i + j
                    act.wait_ge(result_ready, t + 1)
                    act.dma_start(k.outs[bass.ds(t, 1)].rearrange("t p d -> (t p) d"), result[:, j]).then_inc(out_done[j], 16)

                def step(i, j, first=0, last=False):
                    if not last:
                        copy_rows(*((i, j + 1) if j < R - 1 else (i + 1, 0)))
                    silu(i, j)
                    if first < 1:
                        store(*((i, j - 2) if j > 1 else (i - 1, R + j - 2)))

                copy_rows(0, 0)
                for j in range(R):
                    step(0, j, first=2 - j)
                with act.Fori(1, ROUNDS - 1) as i:
                    for j in range(R):
                        step(i, j)
                for j in range(R):
                    step(ROUNDS - 1, j, last=(j == R - 1))
                store(ROUNDS - 1, R - 2)
                store(ROUNDS - 1, R - 1)
                for j in range(R):
                    act.wait_ge(out_done[j], 16 * ROUNDS)

            @block.vector
            def _(dve):
                def gated(i, j):
                    t = R * i + j
                    dve.wait_ge(silu_ready, t + 1)
                    wait(dve, hidden_turned, t - 1)
                    nc.vector.tensor_tensor(hidden[:, j % 2], act_g[:, j % 2], ps[:, 2 + j % 2, FF:2 * FF], ALU.mult).then_inc(hidden_ready, 1)

                def copy_hidden(i, j):
                    t = R * i + j
                    dve.wait_ge(hidden_turned, t + 1)
                    wait(dve, down_ready, t - 1)
                    nc.vector.tensor_copy(hidden_t[:, j % 2], ps[0:FH, 4 + j % 2, 0:2 * P]).then_inc(hidden_copied, 1)

                def weigh(i, j):
                    t = R * i + j
                    expert = dve.value_load(k.table[0:1, 0, bass.ds(t, 1)], min_val=0, max_val=EXPERTS - 1)
                    dve.wait_ge(down_ready, t + 1)
                    if not isinstance(i, int) or i:
                        dve.wait_ge(out_done[j], 16 * i)
                    nc.vector.tensor_scalar(result[:, j], ps[:, 6 + j % 2, 0:D], rows[:, j, bass.ds(expert + D, 1)], None, ALU.mult).then_inc(result_ready, 1)

                def step(i, j, first=False):
                    before = (i, j - 1) if j else (i - 1, R - 1)
                    if not first:
                        copy_hidden(*before)
                    gated(i, j)
                    if not first:
                        weigh(*before)

                for j in range(R):
                    step(0, j, first=(j == 0))
                with dve.Fori(1, ROUNDS) as i:
                    for j in range(R):
                        step(i, j)
                copy_hidden(ROUNDS - 1, R - 1)
                weigh(ROUNDS - 1, R - 1)
        sweep(nc, used)


def combine(nc, k):
    with ExitStack() as ctx:
        sb = lambda n, shape, dt: ctx.enter_context(nc.sbuf_tensor(f"cb_{n}", shape, dt))
        used = []
        sem = phase_semaphores(nc, ctx, "cb", used)
        wq = sb("wq", [P, DC, DC, P], F32)
        idx = sb("idx", [P, 2, 2, TOP_K], I32)
        gathered = sb("gathered", [P, 2, 2, TOP_K, D], F32)
        moe = sb("moe", [P, 2, D], F32)
        eps = sb("eps", [P, 1], F32)
        stats = sb("stats", [P, 2, 6], F32)
        moments = sb("moments", [P, 2, 2], F32)
        deviation = sb("deviation", [P, 2], F32)
        rstd = sb("rstd", [P, 2], F32)
        newton = sb("newton", [P, 2], F32)
        xn = sb("xn", [P, 2, 2, D], F32)
        xn_t = sb("xn_t", [P, 2, DC, SEQ], F32)
        rest = sb("rest", [P, 2, DC * SEQ], F32)
        parts = sb("parts", [P, 2, 3, DC * SEQ], BF16)
        ps = ctx.enter_context(nc.psum_tensor("cb_ps", [P, 8, 512], F32))
        w_in, eps_set, staged = sem("w_in"), sem("eps_set"), sem("staged")
        rows_in = [sem("rows_in0"), sem("rows_in1")]
        own, summed, moments_ready, deviations = sem("own"), sem("summed"), sem("moments_ready"), sem("deviations")
        xn_ready, turned, copied, q_ready = sem("xn_ready"), sem("turned"), sem("copied"), sem("q_ready")
        high, rested, middle, split = sem("high"), sem("rested"), sem("middle"), sem("split")
        written = [sem("written0"), sem("written1")]
        PAIRS = BATCH // 2

        with nc.Block() as block:

            def batches(eng, step):
                for u in range(2):
                    step(0, u, True)
                with eng.Fori(1, PAIRS) as i:
                    for u in range(2):
                        step(i, u, False)

            @block.sync
            def _(sp):
                sp.dma_start(wq[:], k.dram["wq"]).then_inc(w_in, 16)

                def write(i, u, first):
                    b = 2 * i + u
                    sp.wait_ge(split, b + 1)
                    stack = k.q1_stack[bass.ds(b, 1)].rearrange("b t p n -> p (b t) n")
                    at = 0
                    for part, n in Q_PARTS:
                        sp.dma_start(stack[:, at:at + n, :],
                                     parts[:, u, part:part + 1, :].to_broadcast([P, n, DC * SEQ])).then_inc(written[u], 16)
                        at += n

                batches(sp, write)
                for u in range(2):
                    sp.wait_ge(written[u], 16 * len(Q_PARTS) * PAIRS)

            @block.gpsimd
            def _(pool):
                nc.gpsimd.memset(eps[:], EPS).then_inc(eps_set, 1)

                def gather(i, u, first):
                    b = 2 * i + u
                    if not first:
                        pass_on(pool, summed, 2 * b - 2, k.passed)
                    for j in range(2):
                        nc.gpsimd.tensor_copy(idx[:, u, j, :], k.slot[:, bass.ds(2 * b + j, 1), :].rearrange("p a s -> p (a s)")).then_inc(staged, 1)
                    pass_on(pool, staged, 2 * b + 2, k.passed)
                    for j in range(2):
                        for s in range(TOP_K):
                            nc.gpsimd.indirect_dma_start(gathered[:, u, j, s, :], None, k.outs.rearrange("t p d -> (t p) d"),
                                                         bass.IndirectOffsetOnAxis(ap=idx[:, u, j, s:s + 1], axis=0)).then_inc(rows_in[u], 16)

                batches(pool, gather)

            @block.vector
            def _(dve):
                def step(i, u, first):
                    b = 2 * i + u
                    dve.sem_clear(own)
                    for j in range(2):
                        if j == 0:
                            dve.wait_ge(rows_in[u], 16 * 2 * TOP_K * (i + 1))
                        nc.vector.tensor_reduce(moe[:, j, :], gathered[:, u, j].rearrange("p s d -> p d s"), AX.X, ALU.add).then_inc(summed, 1)
                    for j in range(2):
                        tile = k.x[:, bass.ds(2 * b + j, 1), :].rearrange("p a d -> p (a d)")
                        dve.wait_ge(summed, 2 * b + j + 1)
                        nc.vector.tensor_tensor(tile, tile, moe[:, j, :], ALU.add).then_inc(own, 1)
                    for j in range(2):
                        dve.wait_ge(own, 1 + j)
                        nc.vector.bn_stats(stats[:, j, :], k.x[:, bass.ds(2 * b + j, 1), :].rearrange("p a d -> p (a d)")).then_inc(own, 1)
                    for j in range(2):
                        dve.wait_ge(own, 3 + j)
                        nc.vector.bn_aggr(moments[:, j, :], stats[:, j, :]).then_inc(moments_ready, 1)
                    dve.wait_ge(deviations, b + 1)
                    nc.vector.reciprocal(rstd[:], deviation[:]).then_inc(own, 1)
                    dve.wait_ge(own, 5)
                    refine(nc, own, 5, rstd[:], moments[:, :, 1], newton[:])
                    if not first:
                        dve.wait_ge(turned, b - 1)
                    for j in range(2):
                        nc.vector.tensor_scalar(xn[:, u, j, :], k.x[:, bass.ds(2 * b + j, 1), :].rearrange("p a d -> p (a d)"),
                                                moments[:, j, 0:1], rstd[:, j:j + 1], ALU.subtract, ALU.mult).then_inc(xn_ready, 1)
                    dve.wait_ge(high, b + 1)
                    nc.vector.tensor_tensor(rest[:, u, :], ps[:, 2 + u, :], parts[:, u, 0, :], ALU.subtract).then_inc(rested, 1)
                    dve.wait_ge(middle, b + 1)
                    nc.vector.tensor_tensor(parts[:, u, 2, :], rest[:, u, :], parts[:, u, 1, :], ALU.subtract).then_inc(split, 1)

                batches(dve, step)

            @block.scalar
            def _(act):
                act.wait_ge(eps_set, 1)

                def step(i, u, first):
                    b = 2 * i + u
                    act.wait_ge(moments_ready, 2 * b + 2)
                    nc.scalar.activation(deviation[:], moments[:, :, 1], ACT.Sqrt, bias=eps[:, 0:1]).then_inc(deviations, 1)
                    act.wait_ge(turned, b + 1)
                    nc.scalar.copy(xn_t[:, u].rearrange("p c t -> p (c t)"), ps[:, u, :]).then_inc(copied, 1)
                    if not first:
                        act.wait_ge(written[u], 16 * len(Q_PARTS) * i)
                    act.wait_ge(q_ready, b + 1)
                    nc.scalar.copy(parts[:, u, 0, :], ps[:, 2 + u, :]).then_inc(high, 1)
                    act.wait_ge(rested, b + 1)
                    nc.scalar.copy(parts[:, u, 1, :], rest[:, u, :]).then_inc(middle, 1)

                batches(act, step)

            @block.tensor
            def _(pe):
                pe.wait_ge(w_in, 16)

                def step(i, u, first):
                    b = 2 * i + u
                    pe.wait_ge(xn_ready, 2 * b + 2)
                    for j in range(2):
                        for c in range(DC):
                            last = pe.transpose(ps[:, u, c * SEQ + j * P:c * SEQ + (j + 1) * P], xn[:, u, j, c * P:(c + 1) * P], k.ident[:])
                    last.then_inc(turned, 1)
                    pe.wait_ge(copied, b + 1)
                    if not first:
                        pe.wait_ge(rested, b - 1)
                    for m in range(DC):
                        for c in range(DC):
                            last = pe.matmul(ps[:, 2 + u, m * SEQ:(m + 1) * SEQ], wq[:, c, m, :], xn_t[:, u, c, :],
                                             start=(c == 0), stop=(c == DC - 1))
                    last.then_inc(q_ready, 1)

                batches(pe, step)
        sweep(nc, used)


def finish(nc, k):
    with ExitStack() as ctx:
        sb = lambda n, shape, dt: ctx.enter_context(nc.sbuf_tensor(f"ff_{n}", shape, dt))
        used = []
        sem = phase_semaphores(nc, ctx, "ff", used)
        wo = sb("wo", [P, DC, D], F32)
        router = sb("router", [P, DC, BLOCKS], F32)
        router_b = sb("router_b", [P, BLOCKS], F32)
        w1 = sb("w1", [P, DC, HID], F32)
        b1 = sb("b1", [P, FC], F32)
        w2 = sb("w2", [P, FC, D], F32)
        b2 = sb("b2", [P, D], F32)
        spread = sb("spread", [BLOCKS, FC, P], BF16)
        eps = sb("eps", [P, 1], F32)
        ao_t = sb("ao_t", [P, 2, DC * P], F32)
        stats = sb("stats", [P, TILES, 6], F32)
        moments = sb("moments", [P, TILES, 2], F32)
        deviation = sb("deviation", [P, TILES], F32)
        rstd = sb("rstd", [P, TILES], F32)
        newton = sb("newton", [P, TILES], F32)
        xn = sb("xn", [P, 2, D], F32)
        xn_t = sb("xn_t", [P, DC, TOK], F32)
        logits = sb("logits", [P, TILES, BLOCKS], F32)
        best = sb("best", [P, TILES, 8], F32)
        others = sb("others", [P, TILES, BLOCKS], F32)
        closed = sb("closed", [P, TILES, BLOCKS], F32)
        closed_t = sb("closed_t", [BLOCKS, TOK], BF16)
        hidden_t = sb("hidden_t", [P, 2, FC, 512], F32)
        y = sb("y", [P, 2, D], F32)
        ps = ctx.enter_context(nc.psum_tensor("ff_ps", [P, 8, 512], F32))
        logit_ps = ps[:, 6, 0:TILES * BLOCKS].rearrange("p (t e) -> p t e", e=BLOCKS)

        w_in, eps_set, own = sem("w_in"), sem("eps_set"), sem("own")
        a_turned, a_copied, a_ready, x_done = sem("a_turned"), sem("a_copied"), sem("a_ready"), sem("x_done")
        stats_done, moments_done, deviations = sem("stats_done"), sem("moments_done"), sem("deviations")
        xn_ready, turned, copied, logits_ready = sem("xn_ready"), sem("turned"), sem("copied"), sem("logits_ready")
        masks_ready, masks_turned, masks_copied = sem("masks_ready"), sem("masks_turned"), sem("masks_copied")
        x_biased = sem("x_biased")
        hid_ready, relu_done, y_ready, y_done = sem("hid_ready"), sem("relu_done"), sem("y_ready"), sem("y_done")
        out_done = [sem("out_done0"), sem("out_done1")]
        LOADS = 8
        FBLOCKS = TOK // 512
        FT = 512 // P

        with nc.Block() as block:

            @block.sync
            def _(sp):
                for tile, name in ((wo, "wo"), (router, "router"), (w1, "w1"), (b1, "b1"), (w2, "w2"), (spread, "c_spread")):
                    sp.dma_start(tile[:], k.dram[name]).then_inc(w_in, 16)
                sp.dma_start(router_b[:], k.dram["router_b"].to_broadcast([P, BLOCKS])).then_inc(w_in, 16)
                sp.dma_start(b2[:], k.dram["b2"].to_broadcast([P, D])).then_inc(w_in, 16)
                with sp.Fori(0, TILES // 2) as i:
                    for u in range(2):
                        t = 2 * i + u
                        sp.wait_ge(y_done, t + 1)
                        sp.dma_start(k.result[bass.ds(t, 1)].rearrange("t p d -> (t p) d"), y[:, u]).then_inc(out_done[u], 16)
                for u in range(2):
                    sp.wait_ge(out_done[u], 16 * (TILES // 2))

            @block.gpsimd
            def _(pool):
                nc.gpsimd.memset(eps[:], EPS).then_inc(eps_set, 1)
                pool.wait_ge(w_in, 16 * LOADS)
                with pool.Fori(0, TILES) as t:
                    pool.wait_ge(xn_ready, t + 1)
                    nc.gpsimd.tensor_tensor(k.x[:, bass.ds(t, 1), :].rearrange("p a d -> p (a d)"),
                                            k.x[:, bass.ds(t, 1), :].rearrange("p a d -> p (a d)"), b2[:], ALU.add).then_inc(x_biased, 1)

            @block.tensor
            def _(pe):
                pe.wait_ge(w_in, 16 * LOADS)

                for t in range(TILES):
                    u = t % 2
                    for c in range(DC):
                        last = pe.transpose(ps[:, u, c * P:(c + 1) * P], k.ao[:, t, c * P:(c + 1) * P], k.ident[:])
                    last.then_inc(a_turned, 1)
                    pe.wait_ge(a_copied, t + 1)
                    for c in range(DC):
                        last = pe.matmul(ps[:, 2 + u, 0:D], ao_t[:, u, c * P:(c + 1) * P], wo[:, c, :], start=(c == 0), stop=(c == DC - 1))
                    last.then_inc(a_ready, 1)

                for t in range(TILES):
                    u = t % 2
                    pe.wait_ge(xn_ready, t + 1)
                    for c in range(DC):
                        last = pe.transpose(ps[:, u, c * P:(c + 1) * P], xn[:, u, c * P:(c + 1) * P], k.ident[:])
                    last.then_inc(turned, 1)
                    pe.wait_ge(copied, t + 1)
                    for c in range(DC):
                        last = pe.matmul(logit_ps[:, t, :], xn_t[:, c, t * P:(t + 1) * P], router[:, c, :], start=(c == 0), stop=(c == DC - 1))
                    last.then_inc(logits_ready, 1)

                pe.wait_ge(masks_ready, TILES)
                for f in range(FBLOCKS):
                    if f:
                        pe.wait_ge(masks_copied, f)
                    for j in range(FT):
                        last = pe.transpose(ps[0:BLOCKS, 7, j * P:(j + 1) * P], closed[:, FT * f + j, :], k.ident[:])
                    last.then_inc(masks_turned, 1)
                pe.wait_ge(masks_copied, FBLOCKS)

                def hidden(f, u):
                    for m in range(FC):
                        wait(pe, relu_done, FC * f + m - 3)
                        bank = ps[:, 2 + m % 4, :]
                        for c in range(DC):
                            pe.matmul(bank, w1[:, c, m * P:(m + 1) * P], xn_t[:, c, bass.ds(f * 512, 512)], start=(c == 0), stop=False)
                        pe.matmul(bank, spread[:, m, :], closed_t[:, bass.ds(f * 512, 512)], start=False, stop=True).then_inc(hid_ready, 1)

                def output(f, u):
                    for j in range(FT):
                        wait(pe, y_done, FT * f + j - 1)
                        for m in range(FC):
                            if j == 0:
                                pe.wait_ge(relu_done, FC * f + m + 1)
                            last = pe.matmul(ps[:, j % 2, 0:D], hidden_t[:, u, m, j * P:(j + 1) * P], w2[:, m, :],
                                             start=(m == 0), stop=(m == FC - 1))
                        last.then_inc(y_ready, 1)

                hidden(0, 0)
                for f in range(FBLOCKS):
                    if f + 1 < FBLOCKS:
                        hidden(f + 1, (f + 1) % 2)
                    output(f, f % 2)

            @block.scalar
            def _(act):
                def copy_a(i, u, first):
                    t = 2 * i + u
                    act.wait_ge(a_turned, t + 1)
                    if not first:
                        act.wait_ge(x_done, t - 1)
                    nc.scalar.copy(ao_t[:, u], ps[:, u, 0:DC * P]).then_inc(a_copied, 1)

                for u in range(2):
                    copy_a(0, u, True)
                with act.Fori(1, TILES // 2) as i:
                    for u in range(2):
                        copy_a(i, u, False)
                act.wait_ge(eps_set, 1)
                act.wait_ge(moments_done, TILES)
                nc.scalar.activation(deviation[:], moments[:, :, 1], ACT.Sqrt, bias=eps[:, 0:1]).then_inc(deviations, 1)
                with act.Fori(0, TILES // 2) as i:
                    for u in range(2):
                        t = 2 * i + u
                        act.wait_ge(turned, t + 1)
                        nc.scalar.copy(xn_t[:, :, bass.ds(t * P, P)], ps[:, u, 0:DC * P].rearrange("p (c n) -> p c n", c=DC)).then_inc(copied, 1)
                for f in range(FBLOCKS):
                    act.wait_ge(masks_turned, f + 1)
                    nc.scalar.copy(closed_t[:, f * 512:(f + 1) * 512], ps[0:BLOCKS, 7, :]).then_inc(masks_copied, 1)
                for f in range(FBLOCKS):
                    for m in range(FC):
                        act.wait_ge(hid_ready, FC * f + m + 1)
                        if f > 1 and m == 0:
                            act.wait_ge(y_ready, FT * (f - 1))
                        nc.scalar.activation(hidden_t[:, f % 2, m, :], ps[:, 2 + m % 4, :], ACT.Relu, bias=b1[:, m:m + 1]).then_inc(relu_done, 1)

            @block.vector
            def _(dve):
                steps = [0]

                def then(ins):
                    ins.then_inc(own, 1)
                    steps[0] += 1
                    dve.wait_ge(own, steps[0])

                with dve.Fori(0, TILES // 2) as i:
                    for u in range(2):
                        t = 2 * i + u
                        tile = k.x[:, bass.ds(t, 1), :].rearrange("p a d -> p (a d)")
                        dve.wait_ge(a_ready, t + 1)
                        nc.vector.tensor_tensor(tile, tile, ps[:, 2 + u, 0:D], ALU.add).then_inc(x_done, 1)
                        dve.wait_ge(x_done, t + 1)
                        nc.vector.bn_stats(stats[:, bass.ds(t, 1), :].rearrange("p a s -> p (a s)"), tile).then_inc(stats_done, 1)
                dve.wait_ge(stats_done, TILES)
                for t in range(TILES):
                    nc.vector.bn_aggr(moments[:, t, :], stats[:, t, :]).then_inc(moments_done, 1)
                dve.wait_ge(deviations, 1)
                then(nc.vector.reciprocal(rstd[:], deviation[:]))
                refine(nc, own, steps[0], rstd[:], moments[:, :, 1], newton[:])
                steps[0] += NEWTON_STEPS

                def normalise(t, u):
                    nc.vector.tensor_scalar(xn[:, u], k.x[:, bass.ds(t, 1), :].rearrange("p a d -> p (a d)"),
                                            moments[:, bass.ds(t, 1), 0:1].rearrange("p a s -> p (a s)"), rstd[:, bass.ds(t, 1)],
                                            ALU.subtract, ALU.mult).then_inc(xn_ready, 1)

                normalise(0, 0)
                normalise(1, 1)
                with dve.Fori(1, TILES // 2) as i:
                    for u in range(2):
                        dve.wait_ge(turned, 2 * i + u - 1)
                        normalise(2 * i + u, u)

                dve.wait_ge(logits_ready, TILES)
                dve.wait_ge(w_in, 16 * LOADS)
                then(nc.vector.tensor_tensor(logits[:], logit_ps, router_b[:].unsqueeze(1).to_broadcast([P, TILES, BLOCKS]), ALU.add))
                for t in range(TILES):
                    last = nc.vector.max(best[:, t, :], logits[:, t, :])
                then(last)
                then(nc.vector.memset(best[:, :, TOP_B:8], 3.0e38))
                for t in range(TILES):
                    last = nc.vector.match_replace(others[:, t, :], best[:, t, :], logits[:, t, :], -3.0e38)
                then(last)
                then(nc.vector.tensor_tensor(closed[:], others[:], logits[:], ALU.is_equal))
                nc.vector.tensor_scalar(closed[:], closed[:], MASKED, None, ALU.mult).then_inc(masks_ready, TILES)

                dve.wait_ge(x_biased, TILES)
                for t in range(TILES):
                    u = t % 2
                    dve.wait_ge(y_ready, t + 1)
                    if t > 1:
                        dve.wait_ge(out_done[u], 16 * (t // 2))
                    nc.vector.tensor_tensor(y[:, u], k.x[:, t, :], ps[:, u, 0:D], ALU.add).then_inc(y_done, 1)


def build(nc, dram, out):
    k = Kernel()
    k.dram, k.result = dram, out
    scratch = lambda name, shape, dt: nc.dram_tensor(name, shape, dt, kind="Internal").ap()
    stack = (BATCH, TERMS, P, DC * SEQ)
    k.q0_stack, k.k0_stack = scratch("q0_stack", stack, BF16), scratch("k0_stack", stack, BF16)
    k.q1_stack, k.k1_stack = scratch("q1_stack", stack, BF16), scratch("k1_stack", stack, BF16)
    k.v1 = scratch("v1_rows", (BATCH, 2, P, D), F32)
    k.xn = scratch("moe_rows", (TILES, P, D + EXPERTS), F32)
    k.lists = scratch("expert_lists", (EXPERTS * TOK, 1), I32)
    k.outs = scratch("expert_outs", (ETILES, P, D), F32)
    with ExitStack() as ctx:
        sb = lambda n, shape, dt: ctx.enter_context(nc.sbuf_tensor(n, shape, dt))
        k.x = sb("x", [P, TILES, D], F32)
        k.ao = sb("attention_out", [P, TILES, D], F32)
        k.slot = sb("slot", [P, TILES, TOP_K], I32)
        k.table = sb("tile_table", [1, 3, ETABLE], I32)
        k.ids = sb("slot_tokens", [P, ETABLE], I32)
        k.passed = ctx.enter_context(nc.semaphore("passed"))
        constants(nc, k, ctx)
        prepare(nc, k)
        attention(nc, k, "a0", k.q0_stack, k.k0_stack, dram["ctx"], 1.0 / float(np.sqrt(np.float32(D))), False, k.ao)
        route(nc, k)
        experts(nc, k)
        combine(nc, k)
        attention(nc, k, "a1", k.q1_stack, k.k1_stack, k.v1, 1.0 / float(np.sqrt(np.float32(DH))), True, k.ao)
        finish(nc, k)


def _layouts(inputs):
    a = {n: np.ascontiguousarray(v) for n, v in inputs.items()}
    heads = lambda w: w.reshape(DC, HEADS // DC, DH, -1).transpose(0, 2, 1, 3)
    c = a["ctx_1024"]
    out = {
        "x": a["x"].reshape(TILES, P, D),
        "ctx": c.reshape(BATCH, 2, P, D),
        "ctx_t": c.reshape(BATCH, SEQ, DC, HEADS // DC, DH).transpose(0, 4, 3, 2, 1).reshape(BATCH, P, DC, SEQ),
    }
    wk = heads(a["L1_xattn_Wk"]).reshape(DC, P, D)
    wk = heads(wk.transpose(2, 0, 1).reshape(D, D)).reshape(DC, P, DC, P)
    out["wk"] = wk.transpose(1, 0, 2, 3)
    out["wv"] = heads(a["L1_xattn_Wv"].T).reshape(DC, P, D).transpose(1, 0, 2)
    wq = heads(a["L1_xattn_Wq"]).reshape(DC, P, DC, P)
    out["wq"] = wq.transpose(3, 2, 0, 1)
    rows = lambda w: w.T.reshape(DC, P, -1).transpose(1, 0, 2)
    out["wo"] = rows(a["L1_xattn_Wo"])
    out["gate"] = rows(a["L0_ffn_gate_w"])
    out["router"] = rows(a["L1_ffn_router_w"])
    out["router_b"] = a["L1_ffn_router_b"].reshape(1, BLOCKS)
    out["w1"] = rows(a["L1_ffn_w1"])
    out["b1"] = a["L1_ffn_b1"].reshape(FC, P).T
    out["w2"] = a["L1_ffn_w2"].T.reshape(FC, P, D).transpose(1, 0, 2)
    out["b2"] = a["L1_ffn_b2"].reshape(1, D)
    gu = np.stack([a["L0_ffn_w_gate"], a["L0_ffn_w_up"]], 1).reshape(EXPERTS, 2 * FF, DC, P)
    out["w_gu"] = gu.transpose(0, 3, 2, 1)
    out["w_down"] = a["L0_ffn_w_down"].reshape(EXPERTS, D, 2, FH).transpose(0, 3, 2, 1)
    bf16 = mybir.dt.np(BF16)
    p = np.arange(P)
    out["c_ident"] = np.eye(P, dtype=np.float32)
    out["c_ident_b"] = np.eye(P, dtype=np.float32).astype(bf16)
    late = np.where(p[None, :] > p[:, None], np.float32(MASKED), np.float32(0))
    out["c_mask_qk"] = late.astype(bf16)
    out["c_mask_kq"] = late.T.astype(bf16)
    out["c_before"] = (p[:, None] < p[None, :]).astype(bf16)
    out["c_ones"] = np.ones((P, P), bf16)
    out["c_list_end"] = np.broadcast_to(EXPERTS * TOK - TOK * np.arange(EXPERTS, dtype=np.float32), (P, EXPERTS))
    out["c_token"] = (P * np.arange(TILES)[None, :] + p[:, None]).astype(np.int32)
    out["c_tile"] = (P * np.arange(2)[None, :] + p[:, None]).astype(np.float32)
    spread = (np.arange(HID) // (HID // BLOCKS))[None, :] == np.arange(BLOCKS)[:, None]
    out["c_spread"] = spread.reshape(BLOCKS, FC, P).astype(bf16)
    return {n: np.ascontiguousarray(v) for n, v in out.items()}


def kernel(**inputs):
    import numpy as _np
    import concourse.bacc as _bacc
    from concourse import mybir as _mybir
    from concourse.bass_utils import run_bass_kernel_spmd as _run

    nc = _bacc.Bacc("TRN2", target_bir_lowering=False, num_devices=1)
    arrays, dram = {}, {}
    for name, a in _layouts(inputs).items():
        arrays[f"in_{name}_dram"] = a
        dram[name] = nc.dram_tensor(f"in_{name}_dram", a.shape, _mybir.dt.from_np(a.dtype), kind="ExternalInput").ap()
    out = nc.dram_tensor("out_0_dram", (TILES, P, D), _mybir.dt.float32, kind="ExternalOutput").ap()
    build(nc, dram, out)
    r = _run(nc, [arrays], core_ids=[0])
    return _np.asarray(r.results[0]["out_0_dram"]).reshape(BATCH, SEQ, D)
```

```python
from contextlib import ExitStack, nullcontext

import numpy as np

import concourse.bass as bass
from concourse import mybir

F32 = mybir.dt.float32
BF16 = mybir.dt.bfloat16
I32 = mybir.dt.int32
ALU = mybir.AluOpType
ACT = mybir.ActivationFunctionType
AX = mybir.AxisListType

P = 128
BATCH, SEQ, D = 8, 256, 256
PAIRS = BATCH // 2
TOK = BATCH * SEQ
TILES = TOK // P
DC = D // P
HEADS, DH = 16, 16
HSTEP = HEADS // 2
STEPS = 2 * BATCH
TERMS = 6
ROWS = TERMS * DH
MROWS = 2
VW = 32
EPS = 1e-5
MASKED = -1e30

EXPERTS, TOP_K, FF = 64, 8, 192
FH = FF // 2
ETILES = -(-((TOK * TOP_K + EXPERTS * (P - 1)) // P) // 8) * 8
EXPECTED = TOK * TOP_K // P + EXPERTS // 2
ETABLE = 256
ROUNDS = STEPS // 4 + 1
REST = [(ROUNDS, u) for u in range(3)]
SYNC_LEFT = (6, 7)
LISTS = EXPERTS * TILES
WRING = 4

BLOCKS, TOP_B, HID = 16, 4, 1024
FC = HID // P

K_PARTS = [(0, 3), (0, 2), (0, 1)]
Q_PARTS = [(0, 3), (1, 2), (2, 1)]


def wait(eng, sem, count):
    if not (isinstance(count, int) and count <= 0):
        eng.wait_ge(sem, count)


def phase_semaphores(nc, ctx, prefix, used):
    def make(name):
        used.append(ctx.enter_context(nc.semaphore(f"{prefix}_{name}")))
        return used[-1]
    return make


def sweep(nc, used):
    with nc.Block() as block:

        @block.sync
        def _(sp):
            for sem in used:
                sp.sem_clear(sem)


NEWTON_STEPS = 3


def refine(nc, own, n, rstd, variance, scratch):
    nc.vector.scalar_tensor_tensor(scratch, rstd, -0.5, rstd, ALU.mult, ALU.mult).then_inc(own, 1)
    nc.vector.wait_ge(own, n + 1)
    nc.vector.scalar_tensor_tensor(scratch, variance, EPS, scratch, ALU.add, ALU.mult).then_inc(own, 1)
    nc.vector.wait_ge(own, n + 2)
    nc.vector.scalar_tensor_tensor(rstd, scratch, 1.5, rstd, ALU.add, ALU.mult).then_inc(own, 1)


def inverse_root(nc, own, n, rstd, variance, scratch, part):
    if part == 0:
        nc.vector.tensor_scalar(scratch, variance, EPS, None, ALU.add).then_inc(own, 1)
        nc.vector.wait_ge(own, n + 1)
        nc.vector.tensor_scalar(rstd, scratch.bitcast(I32), 1, None, ALU.logical_shift_right).then_inc(own, 1)
        nc.vector.wait_ge(own, n + 2)
        nc.vector.tensor_scalar(rstd, rstd, -1.0, float(0x5F3759DF), ALU.mult, ALU.add).then_inc(own, 1)
    else:
        nc.vector.wait_ge(own, n + NEWTON_STEPS * part)
        refine(nc, own, n + NEWTON_STEPS * part, rstd.bitcast(F32), variance, scratch)


class Kernel:
    pass


def constants(nc, k, ctx):
    sb = lambda name, shape, dt: ctx.enter_context(nc.sbuf_tensor(name, shape, dt))
    k.ident = sb("ident", [P, P], F32)
    k.ident_b = sb("ident_b", [P, P], BF16)
    k.mask_qk = sb("mask_qk", [P, P], BF16)
    k.mask_kq = sb("mask_kq", [P, P], BF16)
    loaded = ctx.enter_context(nc.semaphore("constants_loaded"))
    with nc.Block() as block:

        @block.sync
        def _(sp):
            pairs = [(k.ident, "c_ident"), (k.ident_b, "c_ident_b"), (k.mask_qk, "c_mask_qk"), (k.mask_kq, "c_mask_kq")]
            for tile, name in pairs:
                sp.dma_start(tile[:], k.dram[name]).then_inc(loaded, 16)
            sp.wait_ge(loaded, 16 * len(pairs))


def prepare(nc, k):
    with ExitStack() as ctx:
        sb = lambda name, shape, dt: ctx.enter_context(nc.sbuf_tensor(name, shape, dt))
        used = []
        sem = phase_semaphores(nc, ctx, "prep", used)
        ctx_t = sb("ctx_t", [P, 2, DC, SEQ], F32)
        wk = sb("wk", [P, DC, DC, P], F32)
        wv = sb("wv", [P, DC, D], F32)
        stats = sb("ln0_stats", [P, 2, 6], F32)
        moments = sb("ln0_moments", [P, 2, 2], F32)
        deviation = sb("ln0_deviation", [P, 2], F32)
        rstd = sb("ln0_rstd", [P, 2], F32)
        newton = sb("ln0_newton", [P, 2], F32)
        eps = sb("ln0_eps", [P, 1], F32)
        xn = sb("ln0_out", [P, 2, 2, D], F32)
        rest = sb("split_rest", [P, 2, 3, DC * SEQ], F32)
        parts = sb("split_parts", [P, 2, 3, 3, DC * SEQ], BF16)
        v1 = sb("v1", [P, 2, 2, D], F32)
        ps = ctx.enter_context(nc.psum_tensor("ps_prep", [P, 8, 512], F32))
        w_in = sem("w_in")
        x_in = [sem("x_in0"), sem("x_in1")]
        c_in = [sem("ctx_in0"), sem("ctx_in1")]
        own = sem("own")
        eps_set = sem("eps_set")
        moments_ready = sem("moments")
        deviations = sem("deviations")
        xn_ready = sem("xn_ready")
        q_turned = sem("q_turned")
        k1_ready = sem("k1_ready")
        v1_ready = sem("v1_ready")
        high = sem("high")
        rested = sem("rested")
        middle = sem("middle")
        split = sem("split")
        v1_out = sem("v1_out")
        written = [sem("written0"), sem("written1")]
        WRITES = 10
        K0, Q0, K1 = 0, 1, 2
        stacks = {K0: k.k0_stack, Q0: k.q0_stack, K1: k.k1_stack}

        def source(kind, u):
            if kind == K0:
                return ctx_t[:, u].rearrange("p c t -> p (c t)")
            return ps[:, (0 if kind == Q0 else 2) + u, :]

        with nc.Block() as block:

            @block.sync
            def _(sp):
                sp.dma_start(wk[:], k.dram["wk"]).then_inc(w_in, 16)
                sp.dma_start(wv[:], k.dram["wv"]).then_inc(w_in, 16)

                def load(b, u):
                    sp.dma_start(k.x[:, bass.ds(2 * b, 2), :],
                                 k.dram["x"][bass.ds(2 * b, 2)].rearrange("t p d -> p t d")).then_inc(x_in[u], 16)
                    sp.dma_start(ctx_t[:, u], k.dram["ctx_t"][bass.ds(b, 1)].rearrange("b p c t -> (b p) c t")).then_inc(c_in[u], 16)

                def write(b, u):
                    for kind in (K0, Q0, K1):
                        sp.wait_ge(split, 3 * b + kind + 1)
                        stack = stacks[kind][bass.ds(b, 1)].rearrange("b t p n -> p (b t) n")
                        t = 0
                        for first, n in (Q_PARTS if kind == Q0 else K_PARTS):
                            if kind == Q0:
                                src = parts[:, u, kind, first:first + 1, :].to_broadcast([P, n, DC * SEQ])
                            else:
                                src = parts[:, u, kind, first:first + n, :]
                            sp.dma_start(stack[:, t:t + n, :], src).then_inc(written[u], 16)
                            t += n
                    sp.wait_ge(v1_out, b + 1)
                    sp.dma_start(k.v1[bass.ds(b, 1)].rearrange("b t p d -> p (b t) d"), v1[:, u]).then_inc(written[u], 16)

                load(0, 0)
                load(1, 1)
                with sp.Fori(0, BATCH // 2 - 1) as i:
                    for u in range(2):
                        write(2 * i + u, u)
                        load(2 * i + u + 2, u)
                for u in range(2):
                    write(BATCH - 2 + u, u)
                for u in range(2):
                    sp.wait_ge(written[u], 16 * WRITES * (BATCH // 2))

            @block.vector
            def _(dve):
                with dve.Fori(0, BATCH // 2) as i:
                    for u in range(2):
                        b = 2 * i + u
                        dve.sem_clear(own)
                        dve.wait_ge(x_in[u], 16 * i + 16)
                        for j in range(2):
                            nc.vector.bn_stats(stats[:, j, :], k.x[:, bass.ds(2 * b + j, 1), :].rearrange("p a d -> p (a d)")).then_inc(own, 1)
                        for j in range(2):
                            dve.wait_ge(own, 1 + j)
                            nc.vector.bn_aggr(moments[:, j, :], stats[:, j, :]).then_inc(moments_ready, 1)
                        dve.wait_ge(deviations, b + 1)
                        nc.vector.reciprocal(rstd[:], deviation[:]).then_inc(own, 1)
                        dve.wait_ge(own, 3)
                        refine(nc, own, 3, rstd[:], moments[:, :, 1], newton[:])
                        dve.wait_ge(own, 3 + NEWTON_STEPS)
                        for j in range(2):
                            nc.vector.tensor_scalar(xn[:, u, j, :].rearrange("p (c d h) -> p c h d", c=DC, d=DH),
                                                    k.x[:, bass.ds(2 * b + j, 1), :].rearrange("p a (c h d) -> p (a c) h d", c=DC, d=DH),
                                                    moments[:, j, 0:1], rstd[:, j:j + 1], ALU.subtract, ALU.mult).then_inc(xn_ready, 1)
                        for kind in (K0, Q0, K1):
                            dve.wait_ge(high, 3 * b + kind + 1)
                            nc.vector.tensor_tensor(rest[:, u, kind, :], source(kind, u), parts[:, u, kind, 0, :],
                                                    ALU.subtract).then_inc(rested, 1)

            @block.scalar
            def _(act):
                def take_middle(b, u, kind):
                    act.wait_ge(rested, 3 * b + kind + 1)
                    nc.scalar.copy(parts[:, u, kind, 1, :], rest[:, u, kind, :]).then_inc(middle, 1)

                def batch(i, u, first):
                    b = 2 * i + u
                    act.wait_ge(moments_ready, 2 * b + 2)
                    nc.scalar.activation(deviation[:], moments[:, :, 1], ACT.Sqrt, bias=eps[:, 0:1]).then_inc(deviations, 1)
                    if not first:
                        act.wait_ge(written[u], 16 * WRITES * i)
                    act.wait_ge(c_in[u], 16 * i + 16)
                    nc.scalar.copy(parts[:, u, K0, 0, :], source(K0, u)).then_inc(high, 1)
                    act.wait_ge(q_turned, b + 1)
                    nc.scalar.copy(parts[:, u, Q0, 0, :], source(Q0, u)).then_inc(high, 1)
                    take_middle(b, u, K0)
                    act.wait_ge(k1_ready, b + 1)
                    nc.scalar.copy(parts[:, u, K1, 0, :], source(K1, u)).then_inc(high, 1)
                    take_middle(b, u, Q0)
                    act.wait_ge(v1_ready, b + 1)
                    nc.scalar.copy(v1[:, u].rearrange("p t d -> p (t d)"), ps[:, 4 + u, :]).then_inc(v1_out, 1)
                    take_middle(b, u, K1)

                act.wait_ge(eps_set, 1)
                batch(0, 0, True)
                batch(0, 1, True)
                with act.Fori(1, BATCH // 2) as i:
                    for u in range(2):
                        batch(i, u, False)

            @block.gpsimd
            def _(pool):
                nc.gpsimd.memset(eps[:], EPS).then_inc(eps_set, 1)

                def low(b, u, kind):
                    pool.wait_ge(middle, 3 * b + kind + 1)
                    nc.gpsimd.tensor_tensor(parts[:, u, kind, 2, :], rest[:, u, kind, :], parts[:, u, kind, 1, :],
                                            ALU.subtract).then_inc(split, 1)

                with pool.Fori(0, BATCH // 2) as i:
                    for u in range(2):
                        for kind in (K0, Q0, K1):
                            low(2 * i + u, u, kind)

            @block.tensor
            def _(pe):
                pe.wait_ge(w_in, 32)

                def batch(i, u, first):
                    b = 2 * i + u
                    pe.wait_ge(xn_ready, 2 * b + 2)
                    if not first:
                        pe.wait_ge(rested, 3 * b - 3)
                        pe.wait_ge(v1_out, b - 1)
                    for j in range(2):
                        for c in range(DC):
                            last = pe.transpose(ps[:, u, c * SEQ + j * P:c * SEQ + (j + 1) * P],
                                                xn[:, u, j, c * P:(c + 1) * P], k.ident[:])
                    last.then_inc(q_turned, 1)
                    pe.wait_ge(c_in[u], 16 * i + 16)
                    for m in range(DC):
                        for c in range(DC):
                            last = pe.matmul(ps[:, 2 + u, m * SEQ:(m + 1) * SEQ], wk[:, c, m, :], ctx_t[:, u, c, :],
                                             start=(c == 0), stop=(c == DC - 1))
                    last.then_inc(k1_ready, 1)
                    for j in range(2):
                        for c in range(DC):
                            last = pe.matmul(ps[:, 4 + u, j * D:(j + 1) * D], ctx_t[:, u, c, j * P:(j + 1) * P], wv[:, c, :],
                                             start=(c == 0), stop=(c == DC - 1))
                    last.then_inc(v1_ready, 1)

                batch(0, 0, True)
                batch(0, 1, True)
                with pe.Fori(1, BATCH // 2) as i:
                    for u in range(2):
                        batch(i, u, False)
        sweep(nc, used)


def attention(nc, k, name, q_stack, k_stack, values, scale, causal, out, side):
    blocks = 3 if causal else 4
    cols = blocks * P
    LAG = 2
    with ExitStack() as ctx:
        sb = lambda n, shape, dt: ctx.enter_context(nc.sbuf_tensor(f"{name}_{n}", shape, dt))
        used = []
        sem = phase_semaphores(nc, ctx, name, used)
        kst = sb("kst", [ROWS + MROWS, 4, HSTEP, SEQ], BF16)
        qst = sb("qst", [ROWS + MROWS, 4, HSTEP, SEQ], BF16)
        v_raw = sb("v_raw", [P, 2, 2, D], F32)
        v_aug = sb("v_aug", [P, 2, 2, HEADS, VW], F32)
        probs = sb("probs", [P, HSTEP, 4 * P], F32)
        blockmax = sb("blockmax", [P, 2, HSTEP, 3], F32)
        negmax = sb("negmax", [P, 2, 2, HSTEP], F32)
        maxparts = sb("maxparts", [P, 2, 2, 2, HSTEP], BF16)
        maxrows = sb("maxrows", [2 * HSTEP, 2, SEQ], BF16)
        turned_in = sb("turned_in", [P, 2, SEQ], F32)
        recip = sb("recip", [P, 2, HSTEP], F32)
        ps = ctx.enter_context(nc.psum_tensor(f"{name}_ps", [P, 8, 512], F32))
        QK_BANKS = (0, 1, 5)
        outs_dq = ps[:, 6, 0:SEQ]
        max_t = ps[0:2 * HSTEP, 6, SEQ:SEQ + P].bitcast(BF16)
        outs_qd = ps[:, 7, :].rearrange("p (j n) -> p j n", j=2)

        stack_in = [sem(f"stack_in{j}") for j in range(4)]
        v_in = [sem("v_in0"), sem("v_in1")]
        max_in = [sem(f"max_in{j}") for j in range(4)]
        ones_set = sem("ones_set")
        v_ready = sem("v_ready")
        own = sem("own")
        cut_step = sem("cut_step")
        recips = sem("recips")
        s_ready = sem("s_ready")
        s_free = sem("s_free")
        max_ready = sem("max_ready")
        max_turned = sem("max_turned")
        max_copied = sem("max_copied")
        t_ready = sem("t_ready")
        exped = sem("exped")
        pv_done = sem("pv_done")
        out_copied = sem("out_copied")
        out_turned = sem("out_turned")
        divided = sem("divided")

        LOOPED = STEPS // 4 - side.lead

        def emit(eng, step, last=LOOPED):
            for i in range(1 + side.lag):
                for u in range(4):
                    step((i, u))
            with eng.Fori(1 + side.lag, last) as i:
                for u in range(4):
                    step((i, u))
            for i in range(last, STEPS // 4 + 1):
                for u in range(4):
                    step((i, u))

        def after(st, n):
            i, u = st
            return i + (u + n) // 4, (u + n) % 4

        def number(st):
            return 4 * st[0] + st[1]

        def batch_of(st):
            return 2 * st[0] + st[1] // 2

        side.open(nc, k, ctx, sem, ps[:, 4, :])

        def scores(st):
            return not isinstance(st[0], int) or 0 <= number(st) < STEPS

        with nc.Block() as block:

            @block.sync
            def _(sp):
                half = HSTEP * SEQ

                def load(st):
                    i, u = st
                    b, part = batch_of(st), u % 2
                    if part == 0:
                        side.before_load(sp, i, u // 2)
                    for stack, tile in ((q_stack, qst), (k_stack, kst)):
                        rows = stack[bass.ds(b, 1)].rearrange("b t (d h) n -> (b t d) (h n)", d=DH)
                        sp.dma_start(tile[0:ROWS, u].rearrange("p s n -> p (s n)"),
                                     rows[:, part * half:(part + 1) * half]).then_inc(stack_in[u], 16)
                    if part == 0:
                        wait(sp, v_ready, b - 1)
                        sp.dma_start(v_raw[:, u // 2], values[bass.ds(b, 1)].rearrange("b t p d -> p (b t) d")).then_inc(v_in[u // 2], 16)

                def step(st):
                    if scores(after(st, 1)):
                        wait(sp, t_ready, HSTEP * (number(st) - LAG))
                        load(after(st, 1))
                    before = after(st, -1)
                    if scores(before):
                        sp.wait_ge(max_copied, number(before) + 1)
                        v = before[1]
                        for part in range(MROWS):
                            sp.dma_start(qst[ROWS + part:ROWS + part + 1, v],
                                         maxrows[part * HSTEP:(part + 1) * HSTEP, v % 2, :]).then_inc(max_in[v], 16)
                    side.sync(sp, st)

                side.sync_first(sp)
                load((0, 0))
                emit(sp, step, last=STEPS // 4 - 1)
                side.sync_last(sp)

            @block.gpsimd
            def _(pool):
                side.gpsimd(pool)

            @block.tensor
            def _(pe):
                def scores_qk(st, s):
                    i, u = st
                    h = number(st)
                    if s == 0:
                        pe.wait_ge(stack_in[u], 32 * i + 32)
                    wait(pe, s_free, HSTEP * h + (s - 2 if s > 2 else (-1, 0, -2)[s]))
                    bank = ps[:, QK_BANKS[s % 3], :]
                    for j in range(2):
                        keys = SEQ if not causal or j else P
                        at = j * (P if causal else SEQ)
                        last = pe.matmul(bank[:, at:at + keys], qst[0:ROWS, u, s, j * P:(j + 1) * P], kst[0:ROWS, u, s, 0:keys],
                                         start=True, stop=True)
                        if causal:
                            last = pe.matmul(bank[:, 2 * j * P:(2 * j + 1) * P], k.ident_b[:], k.mask_qk[:], start=False, stop=True,
                                             skip_group_check=True)
                    last.then_inc(s_ready, 1)

                def scores_kq(st, s):
                    i, u = st
                    h = number(st)
                    if s == 0:
                        pe.wait_ge(max_in[u], 32 * i + 32)
                    wait(pe, exped, HSTEP * h + s - 1)
                    bank = ps[:, 2 + s % 2, :]
                    for j in range(2):
                        first = P if causal and j else 0
                        at = j * SEQ
                        last = pe.matmul(bank[:, at:at + SEQ - first], kst[:, u, s, j * P:(j + 1) * P], qst[:, u, s, first:SEQ],
                                         start=True, stop=True)
                        if causal:
                            last = pe.matmul(bank[:, at:at + P], k.ident_b[:], k.mask_kq[:], start=False, stop=True,
                                             skip_group_check=True)
                    last.then_inc(t_ready, 1)

                def outputs(st, g):
                    i, u = st
                    h = number(st)
                    pe.wait_ge(exped, HSTEP * h + 4 * g + 4)
                    wait(pe, out_copied, 2 * h + g)
                    b_par = u // 2
                    if g == 0:
                        pe.wait_ge(max_copied, min(h + LAG, STEPS) if isinstance(h, int) else h + LAG)
                    if g == 0 and u % 2 == 0:
                        pe.wait_ge(v_ready, batch_of(st) + 1)
                    for j in range(2):
                        first = P if causal and j else 0
                        for r in range(4):
                            s = HSTEP * (u % 2) + 4 * g + r
                            last = pe.matmul(outs_dq[VW * r:VW * (r + 1), first:SEQ], v_aug[:, b_par, j, s, :],
                                             probs[:, 4 * g + r, j * SEQ:j * SEQ + SEQ - first],
                                             start=(j == 0), stop=(j == 1), skip_group_check=True)
                    last.then_inc(pv_done, 1)

                def turn_outputs(st, g):
                    h = number(st)
                    pe.wait_ge(out_copied, 2 * h + g + 1)
                    if g == 0:
                        wait(pe, divided, h)
                    for j in range(2):
                        last = pe.transpose(outs_qd[:, j, g * P:(g + 1) * P], turned_in[:, g, j * P:(j + 1) * P], k.ident[:])
                    last.then_inc(out_turned, 1)

                def turn_maxima(st):
                    h, u = number(st), st[1]
                    pe.wait_ge(max_ready, h + 1)
                    wait(pe, out_copied, 2 * h - 2)
                    for j in range(2):
                        last = pe.transpose(max_t[:, j * P:(j + 1) * P],
                                            maxparts[:, u % 2, j].rearrange("p a s -> p (a s)"), k.ident_b[:])
                    last.then_inc(max_turned, 1)

                side.tensor_first(pe)
                pe.wait_ge(ones_set, 1)

                def step(st):
                    t = after(st, -LAG)
                    for s in range(HSTEP):
                        if scores(st):
                            scores_qk(st, s)
                        if scores(t):
                            scores_kq(t, s)
                        if s == 0 and scores(after(t, -1)):
                            turn_outputs(after(t, -1), 0)
                        if s == 1 and scores(after(t, -1)):
                            outputs(after(t, -1), 1)
                        if s == 3 and scores(after(t, -1)):
                            turn_outputs(after(t, -1), 1)
                        if s == 3 and scores(after(st, -1)):
                            turn_maxima(after(st, -1))
                        if s == 6 and scores(t):
                            outputs(t, 0)
                        side.tensor(pe, st, s)

                emit(pe, step)
                side.tensor_last(pe)

            @block.vector
            def _(dve):
                nc.vector.memset(kst[ROWS:ROWS + MROWS], 1.0).then_inc(ones_set, 1)
                side.vector_first(dve)

                def reduce(st, s):
                    h, u = number(st), st[1]
                    dve.wait_ge(s_ready, HSTEP * h + s + 1)
                    if causal:
                        nc.vector.tensor_reduce(blockmax[:, u % 2, s, :], ps[:, QK_BANKS[s % 3], 0:cols].rearrange("p (b n) -> p b n", n=P),
                                                AX.X, ALU.max, negate=True).then_inc(s_free, 1)
                    else:
                        nc.vector.tensor_reduce(negmax[:, u % 2, :, s], ps[:, QK_BANKS[s % 3], :].rearrange("p (j n) -> p j n", j=2),
                                                AX.X, ALU.max, negate=True).then_inc(s_free, 1)

                def cut(st):
                    h, u = number(st), st[1]
                    v = u % 2
                    dve.wait_ge(s_free, HSTEP * h + HSTEP)
                    if causal:
                        nc.vector.tensor_copy(negmax[:, v, 0, :], blockmax[:, v, :, 0]).then_inc(cut_step, 1)
                        nc.vector.tensor_tensor(negmax[:, v, 1, :], blockmax[:, v, :, 1], blockmax[:, v, :, 2], ALU.min).then_inc(cut_step, 1)
                        dve.wait_ge(cut_step, 3 * h + 2)
                    wait(dve, max_turned, h - 1)
                    nc.vector.tensor_copy(maxparts[:, v, :, 0, :], negmax[:, v]).then_inc(cut_step, 1)
                    per = 3 if causal else 1
                    dve.wait_ge(cut_step, per * h + per)
                    nc.vector.tensor_tensor(maxparts[:, v, :, 1, :], negmax[:, v], maxparts[:, v, :, 0, :], ALU.subtract).then_inc(max_ready, 1)

                def divide(st):
                    h, b, half = number(st), batch_of(st), st[1] % 2
                    dve.wait_ge(out_turned, 2 * h + 2)
                    o = outs_qd.rearrange("p j (s e) -> p j s e", e=VW)
                    nc.vector.reciprocal(recip[:], o[:, :, :, DH]).then_inc(recips, 1)
                    dve.wait_ge(recips, h + 1)
                    for j in range(2):
                        dst = out[:, bass.ds(2 * b + j, 1), :].rearrange("p a (c h d) -> p (a c) h d", c=DC, d=DH)
                        dst = dst[:, :, 4 * half:4 * half + 4, :].rearrange("p c h d -> p h c d")
                        last = nc.vector.tensor_tensor(dst, o[:, j, :, 0:DH].rearrange("p (h c) d -> p h c d", c=DC),
                                                       recip[:, j, :].rearrange("p (h c) -> p h c", c=DC).unsqueeze(3).to_broadcast([P, 4, DC, DH]),
                                                       ALU.mult)
                    last.then_inc(divided, 1)


                def step(st):
                    before = after(st, -LAG - 1)
                    for s in range(HSTEP):
                        if scores(st):
                            reduce(st, s)
                        if s == 5 and scores(before):
                            divide(before)
                        side.vector(dve, st, s, divided)
                    if scores(st):
                        cut(st)

                emit(dve, step)
                side.vector_last(dve, divided)

            @block.scalar
            def _(act):
                nc.scalar.memzero(v_aug[:]).then_inc(own, 1)
                act.wait_ge(own, 1)
                nc.scalar.activation(v_aug[:, :, :, :, DH], v_aug[:, :, :, :, DH], ACT.Exp).then_inc(own, 1)

                def exponential(st, s):
                    h = number(st)
                    act.wait_ge(t_ready, HSTEP * h + s + 1)
                    if s % 4 == 0:
                        wait(act, pv_done, 2 * h - 1 + s // 4)
                    nc.scalar.activation(probs[:, s, 0:cols], ps[:, 2 + s % 2, 0:cols], ACT.Exp, scale=scale).then_inc(exped, 1)

                def copy_values(st):
                    b, v = batch_of(st), st[1] // 2
                    act.wait_ge(v_in[v], 16 * st[0] + 16)
                    wait(act, pv_done, 4 * b - 4)
                    for j in range(2):
                        done = nc.scalar.copy(v_aug[:, v, j, :, 0:DH].rearrange("p (h c) d -> p c h d", c=DC),
                                              v_raw[:, v, j, :].rearrange("p (c h d) -> p c h d", c=DC, d=DH))
                    done.then_inc(v_ready, 1)

                def copy_outputs(st, g):
                    h = number(st)
                    act.wait_ge(pv_done, 2 * h + g + 1)
                    wait(act, out_turned, 2 * h + g - 1)
                    nc.scalar.copy(turned_in[:, g, :], outs_dq).then_inc(out_copied, 1)

                def copy_maxima(st):
                    h, u = number(st), st[1]
                    act.wait_ge(max_turned, h + 1)
                    old = after(st, -2)
                    if scores(old):
                        act.wait_ge(max_in[old[1]], 32 * old[0] + 32)
                    nc.scalar.copy(maxrows[:, u % 2, :], max_t).then_inc(max_copied, 1)

                act.wait_ge(own, 2)
                side.scalar_first(act)

                def step(st):
                    t = after(st, -LAG)
                    for s in range(HSTEP):
                        if scores(t):
                            exponential(t, s)
                        if s == 2 and scores(after(t, -1)):
                            copy_outputs(after(t, -1), 1)
                        if s == 3 and scores(after(st, -1)):
                            copy_maxima(after(st, -1))
                        if s == 5 and st[1] % 2 and scores(st):
                            copy_values(st)
                        if s == 7 and scores(t):
                            copy_outputs(t, 0)
                        side.scalar(act, st, s)

                emit(act, step)
                side.scalar_last(act)
        sweep(nc, used)


def pass_on(eng, sem, count, passed):
    eng.wait_ge(sem, count)
    eng.sem_inc(passed, 1)


class Route:
    lead, lag = 0, 1

    def open(self, nc, k, ctx, sem, ps):
        sb = lambda n, shape, dt: ctx.enter_context(nc.sbuf_tensor(f"rt_{n}", shape, dt))
        E = EXPERTS
        self.nc, self.k, self.ps = nc, k, ps
        self.gate = sb("gate", [P, DC, E], F32)
        self.before = sb("before", [P, P], BF16)
        self.ones = sb("ones", [P, P], BF16)
        self.list_end = sb("list_end", [P, E], F32)
        self.token = sb("token", [P, TILES], I32)
        self.tile_no = sb("tile_no", [P, 2], F32)
        self.zeros = sb("zeros", [P, LISTS], I32)
        self.stats = sb("stats", [P, 2, 6], F32)
        self.moments = sb("moments", [P, 2, 2], F32)
        self.rstd = sb("rstd", [P, 2], I32)
        self.newton = sb("newton", [P, 2], F32)
        self.rows = sb("rows", [P, 2, 2, D + E], F32)
        self.xn_t = sb("xn_t", [P, DC * SEQ], F32)
        self.logits = sb("logits", [P, 2, E], F32)
        self.others = sb("others", [P, 2, E], F32)
        self.best = sb("best", [P, 2, 8], F32)
        self.expo = sb("expo", [P, 2, E], F32)
        self.chosen = sb("chosen", [P, 2, E], F32)
        self.total = sb("total", [P, 3, 2], F32)
        self.mask = sb("mask", [P, TILES, E], BF16)
        self.earlier = sb("earlier", [P, TILES + 1, E], BF16)
        self.back = sb("back", [P, 2, E], F32)
        self.now = sb("now", [P, 2, E], F32)
        self.place = sb("place", [P, TILES, E], F32)
        self.top = sb("top", [P, 2, TOP_K], F32)
        self.idx = sb("idx", [P, 2, 2, TOP_K], I32)
        self.number = sb("number", [P, 2, 2], I32)
        self.shift_g = sb("shift_g", [P, E], F32)
        self.place_g = sb("place_g", [P, TILES, E], F32)
        self.top_g = sb("top_g", [P, TILES, TOP_K], F32)
        self.count = sb("count", [P, 6, E], F32)
        self.count_i = sb("count_i", [P, E], I32)
        self.below = sb("below", [P, 2, 3, E], F32)
        self.sums = sb("sums", [P, 2, 4], F32)
        self.distinct = sb("distinct", [P, 1], F32)
        self.row = sb("row", [P, 2], F32)
        self.row_i = sb("row_i", [P, 2], I32)
        self.ids_raw = sb("ids_raw", [P, 2, P], I32)
        self.ids_f = sb("ids_f", [P, 2, P], F32)
        self.line = sb("line", [1, 3, ETABLE], F32)
        self.line_i = sb("line_i", [1, ETABLE], I32)

        self.c_in, self.zero_set, self.zeroed = sem("constants_in"), sem("zero_set"), sem("lists_zeroed")
        self.outs_zeroed = sem("outs_zeroed")
        self.own, self.choice, self.none_set = sem("ln_own"), sem("choice_own"), sem("none_set")
        self.xn_ready, self.xn_turned, self.xn_copied, self.logits_ready = sem("xn_ready"), sem("xn_turned"), sem("xn_copied"), sem("logits_ready")
        self.shifted, self.exped, self.counted, self.ranked = sem("shifted"), sem("route_exped"), sem("counted"), sem("ranked")
        self.ranks_read, self.weights_ready, self.slots_ready, self.staged = sem("ranks_read"), sem("weights_ready"), sem("slots_ready"), sem("staged")
        self.rows_out = [sem("rows_out0"), sem("rows_out1")]
        self.scattered, self.ids_in = [k.indirect("scattered0"), k.indirect("scattered1")], k.indirect("ids_in")
        self.tables, self.counts_ready = sem("tables_own"), sem("counts_ready")
        self.rows_ready, self.ids_f_ready, self.turned = sem("rows_ready"), sem("ids_f_ready"), sem("turned")
        self.constants = [(self.gate, "gate"), (self.before, "c_before"), (self.ones, "c_ones"), (self.list_end, "c_list_end"),
                          (self.token, "c_token"), (self.tile_no, "c_tile")]

    def batch(self, st, rank):
        i, u = st
        i, m = {0: ((i - 1, u // 2) if u % 2 else None), 1: ((i - 1, 0) if u == 2 else (i - 2, 1) if u == 0 else None),
                2: ((i - 1, 0) if u == 3 else (i - 2, 1) if u == 1 else None), 3: ((i - 2, u // 2) if u % 2 == 0 else None)}[rank] or (None, None)
        if i is None or (isinstance(i, int) and not 0 <= i < PAIRS):
            return None
        return i, m

    def before_load(self, sp, i, u):
        pass

    def sync_first(self, sp):
        for tile, name in self.constants:
            sp.dma_start(tile[:], self.k.dram[name]).then_inc(self.c_in, 16)
        sp.wait_ge(self.zero_set, 1)
        sp.dma_start(self.k.lists.rearrange("(p n) o -> p (n o)", p=P), self.zeros[:]).then_inc(self.zeroed, 16)
        four = self.zeros[:].bitcast(F32).rearrange("p (o t d) -> p o t d", o=1, d=D)
        n = LISTS // D
        rest = self.k.outs[EXPECTED:ETILES].rearrange("(g t) p d -> p g t d", t=n)
        for g in range((ETILES - EXPECTED) // n):
            sp.dma_start(rest[:, g], four[:, 0]).then_inc(self.outs_zeroed, 16)

    def write(self, sp, i, u):
        sp.wait_ge(self.weights_ready, 2 * i + u + 1)
        sp.dma_start(self.k.xn[bass.ds(4 * i + 2 * u, 2)].rearrange("t p d -> p t d"), self.rows[:, u]).then_inc(self.rows_out[u], 16)

    def sync(self, sp, st):
        b = self.batch(st, 3)
        if b:
            self.write(sp, *b)

    def sync_last(self, sp):
        for m in SYNC_LEFT:
            self.write(sp, m // 2, m % 2)
        for u in range(2):
            sp.wait_ge(self.rows_out[u], 16 * PAIRS)
        sp.wait_ge(self.outs_zeroed, 16 * ((ETILES - EXPECTED) // (LISTS // D)))

    def gpsimd(self, pool):
        nc, k = self.nc, self.k
        nc.gpsimd.memset(self.zeros[:], 0).then_inc(self.zero_set, 1)
        pool.wait_ge(self.c_in, 16 * len(self.constants))
        pool.wait_ge(self.zeroed, 16)

        def scatter(i, u):
            m = 2 * i + u
            for j in range(2):
                nc.gpsimd.tensor_copy(self.number[:, u, j:j + 1], self.token[:, bass.ds(2 * m + j, 1)]).then_inc(self.staged, 1)
            pass_on(pool, self.staged, 2 * m + 2, k.passed)
            pass_on(pool, self.slots_ready, m + 1, k.passed)
            for j in range(2):
                for s in range(TOP_K):
                    nc.gpsimd.indirect_dma_start(k.lists, bass.IndirectOffsetOnAxis(ap=self.idx[:, u, j, s:s + 1], axis=0),
                                                 self.number[:, u, j:j + 1], None).then_inc(self.scattered[u], 16)

        for u in range(2):
            scatter(0, u)
        with pool.Fori(1, PAIRS) as i:
            for u in range(2):
                pass_on(pool, self.scattered[u], 16 * 2 * TOP_K * i, k.passed)
                scatter(i, u)
        for u in range(2):
            pool.wait_ge(self.scattered[u], 16 * 2 * TOP_K * PAIRS)
        pool.wait_ge(self.rows_ready, 2)
        for a in range(2):
            nc.gpsimd.indirect_dma_start(self.ids_raw[:, a, :], None, k.lists.rearrange("(r n) o -> r (n o)", n=P),
                                         bass.IndirectOffsetOnAxis(ap=self.row_i[:, a:a + 1], axis=0)).then_inc(self.ids_in, 16)
        pool.wait_ge(self.ids_in, 32)

    def pair(self, i, u):
        return bass.ds(4 * i + 2 * u, 2)

    def first(self, dve, s, i, u, divided):
        nc, k, own = self.nc, self.k, self.own
        x2 = k.x[:, self.pair(i, u), :]
        if s == 0:
            dve.sem_clear(own)
            dve.wait_ge(divided, 4 * i + 2 * u + 2)
            nc.vector.tensor_tensor(x2, x2, k.ao[:, self.pair(i, u), :], ALU.add).then_inc(own, 1)
        elif s == 1:
            dve.wait_ge(own, 1)
            for j in range(2):
                nc.vector.bn_stats(self.stats[:, j, :], self.tile(i, u, j)).then_inc(own, 1)
        elif s == 2:
            for j in range(2):
                dve.wait_ge(own, 2 + j)
                nc.vector.bn_aggr(self.moments[:, j, :], self.stats[:, j, :]).then_inc(own, 1)
            dve.wait_ge(own, 5)
            inverse_root(nc, own, 5, self.rstd[:], self.moments[:, :, 1], self.newton[:], 0)
        elif s in (3, 4, 6):
            inverse_root(nc, own, 5, self.rstd[:], self.moments[:, :, 1], self.newton[:], {3: 1, 4: 2, 6: 3}[s])
        elif s == 7:
            dve.wait_ge(own, 5 + 4 * NEWTON_STEPS)
            if not isinstance(i, int) or i:
                dve.wait_ge(self.rows_out[u], 16 * i)
            for j in range(2):
                nc.vector.tensor_scalar(self.rows[:, u, j, 0:D], self.tile(i, u, j), self.moments[:, j, 0:1],
                                        self.rstd[:, j:j + 1].bitcast(F32), ALU.subtract, ALU.mult).then_inc(self.xn_ready, 1)

    def tile(self, i, u, j):
        return self.k.x[:, bass.ds(4 * i + 2 * u + j, 1), :].rearrange("p a d -> p (a d)")

    def logits_ps(self):
        return self.ps[:, 0:2 * EXPERTS].rearrange("p (j e) -> p j e", j=2)

    def ranks_ps(self):
        return self.ps[:, 2 * EXPERTS:4 * EXPERTS].rearrange("p (j e) -> p j e", j=2)

    def second(self, dve, s, i, u):
        nc, own = self.nc, self.choice
        if s == 4:
            dve.sem_clear(own)
            dve.wait_ge(self.logits_ready, 4 * i + 2 * u + 2)
            nc.vector.tensor_copy(self.logits[:], self.logits_ps()).then_inc(own, 1)
        elif s == 5:
            dve.wait_ge(own, 1)
            for j in range(2):
                nc.vector.max(self.best[:, j, :], self.logits[:, j, :]).then_inc(own, 1)
        elif s == 6:
            for j in range(2):
                dve.wait_ge(own, 2 + j)
                nc.vector.match_replace(self.others[:, j, :], self.best[:, j, :], self.logits[:, j, :], -3.0e38).then_inc(own, 1)
        elif s == 7:
            dve.wait_ge(own, 5)
            nc.vector.tensor_tensor(self.mask[:, self.pair(i, u), :], self.others[:], self.logits[:], ALU.not_equal).then_inc(own, 1)
            nc.vector.tensor_tensor(self.expo[:], self.logits[:], self.best[:, :, 0:1].to_broadcast([P, 2, EXPERTS]),
                                    ALU.subtract).then_inc(self.shifted, 1)

    def third(self, dve, s, i, u):
        nc, own = self.nc, self.choice
        t, m = 4 * i + 2 * u, 2 * i + u
        mask2 = self.mask[:, self.pair(i, u), :]
        if s == 0:
            dve.wait_ge(own, 6)
            nc.vector.tensor_tensor(self.earlier[:, bass.ds(t + 1, 1), :], self.earlier[:, bass.ds(t, 1), :],
                                    self.mask[:, bass.ds(t, 1), :], ALU.add).then_inc(own, 1)
        elif s == 1:
            dve.wait_ge(own, 7)
            nc.vector.tensor_tensor(self.earlier[:, bass.ds(t + 2, 1), :], self.earlier[:, bass.ds(t + 1, 1), :],
                                    self.mask[:, bass.ds(t + 1, 1), :], ALU.add).then_inc(self.counted, 1)
        elif s == 3:
            dve.wait_ge(self.exped, m + 1)
            nc.vector.tensor_tensor(self.chosen[:], self.expo[:], mask2, ALU.mult).then_inc(own, 1)
            nc.vector.tensor_reduce(self.total[:, 0, :], self.expo[:], AX.X, ALU.add).then_inc(own, 1)
        elif s == 4:
            dve.wait_ge(own, 8)
            nc.vector.tensor_reduce(self.total[:, 1, :], self.chosen[:], AX.X, ALU.add).then_inc(own, 1)
            dve.wait_ge(self.ranked, m + 1)
            nc.vector.tensor_tensor(self.back[:], self.list_end[:].unsqueeze(1).to_broadcast([P, 2, EXPERTS]), self.ranks_ps(),
                                    ALU.subtract).then_inc(self.ranks_read, 1)
        elif s == 5:
            dve.wait_ge(own, 10)
            nc.vector.scalar_tensor_tensor(self.total[:, 2, :], self.total[:, 0, :], 1e-20, self.total[:, 1, :], ALU.mult, ALU.add).then_inc(own, 1)
        elif s == 6:
            dve.wait_ge(self.ranks_read, m + 1)
            nc.vector.tensor_tensor(self.now[:], self.back[:], mask2, ALU.mult).then_inc(own, 1)
            dve.wait_ge(own, 11)
            nc.vector.reciprocal(self.total[:, 2, :], self.total[:, 2, :]).then_inc(own, 1)
        elif s == 7:
            dve.wait_ge(own, 13)
            for j in range(2):
                nc.vector.max(self.top[:, j, :], self.now[:, j, :]).then_inc(own, 1)
            nc.vector.tensor_copy(self.place[:, self.pair(i, u), :], self.now[:])
            nc.vector.tensor_tensor(self.rows[:, u, :, D:D + EXPERTS], self.chosen[:],
                                    self.total[:, 2, :].unsqueeze(2).to_broadcast([P, 2, EXPERTS]), ALU.mult).then_inc(self.weights_ready, 1)

    def fourth(self, dve, i, u):
        dve.wait_ge(self.choice, 15)
        if not isinstance(i, int) or i:
            dve.wait_ge(self.scattered[u], 16 * 2 * TOP_K * i)
        self.nc.vector.tensor_scalar(self.idx[:, u], self.top[:], -1.0, float(EXPERTS * TOK), ALU.mult, ALU.add).then_inc(self.slots_ready, 1)

    def vector_first(self, dve):
        self.nc.vector.memset(self.earlier[:, 0, :], 0.0).then_inc(self.none_set, 1)
        dve.wait_ge(self.none_set, 1)
        dve.wait_ge(self.c_in, 16 * len(self.constants))

    def vector(self, dve, st, s, divided):
        first, second, third, fourth = (self.batch(st, n) for n in range(4))
        if fourth and s == 0:
            self.fourth(dve, *fourth)
        if third:
            self.third(dve, s, *third)
        if first:
            self.first(dve, s, *first, divided)
        if second:
            self.second(dve, s, *second)

    def vector_last(self, dve, divided):
        for st in REST:
            for s in range(HSTEP):
                self.vector(dve, st, s, divided)
        self.make_tables(dve)

    def make_tables(self, dve):
        nc, k, E = self.nc, self.k, EXPERTS
        own, steps = self.tables, [0]
        count, below, sums, distinct, line = self.count, self.below, self.sums, self.distinct, self.line
        GEND = float((ETILES + 1) * P)

        def then(ins):
            ins.then_inc(own, 1)
            steps[0] += 1
            dve.wait_ge(own, steps[0])

        tiles, ends, starts, one, some = (count[:, n, :] for n in range(5))
        dve.wait_ge(self.counts_ready, 1)
        then(nc.vector.tensor_scalar(self.count_i[:], self.ps[:, 4 * E:5 * E], float(P - 1), None, ALU.add))
        then(nc.vector.tensor_scalar(self.count_i[:], self.count_i[:], 7, None, ALU.logical_shift_right))
        then(nc.vector.tensor_copy(tiles, self.count_i[:]))
        then(nc.vector.memset(one, 1.0))
        then(nc.vector.tensor_tensor_scan(ends, one, tiles, 0.0, ALU.mult, ALU.add))
        then(nc.vector.tensor_tensor(starts, ends, tiles, ALU.subtract))
        then(nc.vector.tensor_copy(k.tiles_used[:], ends[0:1, E - 1:E]))
        then(nc.vector.tensor_scalar(some, tiles, 0.5, None, ALU.is_gt))
        then(nc.vector.tensor_reduce(distinct[:], some, AX.X, ALU.add))
        then(nc.vector.tensor_scalar(distinct[:], distinct[:], -1.0, None, ALU.add))
        for a in range(2):
            then(nc.vector.tensor_scalar(below[:, a, 0, :], ends, self.tile_no[:, a:a + 1], None, ALU.is_le))
            then(nc.vector.tensor_tensor(below[:, a, 1, :], below[:, a, 0, :], some, ALU.mult))
            then(nc.vector.tensor_tensor(below[:, a, 2, :], below[:, a, 0, :], tiles, ALU.mult))
            then(nc.vector.tensor_reduce(sums[:, a, 0:3], below[:, a], AX.X, ALU.add))
            then(nc.vector.tensor_scalar(sums[:, a, 0:1], sums[:, a, 0:1], float(E - 1), None, ALU.min))
            then(nc.vector.tensor_tensor(sums[:, a, 1:2], sums[:, a, 1:2], distinct[:], ALU.min))
            then(nc.vector.tensor_tensor(sums[:, a, 3:4], self.tile_no[:, a:a + 1], sums[:, a, 2:3], ALU.subtract))
            then(nc.vector.tensor_scalar(sums[:, a, 3:4], sums[:, a, 3:4], float(TILES - 1), None, ALU.min))
            then(nc.vector.tensor_scalar(self.row[:, a:a + 1], sums[:, a, 0:1], float(TILES), None, ALU.mult))
            nc.vector.tensor_tensor(self.row_i[:, a:a + 1], self.row[:, a:a + 1], sums[:, a, 3:4], ALU.add).then_inc(self.rows_ready, 1)

        then(nc.vector.tensor_scalar(self.shift_g[:], starts, -float(P), GEND, ALU.mult, ALU.add))
        then(nc.vector.tensor_tensor(self.shift_g[:], self.shift_g[:], self.list_end[:], ALU.subtract))
        then(nc.vector.tensor_tensor(self.place_g[:], self.mask[:], self.shift_g[:].unsqueeze(1).to_broadcast([P, TILES, E]), ALU.mult))
        then(nc.vector.tensor_tensor(self.place_g[:], self.place_g[:], self.place[:], ALU.add))
        for t in range(TILES):
            last = nc.vector.max(self.top_g[:, t, :], self.place_g[:, t, :])
        then(last)
        then(nc.vector.tensor_scalar(k.slot[:], self.top_g[:], -1.0, GEND, ALU.mult, ALU.add))

        dve.wait_ge(self.turned, 1)
        then(nc.vector.tensor_copy(line[:, 0:2, :].rearrange("p q n -> p (q n)"), self.ps[0:1, :]))
        then(nc.vector.memset(line[:, 2, 0:1], 1.0))
        then(nc.vector.tensor_tensor(line[:, 2, 1:ETABLE], line[:, 1, 1:ETABLE], line[:, 1, 0:ETABLE - 1], ALU.not_equal))
        then(nc.vector.tensor_copy(k.table[:, 0, :], line[:, 0, :]))
        then(nc.vector.tensor_copy(self.line_i[:], line[:, 1, :]))
        then(nc.vector.tensor_scalar(k.table[:, 1, :], self.line_i[:], WRING - 1, None, ALU.bitwise_and))
        then(nc.vector.tensor_copy(k.table[:, 2, :], line[:, 2, :]))
        dve.wait_ge(self.ids_in, 32)
        nc.vector.tensor_copy(self.ids_f[:], self.ids_raw[:]).then_inc(self.ids_f_ready, 1)
        dve.wait_ge(self.turned, 2)
        then(nc.vector.tensor_copy(k.ids[:], self.ps[:, 0:ETABLE]))

    def tensor_first(self, pe):
        pe.wait_ge(self.c_in, 16 * len(self.constants))

    def tensor(self, pe, st, s):
        second, third = self.batch(st, 1), self.batch(st, 2)
        if second:
            i, u = second
            m = 2 * i + u
            if s == 0:
                pe.wait_ge(self.xn_ready, 2 * m + 2)
                wait(pe, self.ranks_read, m)
                for j in range(2):
                    for c in range(DC):
                        last = pe.transpose(self.ps[:, (DC * j + c) * P:(DC * j + c + 1) * P], self.rows[:, u, j, c * P:(c + 1) * P], self.k.ident[:])
                last.then_inc(self.xn_turned, 1)
            elif s in (2, 3):
                if s == 2:
                    pe.wait_ge(self.xn_copied, m + 1)
                j = s - 2
                for c in range(DC):
                    last = pe.matmul(self.ps[:, j * EXPERTS:(j + 1) * EXPERTS], self.xn_t[:, (DC * j + c) * P:(DC * j + c + 1) * P],
                                     self.gate[:, c, :], start=(c == 0), stop=(c == DC - 1))
                last.then_inc(self.logits_ready, 1)
        if third and s == 2:
            i, u = third
            pe.wait_ge(self.counted, 2 * i + u + 1)
            pe.matmul(self.ranks_ps(), self.before[:], self.mask[:, self.pair(i, u), :], start=True, stop=False)
            pe.matmul(self.ranks_ps(), self.ones[:], self.earlier[:, self.pair(i, u), :], start=False, stop=True).then_inc(self.ranked, 1)

    def tensor_last(self, pe):
        for st in REST:
            for s in range(HSTEP):
                self.tensor(pe, st, s)
        pe.wait_ge(self.ranks_read, BATCH)
        pe.matmul(self.ps[:, 4 * EXPERTS:5 * EXPERTS], self.ones[:], self.earlier[:, TILES, :], start=True, stop=True).then_inc(self.counts_ready, 1)
        pe.wait_ge(self.rows_ready, 2)
        for a in range(2):
            for q in range(2):
                last = pe.transpose(self.ps[0:1, (2 * q + a) * P:(2 * q + a + 1) * P], self.sums[:, a, q:q + 1], self.k.ident[:])
        last.then_inc(self.turned, 1)
        pe.wait_ge(self.ids_f_ready, 1)
        for a in range(2):
            last = pe.transpose(self.ps[:, a * P:(a + 1) * P], self.ids_f[:, a, :], self.k.ident[:])
        last.then_inc(self.turned, 1)

    def scalar_first(self, act):
        pass

    def scalar(self, act, st, s):
        second, third = self.batch(st, 1), self.batch(st, 2)
        if second and s == 1:
            i, u = second
            act.wait_ge(self.xn_turned, 2 * i + u + 1)
            self.nc.scalar.copy(self.xn_t[:], self.ps).then_inc(self.xn_copied, 1)
        if third and s == 1:
            i, u = third
            act.wait_ge(self.shifted, 2 * i + u + 1)
            self.nc.scalar.activation(self.expo[:], self.expo[:], ACT.Exp).then_inc(self.exped, 1)

    def scalar_last(self, act):
        for st in REST:
            for s in range(HSTEP):
                self.scalar(act, st, s)


def experts(nc, k, begin, end):
    tag = f"ex{begin}"
    with ExitStack() as ctx:
        sb = lambda n, shape, dt: ctx.enter_context(nc.sbuf_tensor(f"{tag}_{n}", shape, dt))
        used = []
        sem = phase_semaphores(nc, ctx, tag, used)
        R = 8
        w_gu = sb("w_gu", [P, WRING, DC, 2 * FF], F32)
        w_down = sb("w_down", [FH, WRING, 2, D], F32)
        idx = sb("idx", [P, R], I32)
        rows = sb("rows", [P, R, D + EXPERTS], F32)
        rows_t = sb("rows_t", [P, 2, DC * P], F32)
        act_g = sb("act_g", [P, 2, FF], F32)
        hidden = sb("hidden", [P, 2, FF], F32)
        hidden_t = sb("hidden_t", [FH, 2, 2 * P], F32)
        result = sb("result", [P, R, D], F32)
        ps = ctx.enter_context(nc.psum_tensor(f"{tag}_ps", [P, 8, 512], F32))
        w_in = [sem(f"w_in{j}") for j in range(R)]
        staged = sem("staged")
        rows_in = [k.indirect(f"{tag}_rows_in{j}") for j in range(R)]
        rows_turned, rows_copied = sem("rows_turned"), sem("rows_copied")
        gu_ready, silu_ready, hidden_ready = sem("gu_ready"), sem("silu_ready"), sem("hidden_ready")
        hidden_turned, hidden_copied, down_ready = sem("hidden_turned"), sem("hidden_copied"), sem("down_ready")
        result_ready = sem("result_ready")
        out_done = [sem(f"out_done{j}") for j in range(R)]
        ROUNDS = (end - begin) // R
        table = k.table[:, :, begin:end]
        ids, outs = k.ids[:, begin:end], k.outs[begin:end]

        def needed(eng):
            if begin == 0:
                return nullcontext()
            return eng.If(eng.value_load(k.tiles_used[0:1, 0:1], min_val=1, max_val=ETILES) > begin)

        with nc.Block() as block:

            def rounds(eng, step, last=ROUNDS):
                for j in range(R):
                    step(0, j)
                with eng.Fori(1, last) as i:
                    for j in range(R):
                        step(i, j)

            @block.sync
            def _(sp):
                def step(i, j):
                    t = R * i + j
                    expert = sp.value_load(table[0:1, 0, bass.ds(t, 1)], min_val=0, max_val=EXPERTS - 1)
                    ring = sp.value_load(table[0:1, 1, bass.ds(t, 1)], min_val=0, max_val=WRING - 1)
                    other = sp.value_load(table[0:1, 2, bass.ds(t, 1)], min_val=0, max_val=1)
                    fresh = None if isinstance(i, int) and t == 0 else other > 0
                    wait(sp, down_ready, t - WRING + 1)
                    sp.dma_start(w_gu[:, bass.ds(ring, 1)].rearrange("p a c n -> p (a c n)"),
                                 k.dram["w_gu"][bass.ds(expert, 1)].rearrange("e p c n -> (e p) (c n)"), cond=fresh).then_inc(w_in[j], 16)
                    sp.dma_start(w_down[:, bass.ds(ring, 1)].rearrange("p a c n -> p (a c n)"),
                                 k.dram["w_down"][bass.ds(expert, 1)].rearrange("e p c n -> (e p) (c n)"), cond=fresh).then_inc(w_in[j], 16)

                with needed(sp):
                    rounds(sp, step)

            @block.gpsimd
            def _(pool):
                def step(i, j):
                    t = R * i + j
                    if not isinstance(i, int):
                        pass_on(pool, result_ready, t - R + 1, k.passed)
                    nc.gpsimd.tensor_copy(idx[:, j:j + 1], ids[:, bass.ds(t, 1)]).then_inc(staged, 1)
                    pass_on(pool, staged, t + 1, k.passed)
                    nc.gpsimd.indirect_dma_start(rows[:, j, :], None, k.xn.rearrange("t p d -> (t p) d"),
                                                 bass.IndirectOffsetOnAxis(ap=idx[:, j:j + 1], axis=0)).then_inc(rows_in[j], 16)

                with needed(pool):
                    rounds(pool, step)

            @block.tensor
            def _(pe):
                def turn_rows(i, j):
                    t = R * i + j
                    pe.wait_ge(rows_in[j], 16 * i + 16)
                    wait(pe, rows_copied, t - 1)
                    for c in range(DC):
                        last = pe.transpose(ps[:, j % 2, c * P:(c + 1) * P], rows[:, j, c * P:(c + 1) * P], k.ident[:])
                    last.then_inc(rows_turned, 1)

                def gate_up(i, j, ring, c):
                    t = R * i + j
                    if c == 0:
                        pe.wait_ge(w_in[j], 32 * i + 32)
                        pe.wait_ge(rows_copied, t + 1)
                        wait(pe, hidden_ready, t - 1)
                    last = pe.matmul(ps[:, 2 + j % 2, 0:2 * FF], rows_t[:, j % 2, c * P:(c + 1) * P],
                                     w_gu[:, bass.ds(ring, 1), c, :].rearrange("p a n -> p (a n)"), start=(c == 0), stop=(c == DC - 1))
                    if c == DC - 1:
                        last.then_inc(gu_ready, 1)

                def turn_hidden(i, j):
                    t = R * i + j
                    pe.wait_ge(hidden_ready, t + 1)
                    wait(pe, hidden_copied, t - 1)
                    for c in range(2):
                        last = pe.transpose(ps[0:FH, 4 + j % 2, c * P:(c + 1) * P], hidden[:, j % 2, c * FH:(c + 1) * FH], k.ident[:])
                    last.then_inc(hidden_turned, 1)

                def down(i, j, ring):
                    t = R * i + j
                    pe.wait_ge(hidden_copied, t + 1)
                    wait(pe, result_ready, t - 1)
                    for c in range(2):
                        last = pe.matmul(ps[:, 6 + j % 2, 0:D], hidden_t[:, j % 2, c * P:(c + 1) * P],
                                         w_down[:, bass.ds(ring, 1), c, :].rearrange("p a n -> p (a n)"), start=(c == 0), stop=(c == 1))
                    last.then_inc(down_ready, 1)

                def buffer_of(i, j):
                    return pe.value_load(table[0:1, 1, bass.ds(R * i + j, 1)], min_val=0, max_val=WRING - 1)

                def after(i, j, n):
                    return (i, j + n) if j + n < R else (i + 1, j + n - R)

                def step(i, j, rings, first=False, left=R):
                    before = (i, j - 1) if j else (i - 1, R - 1)
                    gate_up(i, j, rings[1], 0)
                    if not first:
                        turn_hidden(*before)
                    gate_up(i, j, rings[1], 1)
                    following = buffer_of(*after(i, j, 1)) if left > 1 and j < R - 1 else None
                    if left > 2:
                        turn_rows(*after(i, j, 2))
                    if not first:
                        down(*before, rings[0])
                    return rings[1], following

                def steps(i, last=False):
                    rings = (None, buffer_of(i, 0))
                    if not isinstance(i, int) or i:
                        rings = (buffer_of(i - 1, R - 1), rings[1])
                    for j in range(R):
                        rings = step(i, j, rings, first=(isinstance(i, int) and i == j == 0), left=R - j if last else R)

                with needed(pe):
                    turn_rows(0, 0)
                    turn_rows(0, 1)
                    steps(0)
                    with pe.Fori(1, ROUNDS - 1) as i:
                        steps(i)
                    steps(ROUNDS - 1, last=True)
                    turn_hidden(ROUNDS - 1, R - 1)
                    down(ROUNDS - 1, R - 1, buffer_of(ROUNDS - 1, R - 1))

            @block.scalar
            def _(act):
                def copy_rows(i, j):
                    t = R * i + j
                    act.wait_ge(rows_turned, t + 1)
                    wait(act, gu_ready, t - 1)
                    nc.scalar.copy(rows_t[:, j % 2], ps[:, j % 2, 0:DC * P]).then_inc(rows_copied, 1)

                def silu(i, j):
                    t = R * i + j
                    act.wait_ge(gu_ready, t + 1)
                    wait(act, hidden_ready, t - 1)
                    nc.scalar.activation(act_g[:, j % 2], ps[:, 2 + j % 2, 0:FF], ACT.Silu).then_inc(silu_ready, 1)

                def store(i, j):
                    t = R * i + j
                    act.wait_ge(result_ready, t + 1)
                    act.dma_start(outs[bass.ds(t, 1)].rearrange("t p d -> (t p) d"), result[:, j]).then_inc(out_done[j], 16)

                def step(i, j, first=0, left=R):
                    silu(i, j)
                    if left > 2:
                        copy_rows(*((i, j + 2) if j < R - 2 else (i + 1, j + 2 - R)))
                    if first < 1:
                        store(*((i, j - 2) if j > 1 else (i - 1, R + j - 2)))

                with needed(act):
                    copy_rows(0, 0)
                    copy_rows(0, 1)
                    for j in range(R):
                        step(0, j, first=2 - j)
                    with act.Fori(1, ROUNDS - 1) as i:
                        for j in range(R):
                            step(i, j)
                    for j in range(R):
                        step(ROUNDS - 1, j, left=R - j)
                    store(ROUNDS - 1, R - 2)
                    store(ROUNDS - 1, R - 1)
                    for j in range(R):
                        act.wait_ge(out_done[j], 16 * ROUNDS)

            @block.vector
            def _(dve):
                def gated(i, j):
                    t = R * i + j
                    dve.wait_ge(silu_ready, t + 1)
                    wait(dve, hidden_turned, t - 1)
                    nc.vector.tensor_tensor(hidden[:, j % 2], act_g[:, j % 2], ps[:, 2 + j % 2, FF:2 * FF], ALU.mult).then_inc(hidden_ready, 1)

                def copy_hidden(i, j):
                    t = R * i + j
                    dve.wait_ge(hidden_turned, t + 1)
                    wait(dve, down_ready, t - 1)
                    nc.vector.tensor_copy(hidden_t[:, j % 2], ps[0:FH, 4 + j % 2, 0:2 * P]).then_inc(hidden_copied, 1)

                def weigh(i, j):
                    t = R * i + j
                    expert = dve.value_load(table[0:1, 0, bass.ds(t, 1)], min_val=0, max_val=EXPERTS - 1)
                    dve.wait_ge(down_ready, t + 1)
                    if not isinstance(i, int) or i:
                        dve.wait_ge(out_done[j], 16 * i)
                    nc.vector.tensor_scalar(result[:, j], ps[:, 6 + j % 2, 0:D], rows[:, j, bass.ds(expert + D, 1)], None, ALU.mult).then_inc(result_ready, 1)

                def step(i, j, first=False):
                    before = (i, j - 1) if j else (i - 1, R - 1)
                    if not first:
                        copy_hidden(*before)
                    gated(i, j)
                    if not first:
                        weigh(*before)

                with needed(dve):
                    for j in range(R):
                        step(0, j, first=(j == 0))
                    with dve.Fori(1, ROUNDS) as i:
                        for j in range(R):
                            step(i, j)
                    copy_hidden(ROUNDS - 1, R - 1)
                    weigh(ROUNDS - 1, R - 1)
        sweep(nc, used)


class Combine:
    lead, lag = 1, 0

    def open(self, nc, k, ctx, sem, ps):
        sb = lambda n, shape, dt: ctx.enter_context(nc.sbuf_tensor(f"cb_{n}", shape, dt))
        self.nc, self.k = nc, k
        self.wq = sb("wq", [P, DC, DC, P], F32)
        self.idx = sb("idx", [P, 2, 2, TOP_K], I32)
        self.gathered = sb("gathered", [P, 2, 2, TOP_K, D], F32)
        self.moe = sb("moe", [P, 2, D], F32)
        self.stats = sb("stats", [P, 2, 6], F32)
        self.moments = sb("moments", [P, 2, 2], F32)
        self.rstd = sb("rstd", [P, 2], I32)
        self.newton = sb("newton", [P, 2], F32)
        self.xn = sb("xn", [P, 2, D], F32)
        self.xn_t = sb("xn_t", [P, DC, SEQ], F32)
        self.rest = sb("rest", [P, DC * SEQ], F32)
        self.parts = sb("parts", [P, 2, 3, DC * SEQ], BF16)
        self.ps = ps
        self.w_in, self.staged = sem("wq_in"), sem("idx_staged")
        self.rows_in = [k.indirect("cb_rows_in0"), k.indirect("cb_rows_in1")]
        self.own, self.summed = sem("combine_own"), sem("summed")
        self.xn_ready, self.xn_turned, self.xn_copied, self.q_ready = sem("xn_ready"), sem("xn_turned"), sem("xn_copied"), sem("q_ready")
        self.high, self.rested, self.middle, self.split = sem("high"), sem("rested"), sem("middle"), sem("split")
        self.written = [sem("written0"), sem("written1")]

    def write(self, sp, i, u):
        sp.wait_ge(self.split, 2 * i + u + 1)
        stack = self.k.q1_stack[bass.ds(2 * i + u, 1)].rearrange("b t p n -> p (b t) n")
        at = 0
        for part, n in Q_PARTS:
            sp.dma_start(stack[:, at:at + n, :],
                         self.parts[:, u, part:part + 1, :].to_broadcast([P, n, DC * SEQ])).then_inc(self.written[u], 16)
            at += n

    def sync_first(self, sp):
        sp.dma_start(self.wq[:], self.k.dram["wq"]).then_inc(self.w_in, 16)
        for u in range(2):
            self.write(sp, 0, u)

    def sync(self, sp, st):
        e = self.ending(st)
        if e:
            self.write(sp, *e)

    def sync_last(self, sp):
        for u in range(2):
            sp.wait_ge(self.written[u], 16 * len(Q_PARTS) * PAIRS)

    def before_load(self, sp, i, u):
        sp.wait_ge(self.written[u], 16 * len(Q_PARTS) * (i + 1))

    def gpsimd(self, pool):
        nc, k = self.nc, self.k

        def gather(i, u):
            b = 2 * i + u
            for j in range(2):
                nc.gpsimd.tensor_copy(self.idx[:, u, j, :], k.slot[:, bass.ds(2 * b + j, 1), :].rearrange("p a s -> p (a s)")).then_inc(self.staged, 1)
            pass_on(pool, self.staged, 2 * b + 2, k.passed)
            for j in range(2):
                for s in range(TOP_K):
                    nc.gpsimd.indirect_dma_start(self.gathered[:, u, j, s, :], None, k.outs.rearrange("t p d -> (t p) d"),
                                                 bass.IndirectOffsetOnAxis(ap=self.idx[:, u, j, s:s + 1], axis=0)).then_inc(self.rows_in[u], 16)

        for u in range(2):
            gather(0, u)
        with pool.Fori(1, PAIRS) as i:
            for u in range(2):
                pass_on(pool, self.summed, 8 * (2 * i + u - 1), k.passed)
                gather(i, u)

    def add(self, dve, i, u, piece):
        j, q = piece // 4, piece % 4
        cols = slice(q * D // 4, (q + 1) * D // 4)
        if piece == 0:
            dve.wait_ge(self.rows_in[u], 16 * 2 * TOP_K * (i + 1))
        self.nc.vector.tensor_reduce(self.moe[:, j, cols], self.gathered[:, u, j, :, cols].rearrange("p s d -> p d s"),
                                     AX.X, ALU.add).then_inc(self.summed, 1)

    def tile(self, i, u, j):
        return self.k.x[:, bass.ds(4 * i + 2 * u + j, 1), :].rearrange("p a d -> p (a d)")

    def add_to_x(self, dve, i, u):
        dve.sem_clear(self.own)
        dve.wait_ge(self.summed, 8 * (2 * i + u + 1))
        for j in range(2):
            self.nc.vector.tensor_tensor(self.tile(i, u, j), self.tile(i, u, j), self.moe[:, j, :], ALU.add).then_inc(self.own, 1)

    def statistics(self, dve, i, u):
        for j in range(2):
            dve.wait_ge(self.own, 1 + j)
            self.nc.vector.bn_stats(self.stats[:, j, :], self.tile(i, u, j)).then_inc(self.own, 1)
        for j in range(2):
            dve.wait_ge(self.own, 3 + j)
            self.nc.vector.bn_aggr(self.moments[:, j, :], self.stats[:, j, :]).then_inc(self.own, 1)

    def root(self, dve, part):
        if part == 0:
            dve.wait_ge(self.own, 6)
        inverse_root(self.nc, self.own, 6, self.rstd[:], self.moments[:, :, 1], self.newton[:], part)

    def normalise(self, dve, i, u):
        dve.wait_ge(self.own, 6 + 4 * NEWTON_STEPS)
        wait(dve, self.xn_turned, 2 * i + u)
        for j in range(2):
            self.nc.vector.tensor_scalar(self.xn[:, j, :], self.tile(i, u, j), self.moments[:, j, 0:1], self.rstd[:, j:j + 1].bitcast(F32),
                                         ALU.subtract, ALU.mult).then_inc(self.xn_ready, 1)

    def take_rest(self, dve, i, u):
        dve.wait_ge(self.high, 2 * i + u + 1)
        self.nc.vector.tensor_tensor(self.rest[:], self.ps, self.parts[:, u, 0, :], ALU.subtract).then_inc(self.rested, 1)

    def take_low(self, dve, i, u):
        dve.wait_ge(self.middle, 2 * i + u + 1)
        self.nc.vector.tensor_tensor(self.parts[:, u, 2, :], self.rest[:], self.parts[:, u, 1, :], ALU.subtract).then_inc(self.split, 1)

    def vector_first(self, dve):
        for u in range(2):
            for piece in range(8):
                self.add(dve, 0, u, piece)
            self.add_to_x(dve, 0, u)
            self.statistics(dve, 0, u)
            for part in range(4):
                self.root(dve, part)
            self.normalise(dve, 0, u)
            self.take_rest(dve, 0, u)
            self.take_low(dve, 0, u)

    def started(self, st):
        i, u = st
        if not isinstance(i, int) or 0 <= i < PAIRS - 1:
            return i + 1, u // 2

    def ending(self, st):
        i, u = st
        if u == 0 and (not isinstance(i, int) or 1 <= i < PAIRS):
            return i, 1
        if u == 2:
            return self.started((i, 0))

    def vector(self, dve, st, s, divided):
        b, e, even = self.started(st), self.ending(st), st[1] % 2 == 0
        if b and even and s:
            self.add(dve, *b, s - 1)
        if e and s == 5:
            self.take_rest(dve, *e)
        if e and s == 7:
            self.take_low(dve, *e)
        if b and not even:
            if s == 0:
                self.add(dve, *b, 7)
            elif s == 1:
                self.add_to_x(dve, *b)
            elif s == 2:
                self.statistics(dve, *b)
            elif s < 7:
                self.root(dve, s - 3)
            else:
                self.normalise(dve, *b)

    def vector_last(self, dve, divided):
        pass

    def turn(self, pe, i, u):
        pe.wait_ge(self.xn_ready, 4 * i + 2 * u + 2)
        wait(pe, self.rested, 2 * i + u)
        for j in range(2):
            for c in range(DC):
                last = pe.transpose(self.ps[:, c * SEQ + j * P:c * SEQ + (j + 1) * P], self.xn[:, j, c * P:(c + 1) * P], self.k.ident[:])
        last.then_inc(self.xn_turned, 1)

    def project(self, pe, i, u, m):
        if m == 0:
            pe.wait_ge(self.xn_copied, 2 * i + u + 1)
        for c in range(DC):
            last = pe.matmul(self.ps[:, m * SEQ:(m + 1) * SEQ], self.wq[:, c, m, :], self.xn_t[:, c, :],
                             start=(c == 0), stop=(c == DC - 1))
        last.then_inc(self.q_ready, 1)

    def tensor_first(self, pe):
        pe.wait_ge(self.w_in, 16)
        for u in range(2):
            self.turn(pe, 0, u)
            self.project(pe, 0, u, 0)
            self.project(pe, 0, u, 1)

    def tensor(self, pe, st, s):
        e = self.ending(st)
        if e and s == 0:
            self.turn(pe, *e)
        if e and s in (2, 3):
            self.project(pe, *e, s - 2)

    def tensor_last(self, pe):
        pass

    def copy_turned(self, act, i, u):
        act.wait_ge(self.xn_turned, 2 * i + u + 1)
        self.nc.scalar.copy(self.xn_t[:].rearrange("p c t -> p (c t)"), self.ps).then_inc(self.xn_copied, 1)

    def take_high(self, act, i, u):
        if not isinstance(i, int) or i:
            act.wait_ge(self.written[u], 16 * len(Q_PARTS) * i)
        act.wait_ge(self.q_ready, 4 * i + 2 * u + 2)
        self.nc.scalar.copy(self.parts[:, u, 0, :], self.ps).then_inc(self.high, 1)

    def take_middle(self, act, i, u):
        act.wait_ge(self.rested, 2 * i + u + 1)
        self.nc.scalar.copy(self.parts[:, u, 1, :], self.rest[:]).then_inc(self.middle, 1)

    def scalar_first(self, act):
        for u in range(2):
            self.copy_turned(act, 0, u)
            self.take_high(act, 0, u)
            self.take_middle(act, 0, u)

    def scalar(self, act, st, s):
        e = self.ending(st)
        if e and s == 1:
            self.copy_turned(act, *e)
        if e and s == 4:
            self.take_high(act, *e)
        if e and s == 6:
            self.take_middle(act, *e)

    def scalar_last(self, act):
        pass


def finish(nc, k):
    with ExitStack() as ctx:
        sb = lambda n, shape, dt: ctx.enter_context(nc.sbuf_tensor(f"ff_{n}", shape, dt))
        used = []
        sem = phase_semaphores(nc, ctx, "ff", used)
        wo = sb("wo", [P, DC, D], F32)
        router = sb("router", [P, DC, BLOCKS], F32)
        router_b = sb("router_b", [P, BLOCKS], F32)
        w1 = sb("w1", [P, DC, HID], F32)
        b1 = sb("b1", [P, FC], F32)
        w2 = sb("w2", [P, FC, D], F32)
        b2 = sb("b2", [P, D], F32)
        spread = sb("spread", [BLOCKS, FC, P], BF16)
        eps = sb("eps", [P, 1], F32)
        ao_t = sb("ao_t", [P, 2, DC * P], F32)
        stats = sb("stats", [P, TILES, 6], F32)
        moments = sb("moments", [P, TILES, 2], F32)
        deviation = sb("deviation", [P, TILES], F32)
        rstd = sb("rstd", [P, TILES], F32)
        newton = sb("newton", [P, TILES], F32)
        xn = sb("xn", [P, 2, D], F32)
        xn_t = sb("xn_t", [P, DC, TOK], F32)
        logits = sb("logits", [P, TILES, BLOCKS], F32)
        best = sb("best", [P, TILES, 8], F32)
        others = sb("others", [P, TILES, BLOCKS], F32)
        closed = sb("closed", [P, TILES, BLOCKS], F32)
        closed_t = sb("closed_t", [BLOCKS, TOK], BF16)
        hidden_t = sb("hidden_t", [P, 2, FC, 512], F32)
        y = sb("y", [P, 2, D], F32)
        ps = ctx.enter_context(nc.psum_tensor("ff_ps", [P, 8, 512], F32))
        logit_ps = ps[:, 6, 0:TILES * BLOCKS].rearrange("p (t e) -> p t e", e=BLOCKS)

        w_in, eps_set, own = sem("w_in"), sem("eps_set"), sem("own")
        a_turned, a_copied, a_ready, x_done = sem("a_turned"), sem("a_copied"), sem("a_ready"), sem("x_done")
        stats_done, moments_done, deviations = sem("stats_done"), sem("moments_done"), sem("deviations")
        xn_ready, turned, copied, logits_ready = sem("xn_ready"), sem("turned"), sem("copied"), sem("logits_ready")
        masks_ready, masks_turned, masks_copied = sem("masks_ready"), sem("masks_turned"), sem("masks_copied")
        x_biased = sem("x_biased")
        hid_ready, relu_done, y_ready, y_done = sem("hid_ready"), sem("relu_done"), sem("y_ready"), sem("y_done")
        out_done = [sem("out_done0"), sem("out_done1")]
        LOADS = 8
        FBLOCKS = TOK // 512
        FT = 512 // P

        with nc.Block() as block:

            @block.sync
            def _(sp):
                for tile, name in ((wo, "wo"), (router, "router"), (w1, "w1"), (b1, "b1"), (w2, "w2"), (spread, "c_spread")):
                    sp.dma_start(tile[:], k.dram[name]).then_inc(w_in, 16)
                sp.dma_start(router_b[:], k.dram["router_b"].to_broadcast([P, BLOCKS])).then_inc(w_in, 16)
                sp.dma_start(b2[:], k.dram["b2"].to_broadcast([P, D])).then_inc(w_in, 16)
                with sp.Fori(0, TILES // 2) as i:
                    for u in range(2):
                        t = 2 * i + u
                        sp.wait_ge(y_done, t + 1)
                        sp.dma_start(k.result[bass.ds(t, 1)].rearrange("t p d -> (t p) d"), y[:, u]).then_inc(out_done[u], 16)
                for u in range(2):
                    sp.wait_ge(out_done[u], 16 * (TILES // 2))

            @block.gpsimd
            def _(pool):
                nc.gpsimd.memset(eps[:], EPS).then_inc(eps_set, 1)
                pool.wait_ge(w_in, 16 * LOADS)
                with pool.Fori(0, TILES) as t:
                    pool.wait_ge(xn_ready, t + 1)
                    nc.gpsimd.tensor_tensor(k.x[:, bass.ds(t, 1), :].rearrange("p a d -> p (a d)"),
                                            k.x[:, bass.ds(t, 1), :].rearrange("p a d -> p (a d)"), b2[:], ALU.add).then_inc(x_biased, 1)

            @block.tensor
            def _(pe):
                pe.wait_ge(w_in, 16 * LOADS)

                for t in range(TILES):
                    u = t % 2
                    for c in range(DC):
                        last = pe.transpose(ps[:, u, c * P:(c + 1) * P], k.ao[:, t, c * P:(c + 1) * P], k.ident[:])
                    last.then_inc(a_turned, 1)
                    pe.wait_ge(a_copied, t + 1)
                    for c in range(DC):
                        last = pe.matmul(ps[:, 2 + u, 0:D], ao_t[:, u, c * P:(c + 1) * P], wo[:, c, :], start=(c == 0), stop=(c == DC - 1))
                    last.then_inc(a_ready, 1)

                for t in range(TILES):
                    u = t % 2
                    pe.wait_ge(xn_ready, t + 1)
                    for c in range(DC):
                        last = pe.transpose(ps[:, u, c * P:(c + 1) * P], xn[:, u, c * P:(c + 1) * P], k.ident[:])
                    last.then_inc(turned, 1)
                    pe.wait_ge(copied, t + 1)
                    for c in range(DC):
                        last = pe.matmul(logit_ps[:, t, :], xn_t[:, c, t * P:(t + 1) * P], router[:, c, :], start=(c == 0), stop=(c == DC - 1))
                    last.then_inc(logits_ready, 1)

                pe.wait_ge(masks_ready, TILES)
                for f in range(FBLOCKS):
                    if f:
                        pe.wait_ge(masks_copied, f)
                    for j in range(FT):
                        last = pe.transpose(ps[0:BLOCKS, 7, j * P:(j + 1) * P], closed[:, FT * f + j, :], k.ident[:])
                    last.then_inc(masks_turned, 1)
                pe.wait_ge(masks_copied, FBLOCKS)

                def hidden(f, u):
                    for m in range(FC):
                        wait(pe, relu_done, FC * f + m - 3)
                        bank = ps[:, 2 + m % 4, :]
                        for c in range(DC):
                            pe.matmul(bank, w1[:, c, m * P:(m + 1) * P], xn_t[:, c, bass.ds(f * 512, 512)], start=(c == 0), stop=False)
                        pe.matmul(bank, spread[:, m, :], closed_t[:, bass.ds(f * 512, 512)], start=False, stop=True).then_inc(hid_ready, 1)

                def output(f, u):
                    for j in range(FT):
                        wait(pe, y_done, FT * f + j - 1)
                        for m in range(FC):
                            if j == 0:
                                pe.wait_ge(relu_done, FC * f + m + 1)
                            last = pe.matmul(ps[:, j % 2, 0:D], hidden_t[:, u, m, j * P:(j + 1) * P], w2[:, m, :],
                                             start=(m == 0), stop=(m == FC - 1))
                        last.then_inc(y_ready, 1)

                hidden(0, 0)
                for f in range(FBLOCKS):
                    if f + 1 < FBLOCKS:
                        hidden(f + 1, (f + 1) % 2)
                    output(f, f % 2)

            @block.scalar
            def _(act):
                def copy_a(i, u, first):
                    t = 2 * i + u
                    act.wait_ge(a_turned, t + 1)
                    if not first:
                        act.wait_ge(x_done, t - 1)
                    nc.scalar.copy(ao_t[:, u], ps[:, u, 0:DC * P]).then_inc(a_copied, 1)

                for u in range(2):
                    copy_a(0, u, True)
                with act.Fori(1, TILES // 2) as i:
                    for u in range(2):
                        copy_a(i, u, False)
                act.wait_ge(eps_set, 1)
                act.wait_ge(moments_done, TILES)
                nc.scalar.activation(deviation[:], moments[:, :, 1], ACT.Sqrt, bias=eps[:, 0:1]).then_inc(deviations, 1)
                with act.Fori(0, TILES // 2) as i:
                    for u in range(2):
                        t = 2 * i + u
                        act.wait_ge(turned, t + 1)
                        nc.scalar.copy(xn_t[:, :, bass.ds(t * P, P)], ps[:, u, 0:DC * P].rearrange("p (c n) -> p c n", c=DC)).then_inc(copied, 1)
                for f in range(FBLOCKS):
                    act.wait_ge(masks_turned, f + 1)
                    nc.scalar.copy(closed_t[:, f * 512:(f + 1) * 512], ps[0:BLOCKS, 7, :]).then_inc(masks_copied, 1)
                for f in range(FBLOCKS):
                    for m in range(FC):
                        act.wait_ge(hid_ready, FC * f + m + 1)
                        if f > 1 and m == 0:
                            act.wait_ge(y_ready, FT * (f - 1))
                        nc.scalar.activation(hidden_t[:, f % 2, m, :], ps[:, 2 + m % 4, :], ACT.Relu, bias=b1[:, m:m + 1]).then_inc(relu_done, 1)

            @block.vector
            def _(dve):
                steps = [0]

                def then(ins):
                    ins.then_inc(own, 1)
                    steps[0] += 1
                    dve.wait_ge(own, steps[0])

                with dve.Fori(0, TILES // 2) as i:
                    for u in range(2):
                        t = 2 * i + u
                        tile = k.x[:, bass.ds(t, 1), :].rearrange("p a d -> p (a d)")
                        dve.wait_ge(a_ready, t + 1)
                        nc.vector.tensor_tensor(tile, tile, ps[:, 2 + u, 0:D], ALU.add).then_inc(x_done, 1)
                        dve.wait_ge(x_done, t + 1)
                        nc.vector.bn_stats(stats[:, bass.ds(t, 1), :].rearrange("p a s -> p (a s)"), tile).then_inc(stats_done, 1)
                dve.wait_ge(stats_done, TILES)
                for t in range(TILES):
                    nc.vector.bn_aggr(moments[:, t, :], stats[:, t, :]).then_inc(moments_done, 1)
                dve.wait_ge(deviations, 1)
                then(nc.vector.reciprocal(rstd[:], deviation[:]))
                refine(nc, own, steps[0], rstd[:], moments[:, :, 1], newton[:])
                steps[0] += NEWTON_STEPS
                dve.wait_ge(own, steps[0])

                def normalise(t, u):
                    nc.vector.tensor_scalar(xn[:, u], k.x[:, bass.ds(t, 1), :].rearrange("p a d -> p (a d)"),
                                            moments[:, bass.ds(t, 1), 0:1].rearrange("p a s -> p (a s)"), rstd[:, bass.ds(t, 1)],
                                            ALU.subtract, ALU.mult).then_inc(xn_ready, 1)

                normalise(0, 0)
                normalise(1, 1)
                with dve.Fori(1, TILES // 2) as i:
                    for u in range(2):
                        dve.wait_ge(turned, 2 * i + u - 1)
                        normalise(2 * i + u, u)

                dve.wait_ge(logits_ready, TILES)
                dve.wait_ge(w_in, 16 * LOADS)
                then(nc.vector.tensor_tensor(logits[:], logit_ps, router_b[:].unsqueeze(1).to_broadcast([P, TILES, BLOCKS]), ALU.add))
                for t in range(TILES):
                    last = nc.vector.max(best[:, t, :], logits[:, t, :])
                then(last)
                then(nc.vector.memset(best[:, :, TOP_B:8], 3.0e38))
                for t in range(TILES):
                    last = nc.vector.match_replace(others[:, t, :], best[:, t, :], logits[:, t, :], -3.0e38)
                then(last)
                then(nc.vector.tensor_tensor(closed[:], others[:], logits[:], ALU.is_equal))
                nc.vector.tensor_scalar(closed[:], closed[:], MASKED, None, ALU.mult).then_inc(masks_ready, TILES)

                dve.wait_ge(x_biased, TILES)
                for t in range(TILES):
                    u = t % 2
                    dve.wait_ge(y_ready, t + 1)
                    if t > 1:
                        dve.wait_ge(out_done[u], 16 * (t // 2))
                    nc.vector.tensor_tensor(y[:, u], k.x[:, t, :], ps[:, u, 0:D], ALU.add).then_inc(y_done, 1)


def build(nc, dram, out):
    k = Kernel()
    k.dram, k.result = dram, out
    scratch = lambda name, shape, dt: nc.dram_tensor(name, shape, dt, kind="Internal").ap()
    stack = (BATCH, TERMS, P, DC * SEQ)
    k.q0_stack, k.k0_stack = scratch("q0_stack", stack, BF16), scratch("k0_stack", stack, BF16)
    k.q1_stack, k.k1_stack = scratch("q1_stack", stack, BF16), scratch("k1_stack", stack, BF16)
    k.v1 = scratch("v1_rows", (BATCH, 2, P, D), F32)
    k.xn = scratch("moe_rows", (TILES, P, D + EXPERTS), F32)
    k.lists = scratch("expert_lists", (EXPERTS * TOK, 1), I32)
    k.outs = scratch("expert_outs", (ETILES, P, D), F32)
    with ExitStack() as ctx:
        sb = lambda n, shape, dt: ctx.enter_context(nc.sbuf_tensor(n, shape, dt))
        k.x = sb("x", [P, TILES, D], F32)
        k.ao = sb("attention_out", [P, TILES, D], F32)
        k.slot = sb("slot", [P, TILES, TOP_K], I32)
        k.table = sb("tile_table", [1, 3, ETABLE], I32)
        k.tiles_used = sb("tiles_used", [1, 1], I32)
        k.ids = sb("slot_tokens", [P, ETABLE], I32)
        k.indirect = lambda n: ctx.enter_context(nc.semaphore(f"indirect_{n}"))
        k.passed = ctx.enter_context(nc.semaphore("passed"))
        constants(nc, k, ctx)
        prepare(nc, k)
        attention(nc, k, "a0", k.q0_stack, k.k0_stack, dram["ctx"], 1.0 / float(np.sqrt(np.float32(D))), False, k.ao, Route())
        experts(nc, k, 0, EXPECTED)
        experts(nc, k, EXPECTED, ETILES)
        attention(nc, k, "a1", k.q1_stack, k.k1_stack, k.v1, 1.0 / float(np.sqrt(np.float32(DH))), True, k.ao, Combine())
        finish(nc, k)


def _layouts(inputs):
    a = {n: np.ascontiguousarray(v) for n, v in inputs.items()}
    heads = lambda w: w.reshape(DC, HEADS // DC, DH, -1).transpose(0, 2, 1, 3)
    c = a["ctx_1024"]
    out = {
        "x": a["x"].reshape(TILES, P, D),
        "ctx": c.reshape(BATCH, 2, P, D),
        "ctx_t": c.reshape(BATCH, SEQ, DC, HEADS // DC, DH).transpose(0, 4, 3, 2, 1).reshape(BATCH, P, DC, SEQ),
    }
    wk = heads(a["L1_xattn_Wk"]).reshape(DC, P, D)
    wk = heads(wk.transpose(2, 0, 1).reshape(D, D)).reshape(DC, P, DC, P)
    out["wk"] = wk.transpose(1, 0, 2, 3)
    out["wv"] = heads(a["L1_xattn_Wv"].T).reshape(DC, P, D).transpose(1, 0, 2)
    wq = heads(a["L1_xattn_Wq"]).reshape(DC, P, DC, P)
    out["wq"] = wq.transpose(3, 2, 0, 1)
    rows = lambda w: w.T.reshape(DC, P, -1).transpose(1, 0, 2)
    out["wo"] = rows(a["L1_xattn_Wo"])
    out["gate"] = rows(a["L0_ffn_gate_w"])
    out["router"] = rows(a["L1_ffn_router_w"])
    out["router_b"] = a["L1_ffn_router_b"].reshape(1, BLOCKS)
    out["w1"] = rows(a["L1_ffn_w1"])
    out["b1"] = a["L1_ffn_b1"].reshape(FC, P).T
    out["w2"] = a["L1_ffn_w2"].T.reshape(FC, P, D).transpose(1, 0, 2)
    out["b2"] = a["L1_ffn_b2"].reshape(1, D)
    gu = np.stack([a["L0_ffn_w_gate"], a["L0_ffn_w_up"]], 1).reshape(EXPERTS, 2 * FF, DC, P)
    out["w_gu"] = gu.transpose(0, 3, 2, 1)
    out["w_down"] = a["L0_ffn_w_down"].reshape(EXPERTS, D, 2, FH).transpose(0, 3, 2, 1)
    bf16 = mybir.dt.np(BF16)
    p = np.arange(P)
    out["c_ident"] = np.eye(P, dtype=np.float32)
    out["c_ident_b"] = np.eye(P, dtype=np.float32).astype(bf16)
    late = np.where(p[None, :] > p[:, None], np.float32(MASKED), np.float32(0))
    out["c_mask_qk"] = late.astype(bf16)
    out["c_mask_kq"] = late.T.astype(bf16)
    out["c_before"] = (p[:, None] < p[None, :]).astype(bf16)
    out["c_ones"] = np.ones((P, P), bf16)
    out["c_list_end"] = np.broadcast_to(EXPERTS * TOK - TOK * np.arange(EXPERTS, dtype=np.float32), (P, EXPERTS))
    out["c_token"] = (P * np.arange(TILES)[None, :] + p[:, None]).astype(np.int32)
    out["c_tile"] = (P * np.arange(2)[None, :] + p[:, None]).astype(np.float32)
    spread = (np.arange(HID) // (HID // BLOCKS))[None, :] == np.arange(BLOCKS)[:, None]
    out["c_spread"] = spread.reshape(BLOCKS, FC, P).astype(bf16)
    return {n: np.ascontiguousarray(v) for n, v in out.items()}


def kernel(**inputs):
    import numpy as _np
    import concourse.bacc as _bacc
    from concourse import mybir as _mybir
    from concourse.bass_utils import run_bass_kernel_spmd as _run

    nc = _bacc.Bacc("TRN2", target_bir_lowering=False, num_devices=1)
    arrays, dram = {}, {}
    for name, a in _layouts(inputs).items():
        arrays[f"in_{name}_dram"] = a
        dram[name] = nc.dram_tensor(f"in_{name}_dram", a.shape, _mybir.dt.from_np(a.dtype), kind="ExternalInput").ap()
    out = nc.dram_tensor("out_0_dram", (TILES, P, D), _mybir.dt.float32, kind="ExternalOutput").ap()
    build(nc, dram, out)
    r = _run(nc, [arrays], core_ids=[0])
    return _np.asarray(r.results[0]["out_0_dram"]).reshape(BATCH, SEQ, D)
```

```python
from contextlib import ExitStack, nullcontext

import numpy as np

import concourse.bass as bass
from concourse import mybir

F32 = mybir.dt.float32
BF16 = mybir.dt.bfloat16
I32 = mybir.dt.int32
ALU = mybir.AluOpType
ACT = mybir.ActivationFunctionType
AX = mybir.AxisListType

P = 128
BATCH, SEQ, D = 8, 256, 256
PAIRS = BATCH // 2
TOK = BATCH * SEQ
TILES = TOK // P
DC = D // P
HEADS, DH = 16, 16
HSTEP = HEADS // 2
STEPS = 2 * BATCH
TERMS = 6
ROWS = TERMS * DH
MROWS = 2
VW = 32
EPS = 1e-5
MASKED = -1e30

EXPERTS, TOP_K, FF = 64, 8, 192
FH = FF // 2
ETILES = -(-((TOK * TOP_K + EXPERTS * (P - 1)) // P) // 8) * 8
EXPECTED = TOK * TOP_K // P + EXPERTS // 2
ETABLE = 256
ROUNDS = STEPS // 4 + 1
START = 6
LISTS = EXPERTS * TILES
WRING = 4

BLOCKS, TOP_B, HID = 16, 4, 1024
FC = HID // P

PARTS = 3
RUNS = [3, 2, 1]


def wait(eng, sem, count):
    if not (isinstance(count, int) and count <= 0):
        eng.wait_ge(sem, count)


def phase_semaphores(nc, ctx, prefix, used):
    def make(name):
        used.append(ctx.enter_context(nc.semaphore(f"{prefix}_{name}")))
        return used[-1]
    return make


def sweep(nc, used):
    with nc.Block() as block:

        @block.sync
        def _(sp):
            for sem in used:
                sp.sem_clear(sem)


NEWTON_STEPS = 3


def refine(nc, own, n, rstd, variance, scratch):
    nc.vector.scalar_tensor_tensor(scratch, rstd, -0.5, rstd, ALU.mult, ALU.mult).then_inc(own, 1)
    nc.vector.wait_ge(own, n + 1)
    nc.vector.scalar_tensor_tensor(scratch, variance, EPS, scratch, ALU.add, ALU.mult).then_inc(own, 1)
    nc.vector.wait_ge(own, n + 2)
    nc.vector.scalar_tensor_tensor(rstd, scratch, 1.5, rstd, ALU.add, ALU.mult).then_inc(own, 1)


def inverse_root(nc, own, n, rstd, variance, scratch, part):
    if part == 0:
        nc.vector.tensor_scalar(scratch, variance, EPS, None, ALU.add).then_inc(own, 1)
        nc.vector.wait_ge(own, n + 1)
        nc.vector.tensor_scalar(rstd, scratch.bitcast(I32), 1, None, ALU.logical_shift_right).then_inc(own, 1)
        nc.vector.wait_ge(own, n + 2)
        nc.vector.tensor_scalar(rstd, rstd, -1.0, float(0x5F3759DF), ALU.mult, ALU.add).then_inc(own, 1)
    else:
        nc.vector.wait_ge(own, n + NEWTON_STEPS * part)
        refine(nc, own, n + NEWTON_STEPS * part, rstd.bitcast(F32), variance, scratch)


class Kernel:
    pass


def constants(nc, k, ctx):
    sb = lambda name, shape, dt: ctx.enter_context(nc.sbuf_tensor(name, shape, dt))
    k.ident = sb("ident", [P, P], F32)
    k.ident_b = sb("ident_b", [P, P], BF16)
    k.mask_qk = sb("mask_qk", [P, P], BF16)
    k.mask_kq = sb("mask_kq", [P, P], BF16)
    loaded = ctx.enter_context(nc.semaphore("constants_loaded"))
    with nc.Block() as block:

        @block.sync
        def _(sp):
            pairs = [(k.ident, "c_ident"), (k.ident_b, "c_ident_b"), (k.mask_qk, "c_mask_qk"), (k.mask_kq, "c_mask_kq")]
            for tile, name in pairs:
                sp.dma_start(tile[:], k.dram[name]).then_inc(loaded, 16)
            sp.wait_ge(loaded, 16 * len(pairs))


def prepare(nc, k):
    with ExitStack() as ctx:
        sb = lambda name, shape, dt: ctx.enter_context(nc.sbuf_tensor(name, shape, dt))
        used = []
        sem = phase_semaphores(nc, ctx, "prep", used)
        ctx_t = sb("ctx_t", [P, 2, DC, SEQ], F32)
        wk = sb("wk", [P, DC, DC, P], F32)
        wv = sb("wv", [P, DC, D], F32)
        stats = sb("ln0_stats", [P, 2, 6], F32)
        moments = sb("ln0_moments", [P, 2, 2], F32)
        deviation = sb("ln0_deviation", [P, 2], F32)
        rstd = sb("ln0_rstd", [P, 2], F32)
        newton = sb("ln0_newton", [P, 2], F32)
        eps = sb("ln0_eps", [P, 1], F32)
        xn = sb("ln0_out", [P, 2, 2, D], F32)
        rest = sb("split_rest", [P, 2, 3, DC * SEQ], F32)
        parts = sb("split_parts", [P, 2, 3, 3, DC * SEQ], BF16)
        v1 = sb("v1", [P, 2, 2, D], F32)
        ps = ctx.enter_context(nc.psum_tensor("ps_prep", [P, 8, 512], F32))
        w_in = sem("w_in")
        x_in = [sem("x_in0"), sem("x_in1")]
        c_in = [sem("ctx_in0"), sem("ctx_in1")]
        own = sem("own")
        eps_set = sem("eps_set")
        ones_set = sem("ones_set")
        moments_ready = sem("moments")
        deviations = sem("deviations")
        xn_ready = sem("xn_ready")
        q_turned = sem("q_turned")
        k1_ready = sem("k1_ready")
        v1_ready = sem("v1_ready")
        high = sem("high")
        rested = sem("rested")
        middle = sem("middle")
        split = sem("split")
        v1_out = sem("v1_out")
        written = [sem("written0"), sem("written1")]
        WRITES = 4
        K0, Q0, K1 = 0, 1, 2
        stacks = {K0: k.k0_stack, Q0: k.q0_stack, K1: k.k1_stack}

        def source(kind, u):
            if kind == K0:
                return ctx_t[:, u].rearrange("p c t -> p (c t)")
            return ps[:, (0 if kind == Q0 else 2) + u, :]

        with nc.Block() as block:

            @block.sync
            def _(sp):
                def load_x(b, u):
                    sp.dma_start(k.x[:, bass.ds(2 * b, 2), :],
                                 k.dram["x"][bass.ds(2 * b, 2)].rearrange("t p d -> p t d")).then_inc(x_in[u], 16)

                def load_ctx(b, u):
                    sp.dma_start(ctx_t[:, u], k.dram["ctx_t"][bass.ds(b, 1)].rearrange("b p c t -> (b p) c t")).then_inc(c_in[u], 16)

                def write(b, u):
                    for kind in (K0, Q0, K1):
                        sp.wait_ge(split, 3 * b + kind + 1)
                        stack = stacks[kind][bass.ds(b, 1)].rearrange("b t p n -> p (b t) n")
                        sp.dma_start(stack, parts[:, u, kind]).then_inc(written[u], 16)
                    sp.wait_ge(v1_out, b + 1)
                    sp.dma_start(k.v1[bass.ds(b, 1)].rearrange("b t p d -> p (b t) d"), v1[:, u]).then_inc(written[u], 16)

                for u in range(2):
                    load_x(u, u)
                    load_ctx(u, u)
                sp.dma_start(wk[:], k.dram["wk"]).then_inc(w_in, 16)
                sp.dma_start(wv[:], k.dram["wv"]).then_inc(w_in, 16)
                with sp.Fori(0, PAIRS - 1) as i:
                    for u in range(2):
                        sp.wait_ge(x_in[u], 16 * i + 16)
                        load_x(2 * i + u + 2, u)
                        write(2 * i + u, u)
                        load_ctx(2 * i + u + 2, u)
                for u in range(2):
                    write(BATCH - 2 + u, u)
                for u in range(2):
                    sp.wait_ge(written[u], 16 * WRITES * (BATCH // 2))

            @block.vector
            def _(dve):
                def normalise(i, u):
                    b = 2 * i + u
                    dve.sem_clear(own)
                    dve.wait_ge(x_in[u], 16 * i + 16)
                    for j in range(2):
                        nc.vector.bn_stats(stats[:, j, :], k.x[:, bass.ds(2 * b + j, 1), :].rearrange("p a d -> p (a d)")).then_inc(own, 1)
                    for j in range(2):
                        dve.wait_ge(own, 1 + j)
                        nc.vector.bn_aggr(moments[:, j, :], stats[:, j, :]).then_inc(moments_ready, 1)
                    dve.wait_ge(deviations, b + 1)
                    nc.vector.reciprocal(rstd[:], deviation[:]).then_inc(own, 1)
                    dve.wait_ge(own, 3)
                    refine(nc, own, 3, rstd[:], moments[:, :, 1], newton[:])
                    dve.wait_ge(own, 3 + NEWTON_STEPS)
                    wait(dve, q_turned, b - 1)
                    for j in range(2):
                        nc.vector.tensor_scalar(xn[:, u, j, :].rearrange("p (c d h) -> p c h d", c=DC, d=DH),
                                                k.x[:, bass.ds(2 * b + j, 1), :].rearrange("p a (c h d) -> p (a c) h d", c=DC, d=DH),
                                                moments[:, j, 0:1], rstd[:, j:j + 1], ALU.subtract, ALU.mult).then_inc(xn_ready, 1)

                def rests(i, u):
                    for kind in (K0, Q0, K1):
                        dve.wait_ge(high, 3 * (2 * i + u) + kind + 1)
                        nc.vector.tensor_tensor(rest[:, u, kind, :], source(kind, u), parts[:, u, kind, 0, :],
                                                ALU.subtract).then_inc(rested, 1)

                normalise(0, 0)
                normalise(0, 1)
                rests(0, 0)
                with dve.Fori(1, PAIRS) as i:
                    normalise(i, 0)
                    rests(i - 1, 1)
                    normalise(i, 1)
                    rests(i, 0)
                rests(PAIRS - 1, 1)

            @block.scalar
            def _(act):
                def take_middle(b, u, kind):
                    act.wait_ge(rested, 3 * b + kind + 1)
                    nc.scalar.copy(parts[:, u, kind, 1, :], rest[:, u, kind, :]).then_inc(middle, 1)

                def roots(i, u):
                    act.wait_ge(moments_ready, 4 * i + 2 * u + 2)
                    nc.scalar.activation(deviation[:], moments[:, :, 1], ACT.Sqrt, bias=eps[:, 0:1]).then_inc(deviations, 1)

                def batch(i, u, first):
                    b = 2 * i + u
                    if not first:
                        act.wait_ge(written[u], 16 * WRITES * i)
                    act.wait_ge(c_in[u], 16 * i + 16)
                    nc.scalar.copy(parts[:, u, K0, 0, :], source(K0, u)).then_inc(high, 1)
                    act.wait_ge(q_turned, b + 1)
                    nc.scalar.copy(parts[:, u, Q0, 0, :], source(Q0, u)).then_inc(high, 1)
                    take_middle(b, u, K0)
                    act.wait_ge(k1_ready, b + 1)
                    nc.scalar.copy(parts[:, u, K1, 0, :], source(K1, u)).then_inc(high, 1)
                    take_middle(b, u, Q0)
                    act.wait_ge(v1_ready, b + 1)
                    nc.scalar.copy(v1[:, u].rearrange("p t d -> p (t d)"), ps[:, 4 + u, :]).then_inc(v1_out, 1)
                    take_middle(b, u, K1)

                act.wait_ge(eps_set, 1)
                roots(0, 0)
                roots(0, 1)
                batch(0, 0, True)
                roots(1, 0)
                batch(0, 1, True)
                with act.Fori(1, PAIRS - 1) as i:
                    roots(i, 1)
                    batch(i, 0, False)
                    roots(i + 1, 0)
                    batch(i, 1, False)
                roots(PAIRS - 1, 1)
                for u in range(2):
                    batch(PAIRS - 1, u, False)

            @block.gpsimd
            def _(pool):
                nc.gpsimd.memset(eps[:], EPS).then_inc(eps_set, 1)
                pool.wait_ge(eps_set, 1)
                nc.gpsimd.memset(k.kst[ROWS:ROWS + MROWS], 1.0).then_inc(ones_set, 1)
                pool.wait_ge(ones_set, 1)

                def low(b, u, kind):
                    pool.wait_ge(middle, 3 * b + kind + 1)
                    nc.gpsimd.tensor_tensor(parts[:, u, kind, 2, :], rest[:, u, kind, :], parts[:, u, kind, 1, :],
                                            ALU.subtract).then_inc(split, 1)

                with pool.Fori(0, BATCH // 2) as i:
                    for u in range(2):
                        for kind in (K0, Q0, K1):
                            low(2 * i + u, u, kind)

            @block.tensor
            def _(pe):
                def batch(i, u, first):
                    b = 2 * i + u
                    pe.wait_ge(xn_ready, 2 * b + 2)
                    if not first:
                        pe.wait_ge(rested, 3 * b - 3)
                        pe.wait_ge(v1_out, b - 1)
                    for j in range(2):
                        for c in range(DC):
                            last = pe.transpose(ps[:, u, c * SEQ + j * P:c * SEQ + (j + 1) * P],
                                                xn[:, u, j, c * P:(c + 1) * P], k.ident[:])
                    last.then_inc(q_turned, 1)
                    pe.wait_ge(c_in[u], 16 * i + 16)
                    pe.wait_ge(w_in, 32)
                    for m in range(DC):
                        for c in range(DC):
                            last = pe.matmul(ps[:, 2 + u, m * SEQ:(m + 1) * SEQ], wk[:, c, m, :], ctx_t[:, u, c, :],
                                             start=(c == 0), stop=(c == DC - 1))
                    last.then_inc(k1_ready, 1)
                    for j in range(2):
                        for c in range(DC):
                            last = pe.matmul(ps[:, 4 + u, j * D:(j + 1) * D], ctx_t[:, u, c, j * P:(j + 1) * P], wv[:, c, :],
                                             start=(c == 0), stop=(c == DC - 1))
                    last.then_inc(v1_ready, 1)

                batch(0, 0, True)
                batch(0, 1, True)
                with pe.Fori(1, BATCH // 2) as i:
                    for u in range(2):
                        batch(i, u, False)
        sweep(nc, used)


def attention(nc, k, name, q_stack, k_stack, values, scale, causal, out, side):
    blocks = 3 if causal else 4
    cols = blocks * P
    LAG = 2
    with ExitStack() as ctx:
        sb = lambda n, shape, dt: ctx.enter_context(nc.sbuf_tensor(f"{name}_{n}", shape, dt))
        used = []
        sem = phase_semaphores(nc, ctx, name, used)
        kst = k.kst
        qst = sb("qst", [ROWS + MROWS, 4, HSTEP, SEQ], BF16)
        v_raw = sb("v_raw", [P, 2, 2, D], F32)
        v_aug = sb("v_aug", [P, 2, 2, HEADS, VW], F32)
        probs = sb("probs", [P, HSTEP, 4 * P], F32)
        blockmax = sb("blockmax", [P, 2, HSTEP, 3], F32)
        negmax = sb("negmax", [P, 2, 2, HSTEP], F32)
        maxparts = sb("maxparts", [P, 2, 2, 2, HSTEP], BF16)
        maxrows = sb("maxrows", [2 * HSTEP, 2, SEQ], BF16)
        turned_in = sb("turned_in", [P, 2, SEQ], F32)
        recip = sb("recip", [P, 2, HSTEP], F32)
        ps = ctx.enter_context(nc.psum_tensor(f"{name}_ps", [P, 8, 512], F32))
        QK_BANKS = (0, 1, 5)
        STACK_LOADS = 16 * 2 * len(RUNS)
        outs_dq = ps[:, 6, 0:SEQ]
        max_t = ps[0:2 * HSTEP, 6, SEQ:SEQ + P].bitcast(BF16)
        outs_qd = ps[:, 7, :].rearrange("p (j n) -> p j n", j=2)

        stack_in = [sem(f"stack_in{j}") for j in range(4)]
        v_in = [sem("v_in0"), sem("v_in1")]
        max_in = [sem(f"max_in{j}") for j in range(4)]
        v_ready = sem("v_ready")
        own = sem("own")
        cut_step = sem("cut_step")
        recips = sem("recips")
        s_ready = sem("s_ready")
        s_free = sem("s_free")
        max_ready = sem("max_ready")
        max_turned = sem("max_turned")
        max_copied = sem("max_copied")
        t_ready = sem("t_ready")
        exped = sem("exped")
        pv_done = sem("pv_done")
        out_copied = sem("out_copied")
        out_turned = sem("out_turned")
        divided = sem("divided")

        LOOPED = STEPS // 4 - side.lead

        def emit(eng, step, last=LOOPED):
            for i in range(1 + side.lag):
                for u in range(4):
                    step((i, u))
            with eng.Fori(1 + side.lag, last) as i:
                for u in range(4):
                    step((i, u))
            for i in range(last, STEPS // 4 + 1):
                for u in range(4):
                    step((i, u))

        def after(st, n):
            i, u = st
            return i + (u + n) // 4, (u + n) % 4

        def number(st):
            return 4 * st[0] + st[1]

        def batch_of(st):
            return 2 * st[0] + st[1] // 2

        side.open(nc, k, ctx, sem, ps[:, 4, :])

        def scores(st):
            return not isinstance(st[0], int) or 0 <= number(st) < STEPS

        with nc.Block() as block:

            @block.sync
            def _(sp):
                half = HSTEP * SEQ

                def load(st):
                    i, u = st
                    b, part = batch_of(st), u % 2
                    if part == 0:
                        side.before_load(sp, i, u // 2)
                    for stack, tile in ((q_stack, qst), (k_stack, kst)):
                        rows = stack[bass.ds(b, 1)].rearrange("b t (d h) n -> (b t) d (h n)", d=DH)[:, :, part * half:(part + 1) * half]
                        at = 0
                        for run, n in enumerate(RUNS):
                            src = rows[run:run + 1].to_broadcast([n, DH, half]) if tile is qst else rows[0:n]
                            sp.dma_start(tile[at:at + n * DH, u].rearrange("p s n -> p (s n)"), src).then_inc(stack_in[u], 16)
                            at += n * DH
                    if part == 0:
                        wait(sp, v_ready, b - 1)
                        sp.dma_start(v_raw[:, u // 2], values[bass.ds(b, 1)].rearrange("b t p d -> p (b t) d")).then_inc(v_in[u // 2], 16)

                def step(st):
                    if scores(after(st, 1)):
                        wait(sp, t_ready, HSTEP * (number(st) - LAG))
                        load(after(st, 1))
                    before = after(st, -1)
                    if scores(before):
                        sp.wait_ge(max_copied, number(before) + 1)
                        v = before[1]
                        for part in range(MROWS):
                            sp.dma_start(qst[ROWS + part:ROWS + part + 1, v],
                                         maxrows[part * HSTEP:(part + 1) * HSTEP, v % 2, :]).then_inc(max_in[v], 16)
                    side.sync(sp, st)

                side.sync_first(sp, lambda: load((0, 0)))
                emit(sp, step, last=STEPS // 4 - 1)
                side.sync_last(sp)

            @block.gpsimd
            def _(pool):
                side.gpsimd(pool)

            @block.tensor
            def _(pe):
                def scores_qk(st, s):
                    i, u = st
                    h = number(st)
                    if s == 0:
                        pe.wait_ge(stack_in[u], STACK_LOADS * (i + 1))
                    wait(pe, s_free, HSTEP * h + (s - 2 if s > 2 else (-1, 0, -2)[s]))
                    bank = ps[:, QK_BANKS[s % 3], :]
                    for j in range(2):
                        keys = SEQ if not causal or j else P
                        at = j * (P if causal else SEQ)
                        last = pe.matmul(bank[:, at:at + keys], qst[0:ROWS, u, s, j * P:(j + 1) * P], kst[0:ROWS, u, s, 0:keys],
                                         start=True, stop=True)
                        if causal:
                            last = pe.matmul(bank[:, 2 * j * P:(2 * j + 1) * P], k.ident_b[:], k.mask_qk[:], start=False, stop=True,
                                             skip_group_check=True)
                    last.then_inc(s_ready, 1)

                def scores_kq(st, s):
                    i, u = st
                    h = number(st)
                    if s == 0:
                        pe.wait_ge(max_in[u], 32 * i + 32)
                    wait(pe, exped, HSTEP * h + s - 1)
                    bank = ps[:, 2 + s % 2, :]
                    for j in range(2):
                        first = P if causal and j else 0
                        at = j * SEQ
                        last = pe.matmul(bank[:, at:at + SEQ - first], kst[:, u, s, j * P:(j + 1) * P], qst[:, u, s, first:SEQ],
                                         start=True, stop=True)
                        if causal:
                            last = pe.matmul(bank[:, at:at + P], k.ident_b[:], k.mask_kq[:], start=False, stop=True,
                                             skip_group_check=True)
                    last.then_inc(t_ready, 1)

                def outputs(st, g):
                    i, u = st
                    h = number(st)
                    pe.wait_ge(exped, HSTEP * h + 4 * g + 4)
                    wait(pe, out_copied, 2 * h + g)
                    b_par = u // 2
                    if g == 0:
                        pe.wait_ge(max_copied, min(h + LAG, STEPS) if isinstance(h, int) else h + LAG)
                    if g == 0 and u % 2 == 0:
                        pe.wait_ge(v_ready, batch_of(st) + 1)
                    for j in range(2):
                        first = P if causal and j else 0
                        for r in range(4):
                            s = HSTEP * (u % 2) + 4 * g + r
                            last = pe.matmul(outs_dq[VW * r:VW * (r + 1), first:SEQ], v_aug[:, b_par, j, s, :],
                                             probs[:, 4 * g + r, j * SEQ:j * SEQ + SEQ - first],
                                             start=(j == 0), stop=(j == 1), skip_group_check=True)
                    last.then_inc(pv_done, 1)

                def turn_outputs(st, g):
                    h = number(st)
                    pe.wait_ge(out_copied, 2 * h + g + 1)
                    if g == 0:
                        wait(pe, divided, h)
                    for j in range(2):
                        last = pe.transpose(outs_qd[:, j, g * P:(g + 1) * P], turned_in[:, g, j * P:(j + 1) * P], k.ident[:])
                    last.then_inc(out_turned, 1)

                def turn_maxima(st):
                    h, u = number(st), st[1]
                    pe.wait_ge(max_ready, h + 1)
                    wait(pe, out_copied, 2 * h - 2)
                    for j in range(2):
                        last = pe.transpose(max_t[:, j * P:(j + 1) * P],
                                            maxparts[:, u % 2, j].rearrange("p a s -> p (a s)"), k.ident_b[:])
                    last.then_inc(max_turned, 1)

                side.tensor_first(pe)
                def step(st):
                    t = after(st, -LAG)
                    for s in range(HSTEP):
                        if scores(st):
                            scores_qk(st, s)
                        if scores(t):
                            scores_kq(t, s)
                        if s == 1 and scores(after(t, -1)):
                            turn_outputs(after(t, -1), 0)
                            outputs(after(t, -1), 1)
                        if s == 3 and scores(after(t, -1)):
                            turn_outputs(after(t, -1), 1)
                        if s == 4 and scores(after(st, -1)):
                            turn_maxima(after(st, -1))
                        if s == 7 and scores(t):
                            outputs(t, 0)
                        side.tensor(pe, st, s)

                emit(pe, step)
                side.tensor_last(pe)

            @block.vector
            def _(dve):
                side.vector_first(dve)

                def reduce(st, s):
                    h, u = number(st), st[1]
                    dve.wait_ge(s_ready, HSTEP * h + s + 1)
                    if causal:
                        nc.vector.tensor_reduce(blockmax[:, u % 2, s, :], ps[:, QK_BANKS[s % 3], 0:cols].rearrange("p (b n) -> p b n", n=P),
                                                AX.X, ALU.max, negate=True).then_inc(s_free, 1)
                    else:
                        nc.vector.tensor_reduce(negmax[:, u % 2, :, s], ps[:, QK_BANKS[s % 3], :].rearrange("p (j n) -> p j n", j=2),
                                                AX.X, ALU.max, negate=True).then_inc(s_free, 1)

                def cut(st):
                    h, u = number(st), st[1]
                    v = u % 2
                    dve.wait_ge(s_free, HSTEP * h + HSTEP)
                    if causal:
                        nc.vector.tensor_copy(negmax[:, v, 0, :], blockmax[:, v, :, 0]).then_inc(cut_step, 1)
                        nc.vector.tensor_tensor(negmax[:, v, 1, :], blockmax[:, v, :, 1], blockmax[:, v, :, 2], ALU.min).then_inc(cut_step, 1)
                        dve.wait_ge(cut_step, 3 * h + 2)
                    wait(dve, max_turned, h - 1)
                    nc.vector.tensor_copy(maxparts[:, v, :, 0, :], negmax[:, v]).then_inc(cut_step, 1)
                    per = 3 if causal else 1
                    dve.wait_ge(cut_step, per * h + per)
                    nc.vector.tensor_tensor(maxparts[:, v, :, 1, :], negmax[:, v], maxparts[:, v, :, 0, :], ALU.subtract).then_inc(max_ready, 1)

                def divide(st):
                    h, b, half = number(st), batch_of(st), st[1] % 2
                    dve.wait_ge(out_turned, 2 * h + 2)
                    o = outs_qd.rearrange("p j (s e) -> p j s e", e=VW)
                    nc.vector.reciprocal(recip[:], o[:, :, :, DH]).then_inc(recips, 1)
                    dve.wait_ge(recips, h + 1)
                    for j in range(2):
                        dst = out[:, bass.ds(2 * b + j, 1), :].rearrange("p a (c h d) -> p (a c) h d", c=DC, d=DH)
                        dst = dst[:, :, 4 * half:4 * half + 4, :].rearrange("p c h d -> p h c d")
                        last = nc.vector.tensor_tensor(dst, o[:, j, :, 0:DH].rearrange("p (h c) d -> p h c d", c=DC),
                                                       recip[:, j, :].rearrange("p (h c) -> p h c", c=DC).unsqueeze(3).to_broadcast([P, 4, DC, DH]),
                                                       ALU.mult)
                    last.then_inc(divided, 1)


                def step(st):
                    before = after(st, -LAG - 1)
                    for s in range(HSTEP):
                        if scores(st):
                            reduce(st, s)
                        if s == 5 and scores(before):
                            divide(before)
                        side.vector(dve, st, s, divided)
                    if scores(st):
                        cut(st)

                emit(dve, step)
                side.vector_last(dve, divided)

            @block.scalar
            def _(act):
                nc.scalar.memzero(v_aug[:]).then_inc(own, 1)
                act.wait_ge(own, 1)
                nc.scalar.activation(v_aug[:, :, :, :, DH], v_aug[:, :, :, :, DH], ACT.Exp).then_inc(own, 1)

                def exponential(st, s):
                    h = number(st)
                    act.wait_ge(t_ready, HSTEP * h + s + 1)
                    if s % 4 == 0:
                        wait(act, pv_done, 2 * h - 1 + s // 4)
                    nc.scalar.activation(probs[:, s, 0:cols], ps[:, 2 + s % 2, 0:cols], ACT.Exp, scale=scale).then_inc(exped, 1)

                def copy_values(st):
                    b, v = batch_of(st), st[1] // 2
                    act.wait_ge(v_in[v], 16 * st[0] + 16)
                    wait(act, pv_done, 4 * b - 4)
                    for j in range(2):
                        done = nc.scalar.copy(v_aug[:, v, j, :, 0:DH].rearrange("p (h c) d -> p c h d", c=DC),
                                              v_raw[:, v, j, :].rearrange("p (c h d) -> p c h d", c=DC, d=DH))
                    done.then_inc(v_ready, 1)

                def copy_outputs(st, g):
                    h = number(st)
                    act.wait_ge(pv_done, 2 * h + g + 1)
                    wait(act, out_turned, 2 * h + g - 1)
                    nc.scalar.copy(turned_in[:, g, :], outs_dq).then_inc(out_copied, 1)

                def copy_maxima(st):
                    h, u = number(st), st[1]
                    act.wait_ge(max_turned, h + 1)
                    old = after(st, -2)
                    if scores(old):
                        act.wait_ge(max_in[old[1]], 32 * old[0] + 32)
                    nc.scalar.copy(maxrows[:, u % 2, :], max_t).then_inc(max_copied, 1)

                act.wait_ge(own, 2)
                side.scalar_first(act)

                def step(st):
                    t = after(st, -LAG)
                    for s in range(HSTEP):
                        if scores(t):
                            exponential(t, s)
                        if s == 2 and scores(after(t, -1)):
                            copy_outputs(after(t, -1), 1)
                        if s == 3 and scores(after(st, -1)):
                            copy_maxima(after(st, -1))
                        if s == 5 and st[1] % 2 and scores(st):
                            copy_values(st)
                        if s == 7 and scores(t):
                            copy_outputs(t, 0)
                        side.scalar(act, st, s)

                emit(act, step)
                side.scalar_last(act)
        sweep(nc, used)


def pass_on(eng, sem, count, passed):
    eng.wait_ge(sem, count)
    eng.sem_inc(passed, 1)


class Route:
    lead, lag = 0, 1

    def open(self, nc, k, ctx, sem, ps):
        sb = lambda n, shape, dt: ctx.enter_context(nc.sbuf_tensor(f"rt_{n}", shape, dt))
        E = EXPERTS
        self.nc, self.k, self.ps = nc, k, ps
        self.gate = sb("gate", [P, DC, E], F32)
        self.before = sb("before", [P, P], BF16)
        self.ones = sb("ones", [P, P], BF16)
        self.list_end = sb("list_end", [P, E], F32)
        self.token = sb("token", [P, TILES], I32)
        self.tile_no = sb("tile_no", [P, 2], F32)
        self.zeros = sb("zeros", [P, LISTS], I32)
        self.stats = sb("stats", [P, 2, 6], F32)
        self.moments = sb("moments", [P, 2, 2], F32)
        self.rstd = sb("rstd", [P, 2], I32)
        self.newton = sb("newton", [P, 2], F32)
        self.rows = sb("rows", [P, 2, 2, D + E], F32)
        self.xn_t = sb("xn_t", [P, DC * SEQ], F32)
        self.logits = sb("logits", [P, 2, E], F32)
        self.others = sb("others", [P, 2, E], F32)
        self.best = sb("best", [P, 2, 8], F32)
        self.expo = sb("expo", [P, 2, E], F32)
        self.chosen = sb("chosen", [P, 2, E], F32)
        self.total = sb("total", [P, 3, 2], F32)
        self.mask = sb("mask", [P, TILES, E], BF16)
        self.earlier = sb("earlier", [P, TILES + 1, E], BF16)
        self.back = sb("back", [P, 2, E], F32)
        self.now = sb("now", [P, 2, E], F32)
        self.place = sb("place", [P, TILES, E], F32)
        self.top = sb("top", [P, 2, TOP_K], F32)
        self.idx = sb("idx", [P, 2, 2, TOP_K], I32)
        self.number = sb("number", [P, 2, 2], I32)
        self.shift_g = sb("shift_g", [P, E], F32)
        self.place_g = sb("place_g", [P, TILES, E], F32)
        self.top_g = sb("top_g", [P, TILES, TOP_K], F32)
        self.count = sb("count", [P, 6, E], F32)
        self.count_i = sb("count_i", [P, E], I32)
        self.below = sb("below", [P, 2, 3, E], F32)
        self.sums = sb("sums", [P, 2, 4], F32)
        self.distinct = sb("distinct", [P, 1], F32)
        self.row = sb("row", [P, 2], F32)
        self.row_i = sb("row_i", [P, 2], I32)
        self.ids_raw = sb("ids_raw", [P, 2, P], I32)
        self.ids_f = sb("ids_f", [P, 2, P], F32)
        self.line = sb("line", [1, 3, ETABLE], F32)
        self.line_i = sb("line_i", [1, ETABLE], I32)

        self.c_in, self.zero_set, self.zeroed = sem("constants_in"), sem("zero_set"), sem("lists_zeroed")
        self.outs_zeroed = sem("outs_zeroed")
        self.own, self.none_set = sem("route_own"), sem("none_set")
        self.xn_ready, self.xn_turned, self.xn_copied, self.logits_ready = sem("xn_ready"), sem("xn_turned"), sem("xn_copied"), sem("logits_ready")
        self.shifted, self.exped, self.counted, self.ranked = sem("shifted"), sem("route_exped"), sem("counted"), sem("ranked")
        self.ranks_read, self.weights_ready, self.slots_ready, self.staged = sem("ranks_read"), sem("weights_ready"), sem("slots_ready"), sem("staged")
        self.rows_out = [sem("rows_out0"), sem("rows_out1")]
        self.scattered, self.ids_in = [k.indirect("scattered0"), k.indirect("scattered1")], k.indirect("ids_in")
        self.tables, self.counts_ready = sem("tables_own"), sem("counts_ready")
        self.rows_ready, self.ids_f_ready, self.turned = sem("rows_ready"), sem("ids_f_ready"), sem("turned")
        self.constants = [(self.gate, "gate"), (self.before, "c_before"), (self.ones, "c_ones"), (self.list_end, "c_list_end"),
                          (self.token, "c_token"), (self.tile_no, "c_tile")]

    def position(self, st, s):
        i, u = st
        at = HSTEP * u + s - START
        if at < 0:
            batch, slot = (i - 2, 1), at + 16
        else:
            batch, slot = (i - 1, at // 16), at % 16
        if isinstance(i, int) and not 0 <= batch[0] < PAIRS:
            return None
        return *batch, slot

    def before_load(self, sp, i, u):
        pass

    def sync_first(self, sp, load):
        load()
        for tile, name in self.constants:
            sp.dma_start(tile[:], self.k.dram[name]).then_inc(self.c_in, 16)

    def zero_dram(self, sp):
        sp.wait_ge(self.zero_set, 1)
        sp.dma_start(self.k.lists.rearrange("(p n) o -> p (n o)", p=P), self.zeros[:]).then_inc(self.zeroed, 16)
        part = self.zeros[:].bitcast(F32).rearrange("p (t d) -> p t d", d=D)
        n = LISTS // D
        rest = self.k.outs[EXPECTED:ETILES].rearrange("(g t) p d -> p g t d", t=n)
        for g in range((ETILES - EXPECTED) // n):
            sp.dma_start(rest[:, g], part).then_inc(self.outs_zeroed, 16)

    def write(self, sp, i, u):
        sp.wait_ge(self.weights_ready, 2 * i + u + 1)
        sp.dma_start(self.k.xn[bass.ds(4 * i + 2 * u, 2)].rearrange("t p d -> p t d"), self.rows[:, u]).then_inc(self.rows_out[u], 16)

    def sync(self, sp, st):
        i, u = st
        if isinstance(i, int) and st == (0, 3):
            self.zero_dram(sp)
        done = {1: (i - 2, 1), 3: (i - 1, 0)}.get(u)
        if done and not (isinstance(i, int) and not 0 <= done[0] < PAIRS):
            self.write(sp, *done)

    def sync_last(self, sp):
        self.write(sp, PAIRS - 1, 1)
        for u in range(2):
            sp.wait_ge(self.rows_out[u], 16 * PAIRS)
        sp.wait_ge(self.outs_zeroed, 16 * ((ETILES - EXPECTED) // (LISTS // D)))

    def gpsimd(self, pool):
        nc, k = self.nc, self.k
        nc.gpsimd.memset(self.zeros[:], 0).then_inc(self.zero_set, 1)
        pool.wait_ge(self.c_in, 16 * len(self.constants))
        pool.wait_ge(self.zeroed, 16)

        def scatter(i, u):
            m = 2 * i + u
            for j in range(2):
                nc.gpsimd.tensor_copy(self.number[:, u, j:j + 1], self.token[:, bass.ds(2 * m + j, 1)]).then_inc(self.staged, 1)
            pass_on(pool, self.staged, 2 * m + 2, k.passed)
            pass_on(pool, self.slots_ready, m + 1, k.passed)
            for j in range(2):
                for s in range(TOP_K):
                    nc.gpsimd.indirect_dma_start(k.lists, bass.IndirectOffsetOnAxis(ap=self.idx[:, u, j, s:s + 1], axis=0),
                                                 self.number[:, u, j:j + 1], None).then_inc(self.scattered[u], 16)

        for u in range(2):
            scatter(0, u)
        with pool.Fori(1, PAIRS) as i:
            for u in range(2):
                pass_on(pool, self.scattered[u], 16 * 2 * TOP_K * i, k.passed)
                scatter(i, u)
        for u in range(2):
            pool.wait_ge(self.scattered[u], 16 * 2 * TOP_K * PAIRS)
        pool.wait_ge(self.rows_ready, 2)
        for a in range(2):
            nc.gpsimd.indirect_dma_start(self.ids_raw[:, a, :], None, k.lists.rearrange("(r n) o -> r (n o)", n=P),
                                         bass.IndirectOffsetOnAxis(ap=self.row_i[:, a:a + 1], axis=0)).then_inc(self.ids_in, 16)
        pool.wait_ge(self.ids_in, 32)

    def pair(self, i, u):
        return bass.ds(4 * i + 2 * u, 2)

    def tile(self, i, u, j):
        return self.k.x[:, bass.ds(4 * i + 2 * u + j, 1), :].rearrange("p a d -> p (a d)")

    def logits_ps(self):
        return self.ps[:, 0:2 * EXPERTS].rearrange("p (j e) -> p j e", j=2)

    def ranks_ps(self):
        return self.ps[:, 2 * EXPERTS:4 * EXPERTS].rearrange("p (j e) -> p j e", j=2)

    def vector(self, dve, st, s, divided):
        if not self.position(st, s):
            return
        i, u, slot = self.position(st, s)
        nc, k, own = self.nc, self.k, self.own
        t, m = 4 * i + 2 * u, 2 * i + u
        x2, mask2 = k.x[:, self.pair(i, u), :], self.mask[:, self.pair(i, u), :]
        root = lambda part: inverse_root(nc, own, 5, self.rstd[:], self.moments[:, :, 1], self.newton[:], part)
        later = not isinstance(i, int) or i > 0
        if slot == 0:
            dve.sem_clear(own)
            dve.wait_ge(divided, t + 2)
            nc.vector.tensor_tensor(x2, x2, k.ao[:, self.pair(i, u), :], ALU.add).then_inc(own, 1)
        elif slot == 1:
            dve.wait_ge(own, 1)
            for j in range(2):
                nc.vector.bn_stats(self.stats[:, j, :], self.tile(i, u, j)).then_inc(own, 1)
        elif slot == 2:
            for j in range(2):
                dve.wait_ge(own, 2 + j)
                nc.vector.bn_aggr(self.moments[:, j, :], self.stats[:, j, :]).then_inc(own, 1)
            dve.wait_ge(own, 5)
            root(0)
            root(1)
        elif slot == 3:
            root(2)
            root(3)
            dve.wait_ge(own, 5 + 4 * NEWTON_STEPS)
            if later:
                dve.wait_ge(self.rows_out[u], 16 * i)
            for j in range(2):
                nc.vector.tensor_scalar(self.rows[:, u, j, 0:D], self.tile(i, u, j), self.moments[:, j, 0:1],
                                        self.rstd[:, j:j + 1].bitcast(F32), ALU.subtract, ALU.mult).then_inc(self.xn_ready, 1)
        elif slot == 7:
            dve.wait_ge(self.logits_ready, m + 1)
            nc.vector.tensor_copy(self.logits[:], self.logits_ps()).then_inc(own, 1)
            dve.wait_ge(own, 18)
            for j in range(2):
                nc.vector.max(self.best[:, j, :], self.logits[:, j, :]).then_inc(own, 1)
        elif slot == 8:
            for j in range(2):
                dve.wait_ge(own, 19 + j)
                nc.vector.match_replace(self.others[:, j, :], self.best[:, j, :], self.logits[:, j, :], -3.0e38).then_inc(own, 1)
            dve.wait_ge(own, 22)
            nc.vector.tensor_tensor(mask2, self.others[:], self.logits[:], ALU.not_equal).then_inc(own, 1)
            nc.vector.tensor_tensor(self.expo[:], self.logits[:], self.best[:, :, 0:1].to_broadcast([P, 2, EXPERTS]),
                                    ALU.subtract).then_inc(self.shifted, 1)
        elif slot == 9:
            dve.wait_ge(own, 23)
            nc.vector.tensor_tensor(self.earlier[:, bass.ds(t + 1, 1), :], self.earlier[:, bass.ds(t, 1), :],
                                    self.mask[:, bass.ds(t, 1), :], ALU.add).then_inc(own, 1)
            dve.wait_ge(own, 24)
            nc.vector.tensor_tensor(self.earlier[:, bass.ds(t + 2, 1), :], self.earlier[:, bass.ds(t + 1, 1), :],
                                    self.mask[:, bass.ds(t + 1, 1), :], ALU.add).then_inc(self.counted, 1)
        elif slot == 12:
            dve.wait_ge(self.exped, m + 1)
            nc.vector.tensor_tensor(self.chosen[:], self.expo[:], mask2, ALU.mult).then_inc(own, 1)
            nc.vector.tensor_reduce(self.total[:, 0, :], self.expo[:], AX.X, ALU.add).then_inc(own, 1)
            dve.wait_ge(self.c_in, 16 * len(self.constants))
            dve.wait_ge(self.ranked, m + 1)
            nc.vector.tensor_tensor(self.back[:], self.list_end[:].unsqueeze(1).to_broadcast([P, 2, EXPERTS]), self.ranks_ps(),
                                    ALU.subtract).then_inc(self.ranks_read, 1)
        elif slot == 13:
            dve.wait_ge(own, 26)
            nc.vector.tensor_reduce(self.total[:, 1, :], self.chosen[:], AX.X, ALU.add).then_inc(own, 1)
            dve.wait_ge(self.ranks_read, m + 1)
            nc.vector.tensor_tensor(self.now[:], self.back[:], mask2, ALU.mult).then_inc(own, 1)
        elif slot == 14:
            dve.wait_ge(own, 28)
            nc.vector.scalar_tensor_tensor(self.total[:, 2, :], self.total[:, 0, :], 1e-20, self.total[:, 1, :], ALU.mult, ALU.add).then_inc(own, 1)
            for j in range(2):
                nc.vector.max(self.top[:, j, :], self.now[:, j, :]).then_inc(own, 1)
            dve.wait_ge(own, 31)
            if later:
                dve.wait_ge(self.scattered[u], 16 * 2 * TOP_K * i)
            nc.vector.tensor_scalar(self.idx[:, u], self.top[:], -1.0, float(EXPERTS * TOK), ALU.mult, ALU.add).then_inc(self.slots_ready, 1)
        elif slot == 15:
            nc.vector.reciprocal(self.total[:, 2, :], self.total[:, 2, :]).then_inc(own, 1)
            nc.vector.tensor_copy(self.place[:, self.pair(i, u), :], self.now[:])
            dve.wait_ge(own, 32)
            nc.vector.tensor_tensor(self.rows[:, u, :, D:D + EXPERTS], self.chosen[:],
                                    self.total[:, 2, :].unsqueeze(2).to_broadcast([P, 2, EXPERTS]), ALU.mult).then_inc(self.weights_ready, 1)

    def vector_first(self, dve):
        self.nc.vector.memset(self.earlier[:, 0, :], 0.0).then_inc(self.none_set, 1)
        dve.wait_ge(self.none_set, 1)

    def vector_last(self, dve, divided):
        for s in range(START):
            self.vector(dve, (ROUNDS, 0), s, divided)
        self.make_tables(dve)

    def make_tables(self, dve):
        nc, k, E = self.nc, self.k, EXPERTS
        own, steps = self.tables, [0]
        count, below, sums, distinct, line = self.count, self.below, self.sums, self.distinct, self.line
        GEND = float((ETILES + 1) * P)

        def then(ins):
            ins.then_inc(own, 1)
            steps[0] += 1
            dve.wait_ge(own, steps[0])

        tiles, ends, starts, one, some = (count[:, n, :] for n in range(5))
        dve.wait_ge(self.counts_ready, 1)
        then(nc.vector.tensor_scalar(self.count_i[:], self.ps[:, 4 * E:5 * E], float(P - 1), None, ALU.add))
        then(nc.vector.tensor_scalar(self.count_i[:], self.count_i[:], 7, None, ALU.logical_shift_right))
        then(nc.vector.tensor_copy(tiles, self.count_i[:]))
        then(nc.vector.memset(one, 1.0))
        then(nc.vector.tensor_tensor_scan(ends, one, tiles, 0.0, ALU.mult, ALU.add))
        then(nc.vector.tensor_tensor(starts, ends, tiles, ALU.subtract))
        then(nc.vector.tensor_copy(k.tiles_used[:], ends[0:1, E - 1:E]))
        then(nc.vector.tensor_scalar(some, tiles, 0.5, None, ALU.is_gt))
        then(nc.vector.tensor_reduce(distinct[:], some, AX.X, ALU.add))
        then(nc.vector.tensor_scalar(distinct[:], distinct[:], -1.0, None, ALU.add))
        for a in range(2):
            then(nc.vector.tensor_scalar(below[:, a, 0, :], ends, self.tile_no[:, a:a + 1], None, ALU.is_le))
            then(nc.vector.tensor_tensor(below[:, a, 1, :], below[:, a, 0, :], some, ALU.mult))
            then(nc.vector.tensor_tensor(below[:, a, 2, :], below[:, a, 0, :], tiles, ALU.mult))
            then(nc.vector.tensor_reduce(sums[:, a, 0:3], below[:, a], AX.X, ALU.add))
            then(nc.vector.tensor_scalar(sums[:, a, 0:1], sums[:, a, 0:1], float(E - 1), None, ALU.min))
            then(nc.vector.tensor_tensor(sums[:, a, 1:2], sums[:, a, 1:2], distinct[:], ALU.min))
            then(nc.vector.tensor_tensor(sums[:, a, 3:4], self.tile_no[:, a:a + 1], sums[:, a, 2:3], ALU.subtract))
            then(nc.vector.tensor_scalar(sums[:, a, 3:4], sums[:, a, 3:4], float(TILES - 1), None, ALU.min))
            then(nc.vector.tensor_scalar(self.row[:, a:a + 1], sums[:, a, 0:1], float(TILES), None, ALU.mult))
            nc.vector.tensor_tensor(self.row_i[:, a:a + 1], self.row[:, a:a + 1], sums[:, a, 3:4], ALU.add).then_inc(self.rows_ready, 1)

        then(nc.vector.tensor_scalar(self.shift_g[:], starts, -float(P), GEND, ALU.mult, ALU.add))
        then(nc.vector.tensor_tensor(self.shift_g[:], self.shift_g[:], self.list_end[:], ALU.subtract))
        then(nc.vector.tensor_tensor(self.place_g[:], self.mask[:], self.shift_g[:].unsqueeze(1).to_broadcast([P, TILES, E]), ALU.mult))
        then(nc.vector.tensor_tensor(self.place_g[:], self.place_g[:], self.place[:], ALU.add))
        for t in range(TILES):
            last = nc.vector.max(self.top_g[:, t, :], self.place_g[:, t, :])
        then(last)
        then(nc.vector.tensor_scalar(k.slot[:], self.top_g[:], -1.0, GEND, ALU.mult, ALU.add))

        dve.wait_ge(self.turned, 1)
        then(nc.vector.tensor_copy(line[:, 0:2, :].rearrange("p q n -> p (q n)"), self.ps[0:1, :]))
        then(nc.vector.memset(line[:, 2, 0:1], 1.0))
        then(nc.vector.tensor_tensor(line[:, 2, 1:ETABLE], line[:, 1, 1:ETABLE], line[:, 1, 0:ETABLE - 1], ALU.not_equal))
        then(nc.vector.tensor_copy(k.table[:, 0, :], line[:, 0, :]))
        then(nc.vector.tensor_copy(self.line_i[:], line[:, 1, :]))
        then(nc.vector.tensor_scalar(k.table[:, 1, :], self.line_i[:], WRING - 1, None, ALU.bitwise_and))
        then(nc.vector.tensor_copy(k.table[:, 2, :], line[:, 2, :]))
        dve.wait_ge(self.ids_in, 32)
        nc.vector.tensor_copy(self.ids_f[:], self.ids_raw[:]).then_inc(self.ids_f_ready, 1)
        dve.wait_ge(self.turned, 2)
        then(nc.vector.tensor_copy(k.ids[:], self.ps[:, 0:ETABLE]))

    def tensor_first(self, pe):
        pass

    def tensor(self, pe, st, s):
        if not self.position(st, s):
            return
        i, u, slot = self.position(st, s)
        m = 2 * i + u
        if slot == 6:
            pe.wait_ge(self.xn_ready, 2 * m + 2)
            wait(pe, self.ranks_read, m)
            for j in range(2):
                for c in range(DC):
                    last = pe.transpose(self.ps[:, (DC * j + c) * P:(DC * j + c + 1) * P], self.rows[:, u, j, c * P:(c + 1) * P], self.k.ident[:])
            last.then_inc(self.xn_turned, 1)
        elif slot == 7:
            pe.wait_ge(self.c_in, 16 * len(self.constants))
            pe.wait_ge(self.xn_copied, m + 1)
            for j in range(2):
                for c in range(DC):
                    last = pe.matmul(self.ps[:, j * EXPERTS:(j + 1) * EXPERTS], self.xn_t[:, (DC * j + c) * P:(DC * j + c + 1) * P],
                                     self.gate[:, c, :], start=(c == 0), stop=(c == DC - 1))
            last.then_inc(self.logits_ready, 1)
        elif slot == 12:
            pe.wait_ge(self.counted, m + 1)
            pe.matmul(self.ranks_ps(), self.before[:], self.mask[:, self.pair(i, u), :], start=True, stop=False)
            pe.matmul(self.ranks_ps(), self.ones[:], self.earlier[:, self.pair(i, u), :], start=False, stop=True).then_inc(self.ranked, 1)

    def tensor_last(self, pe):
        for s in range(START):
            self.tensor(pe, (ROUNDS, 0), s)
        pe.wait_ge(self.ranks_read, BATCH)
        pe.matmul(self.ps[:, 4 * EXPERTS:5 * EXPERTS], self.ones[:], self.earlier[:, TILES, :], start=True, stop=True).then_inc(self.counts_ready, 1)
        pe.wait_ge(self.rows_ready, 2)
        for a in range(2):
            for q in range(2):
                last = pe.transpose(self.ps[0:1, (2 * q + a) * P:(2 * q + a + 1) * P], self.sums[:, a, q:q + 1], self.k.ident[:])
        last.then_inc(self.turned, 1)
        pe.wait_ge(self.ids_f_ready, 1)
        for a in range(2):
            last = pe.transpose(self.ps[:, a * P:(a + 1) * P], self.ids_f[:, a, :], self.k.ident[:])
        last.then_inc(self.turned, 1)

    def scalar_first(self, act):
        pass

    def scalar(self, act, st, s):
        if not self.position(st, s):
            return
        i, u, slot = self.position(st, s)
        if slot == 6:
            act.wait_ge(self.xn_turned, 2 * i + u + 1)
            self.nc.scalar.copy(self.xn_t[:], self.ps).then_inc(self.xn_copied, 1)
        elif slot == 11:
            act.wait_ge(self.shifted, 2 * i + u + 1)
            self.nc.scalar.activation(self.expo[:], self.expo[:], ACT.Exp).then_inc(self.exped, 1)

    def scalar_last(self, act):
        for s in range(START):
            self.scalar(act, (ROUNDS, 0), s)


def experts(nc, k, begin, end):
    tag = f"ex{begin}"
    with ExitStack() as ctx:
        sb = lambda n, shape, dt: ctx.enter_context(nc.sbuf_tensor(f"{tag}_{n}", shape, dt))
        used = []
        sem = phase_semaphores(nc, ctx, tag, used)
        R = 8
        w_gu = sb("w_gu", [P, WRING, DC, 2 * FF], F32)
        w_down = sb("w_down", [FH, WRING, 2, D], F32)
        idx = sb("idx", [P, R], I32)
        rows = sb("rows", [P, R, D + EXPERTS], F32)
        rows_t = sb("rows_t", [P, 2, DC * P], F32)
        act_g = sb("act_g", [P, 2, FF], F32)
        hidden = sb("hidden", [P, 2, FF], F32)
        hidden_t = sb("hidden_t", [FH, 2, 2 * P], F32)
        result = sb("result", [P, R, D], F32)
        ps = ctx.enter_context(nc.psum_tensor(f"{tag}_ps", [P, 8, 512], F32))
        w_in = [sem(f"w_in{j}") for j in range(R)]
        staged = sem("staged")
        rows_in = [k.indirect(f"{tag}_rows_in{j}") for j in range(R)]
        rows_turned, rows_copied = sem("rows_turned"), sem("rows_copied")
        gu_ready, silu_ready, hidden_ready = sem("gu_ready"), sem("silu_ready"), sem("hidden_ready")
        hidden_turned, hidden_copied, down_ready = sem("hidden_turned"), sem("hidden_copied"), sem("down_ready")
        result_ready = sem("result_ready")
        out_done = [sem(f"out_done{j}") for j in range(R)]
        ROUNDS = (end - begin) // R
        table = k.table[:, :, begin:end]
        ids, outs = k.ids[:, begin:end], k.outs[begin:end]

        def needed(eng):
            if begin == 0:
                return nullcontext()
            return eng.If(eng.value_load(k.tiles_used[0:1, 0:1], min_val=1, max_val=ETILES) > begin)

        with nc.Block() as block:

            def rounds(eng, step, last=ROUNDS):
                for j in range(R):
                    step(0, j)
                with eng.Fori(1, last) as i:
                    for j in range(R):
                        step(i, j)

            @block.sync
            def _(sp):
                def step(i, j):
                    t = R * i + j
                    expert = sp.value_load(table[0:1, 0, bass.ds(t, 1)], min_val=0, max_val=EXPERTS - 1)
                    ring = sp.value_load(table[0:1, 1, bass.ds(t, 1)], min_val=0, max_val=WRING - 1)
                    other = sp.value_load(table[0:1, 2, bass.ds(t, 1)], min_val=0, max_val=1)
                    fresh = None if isinstance(i, int) and t == 0 else other > 0
                    wait(sp, down_ready, t - WRING + 1)
                    sp.dma_start(w_gu[:, bass.ds(ring, 1)].rearrange("p a c n -> p (a c n)"),
                                 k.dram["w_gu"][bass.ds(expert, 1)].rearrange("e p c n -> (e p) (c n)"), cond=fresh).then_inc(w_in[j], 16)
                    sp.dma_start(w_down[:, bass.ds(ring, 1)].rearrange("p a c n -> p (a c n)"),
                                 k.dram["w_down"][bass.ds(expert, 1)].rearrange("e p c n -> (e p) (c n)"), cond=fresh).then_inc(w_in[j], 16)

                with needed(sp):
                    rounds(sp, step)

            @block.gpsimd
            def _(pool):
                def step(i, j):
                    t = R * i + j
                    if not isinstance(i, int):
                        pass_on(pool, result_ready, t - R + 1, k.passed)
                    nc.gpsimd.tensor_copy(idx[:, j:j + 1], ids[:, bass.ds(t, 1)]).then_inc(staged, 1)
                    pass_on(pool, staged, t + 1, k.passed)
                    nc.gpsimd.indirect_dma_start(rows[:, j, :], None, k.xn.rearrange("t p d -> (t p) d"),
                                                 bass.IndirectOffsetOnAxis(ap=idx[:, j:j + 1], axis=0)).then_inc(rows_in[j], 16)

                with needed(pool):
                    rounds(pool, step)

            @block.tensor
            def _(pe):
                def turn_rows(i, j):
                    t = R * i + j
                    pe.wait_ge(rows_in[j], 16 * i + 16)
                    wait(pe, rows_copied, t - 1)
                    for c in range(DC):
                        last = pe.transpose(ps[:, j % 2, c * P:(c + 1) * P], rows[:, j, c * P:(c + 1) * P], k.ident[:])
                    last.then_inc(rows_turned, 1)

                def gate_up(i, j, ring, c):
                    t = R * i + j
                    if c == 0:
                        pe.wait_ge(w_in[j], 32 * i + 32)
                        pe.wait_ge(rows_copied, t + 1)
                        wait(pe, hidden_ready, t - 1)
                    last = pe.matmul(ps[:, 2 + j % 2, 0:2 * FF], rows_t[:, j % 2, c * P:(c + 1) * P],
                                     w_gu[:, bass.ds(ring, 1), c, :].rearrange("p a n -> p (a n)"), start=(c == 0), stop=(c == DC - 1))
                    if c == DC - 1:
                        last.then_inc(gu_ready, 1)

                def turn_hidden(i, j):
                    t = R * i + j
                    pe.wait_ge(hidden_ready, t + 1)
                    wait(pe, hidden_copied, t - 1)
                    for c in range(2):
                        last = pe.transpose(ps[0:FH, 4 + j % 2, c * P:(c + 1) * P], hidden[:, j % 2, c * FH:(c + 1) * FH], k.ident[:])
                    last.then_inc(hidden_turned, 1)

                def down(i, j, ring):
                    t = R * i + j
                    pe.wait_ge(hidden_copied, t + 1)
                    wait(pe, result_ready, t - 1)
                    for c in range(2):
                        last = pe.matmul(ps[:, 6 + j % 2, 0:D], hidden_t[:, j % 2, c * P:(c + 1) * P],
                                         w_down[:, bass.ds(ring, 1), c, :].rearrange("p a n -> p (a n)"), start=(c == 0), stop=(c == 1))
                    last.then_inc(down_ready, 1)

                def buffer_of(i, j):
                    return pe.value_load(table[0:1, 1, bass.ds(R * i + j, 1)], min_val=0, max_val=WRING - 1)

                def after(i, j, n):
                    return (i, j + n) if j + n < R else (i + 1, j + n - R)

                def step(i, j, rings, first=False, left=R):
                    before = (i, j - 1) if j else (i - 1, R - 1)
                    gate_up(i, j, rings[1], 0)
                    if not first:
                        turn_hidden(*before)
                    gate_up(i, j, rings[1], 1)
                    following = buffer_of(*after(i, j, 1)) if left > 1 and j < R - 1 else None
                    if left > 2:
                        turn_rows(*after(i, j, 2))
                    if not first:
                        down(*before, rings[0])
                    return rings[1], following

                def steps(i, last=False):
                    rings = (None, buffer_of(i, 0))
                    if not isinstance(i, int) or i:
                        rings = (buffer_of(i - 1, R - 1), rings[1])
                    for j in range(R):
                        rings = step(i, j, rings, first=(isinstance(i, int) and i == j == 0), left=R - j if last else R)

                with needed(pe):
                    turn_rows(0, 0)
                    turn_rows(0, 1)
                    steps(0)
                    with pe.Fori(1, ROUNDS - 1) as i:
                        steps(i)
                    steps(ROUNDS - 1, last=True)
                    turn_hidden(ROUNDS - 1, R - 1)
                    down(ROUNDS - 1, R - 1, buffer_of(ROUNDS - 1, R - 1))

            @block.scalar
            def _(act):
                def copy_rows(i, j):
                    t = R * i + j
                    act.wait_ge(rows_turned, t + 1)
                    wait(act, gu_ready, t - 1)
                    nc.scalar.copy(rows_t[:, j % 2], ps[:, j % 2, 0:DC * P]).then_inc(rows_copied, 1)

                def silu(i, j):
                    t = R * i + j
                    act.wait_ge(gu_ready, t + 1)
                    wait(act, hidden_ready, t - 1)
                    nc.scalar.activation(act_g[:, j % 2], ps[:, 2 + j % 2, 0:FF], ACT.Silu).then_inc(silu_ready, 1)

                def store(i, j):
                    t = R * i + j
                    act.wait_ge(result_ready, t + 1)
                    act.dma_start(outs[bass.ds(t, 1)].rearrange("t p d -> (t p) d"), result[:, j]).then_inc(out_done[j], 16)

                def step(i, j, first=0, left=R):
                    silu(i, j)
                    if left > 2:
                        copy_rows(*((i, j + 2) if j < R - 2 else (i + 1, j + 2 - R)))
                    if first < 1:
                        store(*((i, j - 2) if j > 1 else (i - 1, R + j - 2)))

                with needed(act):
                    copy_rows(0, 0)
                    copy_rows(0, 1)
                    for j in range(R):
                        step(0, j, first=2 - j)
                    with act.Fori(1, ROUNDS - 1) as i:
                        for j in range(R):
                            step(i, j)
                    for j in range(R):
                        step(ROUNDS - 1, j, left=R - j)
                    store(ROUNDS - 1, R - 2)
                    store(ROUNDS - 1, R - 1)
                    for j in range(R):
                        act.wait_ge(out_done[j], 16 * ROUNDS)

            @block.vector
            def _(dve):
                def gated(i, j):
                    t = R * i + j
                    dve.wait_ge(silu_ready, t + 1)
                    wait(dve, hidden_turned, t - 1)
                    nc.vector.tensor_tensor(hidden[:, j % 2], act_g[:, j % 2], ps[:, 2 + j % 2, FF:2 * FF], ALU.mult).then_inc(hidden_ready, 1)

                def copy_hidden(i, j):
                    t = R * i + j
                    dve.wait_ge(hidden_turned, t + 1)
                    wait(dve, down_ready, t - 1)
                    nc.vector.tensor_copy(hidden_t[:, j % 2], ps[0:FH, 4 + j % 2, 0:2 * P]).then_inc(hidden_copied, 1)

                def weigh(i, j):
                    t = R * i + j
                    expert = dve.value_load(table[0:1, 0, bass.ds(t, 1)], min_val=0, max_val=EXPERTS - 1)
                    dve.wait_ge(down_ready, t + 1)
                    if not isinstance(i, int) or i:
                        dve.wait_ge(out_done[j], 16 * i)
                    nc.vector.tensor_scalar(result[:, j], ps[:, 6 + j % 2, 0:D], rows[:, j, bass.ds(expert + D, 1)], None, ALU.mult).then_inc(result_ready, 1)

                def step(i, j, first=False):
                    before = (i, j - 1) if j else (i - 1, R - 1)
                    if not first:
                        copy_hidden(*before)
                    gated(i, j)
                    if not first:
                        weigh(*before)

                with needed(dve):
                    for j in range(R):
                        step(0, j, first=(j == 0))
                    with dve.Fori(1, ROUNDS) as i:
                        for j in range(R):
                            step(i, j)
                    copy_hidden(ROUNDS - 1, R - 1)
                    weigh(ROUNDS - 1, R - 1)
        sweep(nc, used)


ADDS = 7


class Combine:
    lead, lag = 1, 0

    def open(self, nc, k, ctx, sem, ps):
        sb = lambda n, shape, dt: ctx.enter_context(nc.sbuf_tensor(f"cb_{n}", shape, dt))
        self.nc, self.k = nc, k
        self.wq = sb("wq", [P, DC, DC, P], F32)
        self.idx = sb("idx", [P, 2, 2, TOP_K], I32)
        self.gathered = sb("gathered", [P, 2, 2, TOP_K, D], F32)
        self.moe = sb("moe", [P, 2, D], F32)
        self.stats = sb("stats", [P, 2, 6], F32)
        self.moments = sb("moments", [P, 2, 2], F32)
        self.rstd = sb("rstd", [P, 2], I32)
        self.newton = sb("newton", [P, 2], F32)
        self.xn = sb("xn", [P, 2, D], F32)
        self.xn_t = sb("xn_t", [P, DC, SEQ], F32)
        self.rest = sb("rest", [P, DC * SEQ], F32)
        self.parts = sb("parts", [P, 2, 3, DC * SEQ], BF16)
        self.ps = ps
        self.w_in, self.staged = sem("wq_in"), sem("idx_staged")
        self.rows_in = [k.indirect("cb_rows_in0"), k.indirect("cb_rows_in1")]
        self.own, self.summed = sem("combine_own"), sem("summed")
        self.xn_ready, self.xn_turned, self.xn_copied, self.q_ready = sem("xn_ready"), sem("xn_turned"), sem("xn_copied"), sem("q_ready")
        self.high, self.rested, self.middle, self.split = sem("high"), sem("rested"), sem("middle"), sem("split")
        self.written = [sem("written0"), sem("written1")]

    def write(self, sp, i, u):
        sp.wait_ge(self.split, 2 * i + u + 1)
        stack = self.k.q1_stack[bass.ds(2 * i + u, 1)].rearrange("b t p n -> p (b t) n")
        sp.dma_start(stack, self.parts[:, u]).then_inc(self.written[u], 16)

    def sync_first(self, sp, load):
        sp.dma_start(self.wq[:], self.k.dram["wq"]).then_inc(self.w_in, 16)
        self.write(sp, 0, 0)
        load()
        self.write(sp, 0, 1)

    def sync(self, sp, st):
        e = self.ending(st)
        if e:
            self.write(sp, *e)

    def sync_last(self, sp):
        for u in range(2):
            sp.wait_ge(self.written[u], 16 * PAIRS)

    def before_load(self, sp, i, u):
        sp.wait_ge(self.written[u], 16 * (i + 1))

    def gpsimd(self, pool):
        nc, k = self.nc, self.k

        def gather(i, u):
            b = 2 * i + u
            for j in range(2):
                nc.gpsimd.tensor_copy(self.idx[:, u, j, :], k.slot[:, bass.ds(2 * b + j, 1), :].rearrange("p a s -> p (a s)")).then_inc(self.staged, 1)
            pass_on(pool, self.staged, 2 * b + 2, k.passed)
            for j in range(2):
                for s in range(TOP_K):
                    nc.gpsimd.indirect_dma_start(self.gathered[:, u, j, s, :], None, k.outs.rearrange("t p d -> (t p) d"),
                                                 bass.IndirectOffsetOnAxis(ap=self.idx[:, u, j, s:s + 1], axis=0)).then_inc(self.rows_in[u], 16)

        for u in range(2):
            gather(0, u)
        with pool.Fori(1, PAIRS) as i:
            for u in range(2):
                pass_on(pool, self.summed, ADDS * (2 * i + u - 1), k.passed)
                gather(i, u)

    def add(self, dve, i, u, piece):
        before = ADDS * (2 * i + u)
        rows = self.gathered[:, u]
        if piece == 0:
            dve.wait_ge(self.rows_in[u], 16 * 2 * TOP_K * (i + 1))
        if piece == ADDS - 1:
            dve.wait_ge(self.summed, before + piece)
            to, what = rows[:, :, 0, :], rows[:, :, 1, :]
        elif piece % 3 == 2:
            dve.wait_ge(self.summed, before + piece)
            to, what = rows[:, piece // 3, 0:2, :], rows[:, piece // 3, 2:4, :]
        else:
            at = 2 * (piece % 3)
            to, what = rows[:, piece // 3, at:at + 2, :], rows[:, piece // 3, at + 4:at + 6, :]
        if piece == ADDS - 1:
            self.nc.vector.tensor_tensor(self.moe[:], to, what, ALU.add).then_inc(self.summed, 1)
        else:
            self.nc.vector.tensor_tensor(to, to, what, ALU.add).then_inc(self.summed, 1)

    def tile(self, i, u, j):
        return self.k.x[:, bass.ds(4 * i + 2 * u + j, 1), :].rearrange("p a d -> p (a d)")

    def add_to_x(self, dve, i, u):
        dve.sem_clear(self.own)
        dve.wait_ge(self.summed, ADDS * (2 * i + u + 1))
        x2 = self.k.x[:, bass.ds(4 * i + 2 * u, 2), :]
        self.nc.vector.tensor_tensor(x2, x2, self.moe[:], ALU.add).then_inc(self.own, 1)

    def statistics(self, dve, i, u):
        dve.wait_ge(self.own, 1)
        for j in range(2):
            self.nc.vector.bn_stats(self.stats[:, j, :], self.tile(i, u, j)).then_inc(self.own, 1)
        for j in range(2):
            dve.wait_ge(self.own, 2 + j)
            self.nc.vector.bn_aggr(self.moments[:, j, :], self.stats[:, j, :]).then_inc(self.own, 1)

    def root(self, dve, part):
        if part == 0:
            dve.wait_ge(self.own, 5)
        inverse_root(self.nc, self.own, 5, self.rstd[:], self.moments[:, :, 1], self.newton[:], part)

    def normalise(self, dve, i, u):
        dve.wait_ge(self.own, 5 + 4 * NEWTON_STEPS)
        wait(dve, self.xn_turned, 2 * i + u)
        for j in range(2):
            self.nc.vector.tensor_scalar(self.xn[:, j, :], self.tile(i, u, j), self.moments[:, j, 0:1], self.rstd[:, j:j + 1].bitcast(F32),
                                         ALU.subtract, ALU.mult).then_inc(self.xn_ready, 1)

    def take_rest(self, dve, i, u):
        dve.wait_ge(self.high, 2 * i + u + 1)
        self.nc.vector.tensor_tensor(self.rest[:], self.ps, self.parts[:, u, 0, :], ALU.subtract).then_inc(self.rested, 1)

    def take_low(self, dve, i, u):
        dve.wait_ge(self.middle, 2 * i + u + 1)
        self.nc.vector.tensor_tensor(self.parts[:, u, 2, :], self.rest[:], self.parts[:, u, 1, :], ALU.subtract).then_inc(self.split, 1)

    def vector_first(self, dve):
        for u in range(2):
            for piece in range(ADDS):
                self.add(dve, 0, u, piece)
            self.add_to_x(dve, 0, u)
            self.statistics(dve, 0, u)
            for part in range(4):
                self.root(dve, part)
            self.normalise(dve, 0, u)
            self.take_rest(dve, 0, u)
            self.take_low(dve, 0, u)

    def started(self, st):
        i, u = st
        if not isinstance(i, int) or 0 <= i < PAIRS - 1:
            return i + 1, u // 2

    def ending(self, st):
        i, u = st
        if u == 0 and (not isinstance(i, int) or 1 <= i < PAIRS):
            return i, 1
        if u == 2:
            return self.started((i, 0))

    def vector(self, dve, st, s, divided):
        b, e, even = self.started(st), self.ending(st), st[1] % 2 == 0
        if b and even and s < ADDS:
            self.add(dve, *b, s)
        if b and even and s == 7:
            self.add_to_x(dve, *b)
        if e and s == 5:
            self.take_rest(dve, *e)
        if e and s == 6:
            self.take_low(dve, *e)
        if b and not even:
            if s == 0:
                self.statistics(dve, *b)
            elif s < 5:
                self.root(dve, s - 1)
            elif s == 5:
                self.normalise(dve, *b)

    def vector_last(self, dve, divided):
        pass

    def turn(self, pe, i, u):
        pe.wait_ge(self.xn_ready, 4 * i + 2 * u + 2)
        wait(pe, self.rested, 2 * i + u)
        for j in range(2):
            for c in range(DC):
                last = pe.transpose(self.ps[:, c * SEQ + j * P:c * SEQ + (j + 1) * P], self.xn[:, j, c * P:(c + 1) * P], self.k.ident[:])
        last.then_inc(self.xn_turned, 1)

    def project(self, pe, i, u, m):
        if m == 0:
            pe.wait_ge(self.xn_copied, 2 * i + u + 1)
        for c in range(DC):
            last = pe.matmul(self.ps[:, m * SEQ:(m + 1) * SEQ], self.wq[:, c, m, :], self.xn_t[:, c, :],
                             start=(c == 0), stop=(c == DC - 1))
        last.then_inc(self.q_ready, 1)

    def tensor_first(self, pe):
        pe.wait_ge(self.w_in, 16)
        for u in range(2):
            self.turn(pe, 0, u)
            self.project(pe, 0, u, 0)
            self.project(pe, 0, u, 1)

    def tensor(self, pe, st, s):
        e = self.ending(st)
        if e and s == 0:
            self.turn(pe, *e)
        if e and s in (2, 3):
            self.project(pe, *e, s - 2)

    def tensor_last(self, pe):
        pass

    def copy_turned(self, act, i, u):
        act.wait_ge(self.xn_turned, 2 * i + u + 1)
        self.nc.scalar.copy(self.xn_t[:].rearrange("p c t -> p (c t)"), self.ps).then_inc(self.xn_copied, 1)

    def take_high(self, act, i, u):
        if not isinstance(i, int) or i:
            act.wait_ge(self.written[u], 16 * i)
        act.wait_ge(self.q_ready, 4 * i + 2 * u + 2)
        self.nc.scalar.copy(self.parts[:, u, 0, :], self.ps).then_inc(self.high, 1)

    def take_middle(self, act, i, u):
        act.wait_ge(self.rested, 2 * i + u + 1)
        self.nc.scalar.copy(self.parts[:, u, 1, :], self.rest[:]).then_inc(self.middle, 1)

    def scalar_first(self, act):
        for u in range(2):
            self.copy_turned(act, 0, u)
            self.take_high(act, 0, u)
            self.take_middle(act, 0, u)

    def scalar(self, act, st, s):
        e = self.ending(st)
        if e and s == 0:
            self.copy_turned(act, *e)
        if e and s == 3:
            self.take_high(act, *e)
        if e and s == 7:
            self.take_middle(act, *e)

    def scalar_last(self, act):
        pass


def finish(nc, k):
    with ExitStack() as ctx:
        sb = lambda n, shape, dt: ctx.enter_context(nc.sbuf_tensor(f"ff_{n}", shape, dt))
        used = []
        sem = phase_semaphores(nc, ctx, "ff", used)
        GT = 4
        GROUPS = TILES // GT
        wo = sb("wo", [P, DC, D], F32)
        router = sb("router", [P, DC, BLOCKS], F32)
        router_b = sb("router_b", [P, BLOCKS], F32)
        w1 = sb("w1", [P, DC, HID], F32)
        b1 = sb("b1", [P, FC], F32)
        w2 = sb("w2", [P, FC, D], F32)
        b2 = sb("b2", [P, D], F32)
        spread = sb("spread", [BLOCKS, FC, P], BF16)
        ao_t = sb("ao_t", [P, DC * P], F32)
        stats = sb("stats", [P, GT, 6], F32)
        moments = sb("moments", [P, GT, 2], F32)
        rstd = sb("rstd", [P, GT], I32)
        newton = sb("newton", [P, GT], F32)
        xn = sb("xn", [P, GT, D], F32)
        xn_t = sb("xn_t", [P, 2, DC, GT * P], F32)
        logits = sb("logits", [P, GT, BLOCKS], F32)
        best = sb("best", [P, GT, 8], F32)
        others = sb("others", [P, GT, BLOCKS], F32)
        closed = sb("closed", [P, GT, BLOCKS], F32)
        closed_t = sb("closed_t", [BLOCKS, 2, GT * P], BF16)
        hidden_t = sb("hidden_t", [P, FC, GT * P], F32)
        y = sb("y", [P, 2, D], F32)
        ps = ctx.enter_context(nc.psum_tensor("ff_ps", [P, 8, 512], F32))
        logit_ps = ps[:, 5, 0:GT * BLOCKS].rearrange("p (t e) -> p t e", e=BLOCKS)
        masks_ps = ps[0:BLOCKS, 5, :]
        HBANKS = 3

        wo_in, w_in, own = sem("wo_in"), sem("w_in"), sem("own")
        a_turned, a_copied, a_ready, x_done = sem("a_turned"), sem("a_copied"), sem("a_ready"), sem("x_done")
        xn_ready, turned, copied, logits_ready = sem("xn_ready"), sem("turned"), sem("copied"), sem("logits_ready")
        masks_ready, masks_turned, masks_copied = sem("masks_ready"), sem("masks_turned"), sem("masks_copied")
        x_biased = sem("x_biased")
        hid_ready, relu_done, y_ready, y_done = sem("hid_ready"), sem("relu_done"), sem("y_ready"), sem("y_done")
        out_done = [sem("out_done0"), sem("out_done1")]
        LOADS = 7

        with nc.Block() as block:

            @block.sync
            def _(sp):
                sp.dma_start(wo[:], k.dram["wo"]).then_inc(wo_in, 16)
                for tile, name in ((router, "router"), (w1, "w1"), (b1, "b1"), (w2, "w2"), (spread, "c_spread")):
                    sp.dma_start(tile[:], k.dram[name]).then_inc(w_in, 16)
                sp.dma_start(router_b[:], k.dram["router_b"].to_broadcast([P, BLOCKS])).then_inc(w_in, 16)
                sp.dma_start(b2[:], k.dram["b2"].to_broadcast([P, D])).then_inc(w_in, 16)
                with sp.Fori(0, TILES // 2) as i:
                    for u in range(2):
                        t = 2 * i + u
                        sp.wait_ge(y_done, t + 1)
                        sp.dma_start(k.result[bass.ds(t, 1)].rearrange("t p d -> (t p) d"), y[:, u]).then_inc(out_done[u], 16)
                for u in range(2):
                    sp.wait_ge(out_done[u], 16 * (TILES // 2))

            @block.gpsimd
            def _(pool):
                pool.wait_ge(w_in, 16 * LOADS)
                with pool.Fori(0, TILES) as t:
                    pool.wait_ge(xn_ready, t + 1)
                    nc.gpsimd.tensor_tensor(k.x[:, bass.ds(t, 1), :].rearrange("p a d -> p (a d)"),
                                            k.x[:, bass.ds(t, 1), :].rearrange("p a d -> p (a d)"), b2[:], ALU.add).then_inc(x_biased, 1)

            @block.tensor
            def _(pe):
                def turn_attention(g, j):
                    t = GT * g + j
                    wait(pe, a_copied, t)
                    if j == 0:
                        wait(pe, copied, GT * g)
                    for c in range(DC):
                        last = pe.transpose(ps[:, 6, c * P:(c + 1) * P], k.ao[:, t, c * P:(c + 1) * P], k.ident[:])
                    last.then_inc(a_turned, 1)

                def attention_wo(g, j):
                    t = GT * g + j
                    pe.wait_ge(a_copied, t + 1)
                    wait(pe, x_done, t)
                    for c in range(DC):
                        last = pe.matmul(ps[:, 7, 0:D], ao_t[:, c * P:(c + 1) * P], wo[:, c, :], start=(c == 0), stop=(c == DC - 1))
                    last.then_inc(a_ready, 1)

                def turn(g, j):
                    t = GT * g + j
                    pe.wait_ge(xn_ready, t + 1)
                    if j > 1:
                        pe.wait_ge(copied, t - 1)
                    for c in range(DC):
                        last = pe.transpose(ps[:, 6 + j % 2, c * P:(c + 1) * P], xn[:, j, c * P:(c + 1) * P], k.ident[:])
                    last.then_inc(turned, 1)

                def route_group(g):
                    wait(pe, masks_copied, g)
                    pe.wait_ge(copied, GT * g + GT)
                    for j in range(GT):
                        for c in range(DC):
                            last = pe.matmul(logit_ps[:, j, :], xn_t[:, g % 2, c, j * P:(j + 1) * P], router[:, c, :],
                                             start=(c == 0), stop=(c == DC - 1))
                    last.then_inc(logits_ready, 1)

                def turn_masks(g):
                    pe.wait_ge(masks_ready, g + 1)
                    for j in range(GT):
                        last = pe.transpose(masks_ps[:, j * P:(j + 1) * P], closed[:, j, :], k.ident[:])
                    last.then_inc(masks_turned, 1)

                def hidden(f, m):
                    wait(pe, relu_done, FC * f + m - HBANKS + 1)
                    bank = ps[:, 2 + (FC * f + m) % HBANKS, :]
                    for c in range(DC):
                        pe.matmul(bank, w1[:, c, m * P:(m + 1) * P], xn_t[:, f % 2, c, :], start=(c == 0), stop=False)
                    if m == 0:
                        pe.wait_ge(masks_copied, f + 1)
                    pe.matmul(bank, spread[:, m, :], closed_t[:, f % 2, :], start=False, stop=True).then_inc(hid_ready, 1)

                def output(f, j):
                    t = GT * f + j
                    wait(pe, y_done, t - 1)
                    for m in range(FC):
                        if j == 0:
                            pe.wait_ge(relu_done, FC * f + m + 1)
                        last = pe.matmul(ps[:, j % 2, 0:D], hidden_t[:, m, j * P:(j + 1) * P], w2[:, m, :],
                                         start=(m == 0), stop=(m == FC - 1))
                    last.then_inc(y_ready, 1)

                pe.wait_ge(wo_in, 16)
                for j in range(GT):
                    turn_attention(0, j)
                    attention_wo(0, j)
                for j in range(GT):
                    turn(0, j)
                pe.wait_ge(w_in, 16 * LOADS)
                route_group(0)
                turn_masks(0)
                for f in range(GROUPS):
                    g = f + 1
                    ahead = g < GROUPS
                    for m in range(FC):
                        hidden(f, m)
                        if ahead and 1 <= m <= GT:
                            attention_wo(g, m - 1)
                        if ahead and m < GT:
                            turn_attention(g, m)
                    for j in range(GT):
                        output(f, j)
                        if ahead and j < 2:
                            turn(g, 2 * j)
                            turn(g, 2 * j + 1)
                        if ahead and j == 2:
                            route_group(g)
                    if ahead:
                        turn_masks(g)

            @block.scalar
            def _(act):
                def copy_attention(g, j):
                    act.wait_ge(a_turned, GT * g + j + 1)
                    wait(act, a_ready, GT * g + j)
                    nc.scalar.copy(ao_t[:], ps[:, 6, 0:DC * P]).then_inc(a_copied, 1)

                def copy_turned(g, j):
                    act.wait_ge(turned, GT * g + j + 1)
                    nc.scalar.copy(xn_t[:, g % 2, :, j * P:(j + 1) * P], ps[:, 6 + j % 2, 0:DC * P].rearrange("p (c n) -> p c n", c=DC)).then_inc(copied, 1)

                def copy_masks(g):
                    act.wait_ge(masks_turned, g + 1)
                    nc.scalar.copy(closed_t[:, g % 2, :], masks_ps).then_inc(masks_copied, 1)

                for j in range(GT):
                    copy_attention(0, j)
                for j in range(GT):
                    copy_turned(0, j)
                copy_masks(0)
                act.wait_ge(w_in, 16 * LOADS)
                for f in range(GROUPS):
                    g = f + 1
                    for m in range(FC):
                        act.wait_ge(hid_ready, FC * f + m + 1)
                        nc.scalar.activation(hidden_t[:, m, :], ps[:, 2 + (FC * f + m) % HBANKS, :], ACT.Relu, bias=b1[:, m:m + 1]).then_inc(relu_done, 1)
                        if g < GROUPS and m < GT:
                            copy_attention(g, m)
                    if g < GROUPS:
                        for j in range(GT):
                            copy_turned(g, j)
                        copy_masks(g)

            @block.vector
            def _(dve):
                steps = [0]

                def then(ins):
                    ins.then_inc(own, 1)
                    steps[0] += 1
                    dve.wait_ge(own, steps[0])

                def normalise_group(g):
                    for j in range(GT):
                        t = GT * g + j
                        dve.wait_ge(a_ready, t + 1)
                        nc.vector.tensor_tensor(k.x[:, t, :], k.x[:, t, :], ps[:, 7, 0:D], ALU.add).then_inc(x_done, 1)
                        dve.wait_ge(x_done, t + 1)
                        then(nc.vector.bn_stats(stats[:, j, :], k.x[:, t, :]))
                    for j in range(GT):
                        last = nc.vector.bn_aggr(moments[:, j, :], stats[:, j, :])
                    then(last)
                    for part in range(4):
                        inverse_root(nc, own, steps[0], rstd[:], moments[:, :, 1], newton[:], part)
                    steps[0] += 4 * NEWTON_STEPS
                    dve.wait_ge(own, steps[0])
                    wait(dve, turned, GT * g)
                    for j in range(GT):
                        nc.vector.tensor_scalar(xn[:, j, :], k.x[:, GT * g + j, :], moments[:, j, 0:1], rstd[:, j:j + 1].bitcast(F32),
                                                ALU.subtract, ALU.mult).then_inc(xn_ready, 1)

                def close_blocks(g):
                    dve.wait_ge(logits_ready, g + 1)
                    then(nc.vector.tensor_tensor(logits[:], logit_ps, router_b[:].unsqueeze(1).to_broadcast([P, GT, BLOCKS]), ALU.add))
                    for j in range(GT):
                        last = nc.vector.max(best[:, j, :], logits[:, j, :])
                    then(last)
                    then(nc.vector.memset(best[:, :, TOP_B:8], 3.0e38))
                    for j in range(GT):
                        last = nc.vector.match_replace(others[:, j, :], best[:, j, :], logits[:, j, :], -3.0e38)
                    then(last)
                    wait(dve, masks_turned, g)
                    then(nc.vector.tensor_tensor(closed[:], others[:], logits[:], ALU.is_equal))
                    nc.vector.tensor_scalar(closed[:], closed[:], MASKED, None, ALU.mult).then_inc(masks_ready, 1)

                def emit_output(f, j):
                    t = GT * f + j
                    dve.wait_ge(x_biased, t + 1)
                    dve.wait_ge(y_ready, t + 1)
                    if t > 1:
                        dve.wait_ge(out_done[t % 2], 16 * (t // 2))
                    nc.vector.tensor_tensor(y[:, t % 2], k.x[:, t, :], ps[:, j % 2, 0:D], ALU.add).then_inc(y_done, 1)

                normalise_group(0)
                dve.wait_ge(w_in, 16 * LOADS)
                close_blocks(0)
                for f in range(GROUPS):
                    g = f + 1
                    if g < GROUPS:
                        normalise_group(g)
                    for j in range(GT):
                        if g < GROUPS and j == GT - 1:
                            close_blocks(g)
                        emit_output(f, j)


def build(nc, dram, out):
    k = Kernel()
    k.dram, k.result = dram, out
    scratch = lambda name, shape, dt: nc.dram_tensor(name, shape, dt, kind="Internal").ap()
    stack = (BATCH, PARTS, P, DC * SEQ)
    k.q0_stack, k.k0_stack = scratch("q0_stack", stack, BF16), scratch("k0_stack", stack, BF16)
    k.q1_stack, k.k1_stack = scratch("q1_stack", stack, BF16), scratch("k1_stack", stack, BF16)
    k.v1 = scratch("v1_rows", (BATCH, 2, P, D), F32)
    k.xn = scratch("moe_rows", (TILES, P, D + EXPERTS), F32)
    k.lists = scratch("expert_lists", (EXPERTS * TOK, 1), I32)
    k.outs = scratch("expert_outs", (ETILES, P, D), F32)
    with ExitStack() as ctx:
        sb = lambda n, shape, dt: ctx.enter_context(nc.sbuf_tensor(n, shape, dt))
        k.x = sb("x", [P, TILES, D], F32)
        k.kst = sb("stacked_keys", [ROWS + MROWS, 4, HSTEP, SEQ], BF16)
        k.ao = sb("attention_out", [P, TILES, D], F32)
        k.slot = sb("slot", [P, TILES, TOP_K], I32)
        k.table = sb("tile_table", [1, 3, ETABLE], I32)
        k.tiles_used = sb("tiles_used", [1, 1], I32)
        k.ids = sb("slot_tokens", [P, ETABLE], I32)
        k.indirect = lambda n: ctx.enter_context(nc.semaphore(f"indirect_{n}"))
        k.passed = ctx.enter_context(nc.semaphore("passed"))
        constants(nc, k, ctx)
        prepare(nc, k)
        attention(nc, k, "a0", k.q0_stack, k.k0_stack, dram["ctx"], 1.0 / float(np.sqrt(np.float32(D))), False, k.ao, Route())
        experts(nc, k, 0, EXPECTED)
        experts(nc, k, EXPECTED, ETILES)
        attention(nc, k, "a1", k.q1_stack, k.k1_stack, k.v1, 1.0 / float(np.sqrt(np.float32(DH))), True, k.ao, Combine())
        finish(nc, k)


def _layouts(inputs):
    a = {n: np.ascontiguousarray(v) for n, v in inputs.items()}
    heads = lambda w: w.reshape(DC, HEADS // DC, DH, -1).transpose(0, 2, 1, 3)
    c = a["ctx_1024"]
    out = {
        "x": a["x"].reshape(TILES, P, D),
        "ctx": c.reshape(BATCH, 2, P, D),
        "ctx_t": c.reshape(BATCH, SEQ, DC, HEADS // DC, DH).transpose(0, 4, 3, 2, 1).reshape(BATCH, P, DC, SEQ),
    }
    wk = heads(a["L1_xattn_Wk"]).reshape(DC, P, D)
    wk = heads(wk.transpose(2, 0, 1).reshape(D, D)).reshape(DC, P, DC, P)
    out["wk"] = wk.transpose(1, 0, 2, 3)
    out["wv"] = heads(a["L1_xattn_Wv"].T).reshape(DC, P, D).transpose(1, 0, 2)
    wq = heads(a["L1_xattn_Wq"]).reshape(DC, P, DC, P)
    out["wq"] = wq.transpose(3, 2, 0, 1)
    rows = lambda w: w.T.reshape(DC, P, -1).transpose(1, 0, 2)
    out["wo"] = rows(a["L1_xattn_Wo"])
    out["gate"] = rows(a["L0_ffn_gate_w"])
    out["router"] = rows(a["L1_ffn_router_w"])
    out["router_b"] = a["L1_ffn_router_b"].reshape(1, BLOCKS)
    out["w1"] = rows(a["L1_ffn_w1"])
    out["b1"] = a["L1_ffn_b1"].reshape(FC, P).T
    out["w2"] = a["L1_ffn_w2"].T.reshape(FC, P, D).transpose(1, 0, 2)
    out["b2"] = a["L1_ffn_b2"].reshape(1, D)
    gu = np.stack([a["L0_ffn_w_gate"], a["L0_ffn_w_up"]], 1).reshape(EXPERTS, 2 * FF, DC, P)
    out["w_gu"] = gu.transpose(0, 3, 2, 1)
    out["w_down"] = a["L0_ffn_w_down"].reshape(EXPERTS, D, 2, FH).transpose(0, 3, 2, 1)
    bf16 = mybir.dt.np(BF16)
    p = np.arange(P)
    out["c_ident"] = np.eye(P, dtype=np.float32)
    out["c_ident_b"] = np.eye(P, dtype=np.float32).astype(bf16)
    late = np.where(p[None, :] > p[:, None], np.float32(MASKED), np.float32(0))
    out["c_mask_qk"] = late.astype(bf16)
    out["c_mask_kq"] = late.T.astype(bf16)
    out["c_before"] = (p[:, None] < p[None, :]).astype(bf16)
    out["c_ones"] = np.ones((P, P), bf16)
    out["c_list_end"] = np.broadcast_to(EXPERTS * TOK - TOK * np.arange(EXPERTS, dtype=np.float32), (P, EXPERTS))
    out["c_token"] = (P * np.arange(TILES)[None, :] + p[:, None]).astype(np.int32)
    out["c_tile"] = (P * np.arange(2)[None, :] + p[:, None]).astype(np.float32)
    spread = (np.arange(HID) // (HID // BLOCKS))[None, :] == np.arange(BLOCKS)[:, None]
    out["c_spread"] = spread.reshape(BLOCKS, FC, P).astype(bf16)
    return {n: np.ascontiguousarray(v) for n, v in out.items()}


def kernel(**inputs):
    import numpy as _np
    import concourse.bacc as _bacc
    from concourse import mybir as _mybir
    from concourse.bass_utils import run_bass_kernel_spmd as _run

    nc = _bacc.Bacc("TRN2", target_bir_lowering=False, num_devices=1)
    arrays, dram = {}, {}
    for name, a in _layouts(inputs).items():
        arrays[f"in_{name}_dram"] = a
        dram[name] = nc.dram_tensor(f"in_{name}_dram", a.shape, _mybir.dt.from_np(a.dtype), kind="ExternalInput").ap()
    out = nc.dram_tensor("out_0_dram", (TILES, P, D), _mybir.dt.float32, kind="ExternalOutput").ap()
    build(nc, dram, out)
    r = _run(nc, [arrays], core_ids=[0])
    return _np.asarray(r.results[0]["out_0_dram"]).reshape(BATCH, SEQ, D)
```
